# Optimizing a Trainium2 kernel written in Bass

```python
import numpy as np
import jax
import jax.numpy as jnp

def _softmax(x, axis=-1):
    return jax.nn.softmax(x, axis=axis)

def _gelu(x):
    return jax.nn.gelu(x, approximate=True)

def _silu(x):
    return jax.nn.silu(x)

def _sigmoid(x):
    return jax.nn.sigmoid(x)

def _layernorm(x, axis=-1, eps=1e-05):
    m = jnp.mean(x, axis=axis, keepdims=True)
    v = jnp.var(x, axis=axis, keepdims=True)
    return (x - m) / jnp.sqrt(v + eps)

def _scatter_add(tgt, idx, src, axis=0):
    return tgt.at[idx].add(src)

def _segment_sum(src, seg, n):
    return jax.ops.segment_sum(src, seg, n)
kernel_name = 'mk_adj_preln_d2_adj_r2_8899ae'

def setup_inputs(seed: int=0):
    np.random.seed(seed)
    _w = jnp.asarray

    def _rec_inputs():
        import jax
        import jax.numpy as jnp
        _gk = jax.random.key(seed)
        x = -0.0002928 + 1 * jax.random.normal(jax.random.fold_in(_gk, 1), (4096, 512), jnp.float32)
        _a = jax.random.bernoulli(jax.random.fold_in(_gk, 2), 0.000976562, (4096, 4096))
        _a = jnp.logical_or(_a, jnp.eye(4096, dtype=bool))
        _af = _a.astype(jnp.float32)
        adj = _af
        return (x, adj)
    x, adj = _rec_inputs()

    def _L0_gnn_setup():
        import jax, jax.numpy as jnp
        import numpy as np
        ALPHA = 0.2
        NEG = -9000000000000000.0
        N, NFEAT, NHID, NHEADS = (2048, 512, 64, 8)
        EMB = NHID * NHEADS
        key = jax.random.key(seed)
        ks = jax.random.split(key, 16)
        x = jax.random.normal(ks[0], (N, NFEAT), dtype=jnp.float32)
        adj = (jax.random.uniform(ks[1], (N, N)) < 0.01).astype(jnp.float32)
        adj = jnp.maximum(adj, jnp.eye(N, dtype=jnp.float32))
        s = 0.05
        W = jax.random.normal(ks[2], (NHEADS, NFEAT, NHID), dtype=jnp.float32) * s
        a1 = jax.random.normal(ks[3], (NHEADS, NHID), dtype=jnp.float32) * s
        a2 = jax.random.normal(ks[4], (NHEADS, NHID), dtype=jnp.float32) * s
        W1 = jax.random.normal(ks[5], (EMB // 2, EMB), dtype=jnp.float32) * s
        b1 = jnp.zeros((EMB // 2,), dtype=jnp.float32)
        W2 = jax.random.normal(ks[6], (NFEAT // 4, EMB // 2), dtype=jnp.float32) * s
        b2 = jnp.zeros((NFEAT // 4,), dtype=jnp.float32)
        W3 = jax.random.normal(ks[7], (NFEAT // 2, NFEAT // 4), dtype=jnp.float32) * s
        b3 = jnp.zeros((NFEAT // 2,), dtype=jnp.float32)
        W4 = jax.random.normal(ks[8], (NFEAT, NFEAT // 2), dtype=jnp.float32) * s
        b4 = jnp.zeros((NFEAT,), dtype=jnp.float32)
        return {'x': x, 'adj': adj, 'W': W, 'a1': a1, 'a2': a2, 'W1': W1, 'b1': b1, 'W2': W2, 'b2': b2, 'W3': W3, 'b3': b3, 'W4': W4, 'b4': b4}
    _L0_gnn_all = _L0_gnn_setup()
    _L0_gnn_in = {k: v for k, v in _L0_gnn_all.items() if k in ('W', 'a1', 'a2', 'W1', 'b1', 'W2', 'b2', 'W3', 'b3', 'W4', 'b4')}
    del _L0_gnn_all

    def _L1_gnn_setup():
        import jax, jax.numpy as jnp
        import numpy as np
        N, H, E, HEADS = (1500, 512, 10000, 8)
        DK = H // HEADS
        key = jax.random.key(seed)
        k1, k2, k3, k4 = jax.random.split(key, 4)
        inst_feature = jax.random.normal(k1, (N, H), dtype=jnp.float32)
        rel_pair_index = jax.random.randint(k2, (E, 2), 0, N, dtype=jnp.int64)
        agg = jnp.zeros((N, N), dtype=jnp.float32)
        agg = agg.at[rel_pair_index[:, 0], rel_pair_index[:, 1]].set(1.0)
        agg = agg.at[jnp.arange(N), jnp.arange(N)].set(1.0)
        std = float(np.sqrt(2.0 / (H + DK)))
        Wq = jax.random.normal(k3, (H, H), dtype=jnp.float32) * std
        Wk = jax.random.normal(k4, (H, H), dtype=jnp.float32) * std
        bq = jnp.zeros((H,), dtype=jnp.float32)
        bk = jnp.zeros((H,), dtype=jnp.float32)
        return {'inst_feature': inst_feature, 'aggregator_matrix': agg, 'rel_pair_index': rel_pair_index, 'Wq': Wq, 'bq': bq, 'Wk': Wk, 'bk': bk}
    _L1_gnn_all = _L1_gnn_setup()
    _L1_gnn_in = {k: v for k, v in _L1_gnn_all.items() if k in ('rel_pair_index', 'Wq', 'bq', 'Wk', 'bk')}
    del _L1_gnn_all
    return {'x': x, 'adj': adj, 'L0_gnn_W': _L0_gnn_in['W'], 'L0_gnn_a1': _L0_gnn_in['a1'], 'L0_gnn_a2': _L0_gnn_in['a2'], 'L0_gnn_W1': _L0_gnn_in['W1'], 'L0_gnn_b1': _L0_gnn_in['b1'], 'L0_gnn_W2': _L0_gnn_in['W2'], 'L0_gnn_b2': _L0_gnn_in['b2'], 'L0_gnn_W3': _L0_gnn_in['W3'], 'L0_gnn_b3': _L0_gnn_in['b3'], 'L0_gnn_W4': _L0_gnn_in['W4'], 'L0_gnn_b4': _L0_gnn_in['b4'], 'L1_gnn_rel_pair_index': _L1_gnn_in['rel_pair_index'], 'L1_gnn_Wq': _L1_gnn_in['Wq'], 'L1_gnn_bq': _L1_gnn_in['bq'], 'L1_gnn_Wk': _L1_gnn_in['Wk'], 'L1_gnn_bk': _L1_gnn_in['bk']}

def reference(x, adj, L0_gnn_W, L0_gnn_a1, L0_gnn_a2, L0_gnn_W1, L0_gnn_b1, L0_gnn_W2, L0_gnn_b2, L0_gnn_W3, L0_gnn_b3, L0_gnn_W4, L0_gnn_b4, L1_gnn_rel_pair_index, L1_gnn_Wq, L1_gnn_bq, L1_gnn_Wk, L1_gnn_bk):
    import jax
    import jax.numpy as jnp

    def _L0_gnn_ref(x, adj, W, a1, a2, W1, b1, W2, b2, W3, b3, W4, b4):
        import jax, jax.numpy as jnp
        import numpy as np
        ALPHA = 0.2
        NEG = -9000000000000000.0
        N, NFEAT, NHID, NHEADS = (2048, 512, 64, 8)
        EMB = NHID * NHEADS
        Wh = jnp.einsum('nf,hfd->hnd', x, W)
        e_src = jnp.einsum('hnd,hd->hn', Wh, a1)
        e_dst = jnp.einsum('hnd,hd->hn', Wh, a2)
        e = jax.nn.leaky_relu(e_src[:, :, None] + e_dst[:, None, :], ALPHA)
        e = jnp.where(adj[None] > 0, e, NEG)
        att = jax.nn.softmax(e, axis=-1)
        h = jnp.einsum('hnm,hmd->hnd', att, Wh)
        h = jax.nn.elu(h)
        enc = jnp.transpose(h, (1, 0, 2)).reshape(x.shape[0], -1)
        out = jax.nn.relu(enc @ W1.T + b1)
        out = jax.nn.relu(out @ W2.T + b2)
        out = jax.nn.relu(out @ W3.T + b3)
        out = out @ W4.T + b4
        return out

    def _L1_gnn_ref(inst_feature, aggregator_matrix, rel_pair_index, Wq, bq, Wk, bk):
        import jax, jax.numpy as jnp
        import numpy as np
        N, H, E, HEADS = (1500, 512, 10000, 8)
        DK = H // HEADS
        n = inst_feature.shape[0]
        sub = rel_pair_index[:, 0]
        obj = rel_pair_index[:, 1]
        q = (inst_feature[sub] @ Wq.T + bq).reshape(-1, HEADS, DK)
        k = (inst_feature[obj] @ Wk.T + bk).reshape(-1, HEADS, DK)
        att = ((q * k).sum(-1) / np.sqrt(DK)).T.astype(inst_feature.dtype)
        scores = jnp.zeros((HEADS, n, n), dtype=inst_feature.dtype)
        scores = scores.at[:, sub, obj].set(att)
        mask = (1.0 - aggregator_matrix).astype(bool)
        scores = jnp.where(mask[None], -jnp.inf, scores)
        di = jnp.arange(n)
        scores = scores.at[:, di, di].set(1e-07)
        attn = jax.nn.softmax(scores, axis=2)
        aggregator_factor = attn.sum(axis=0) / HEADS
        return aggregator_factor @ inst_feature
    h = jnp.maximum(_layernorm(x, axis=-1), 0.0)
    x = x + _L0_gnn_ref(h, adj, L0_gnn_W, L0_gnn_a1, L0_gnn_a2, L0_gnn_W1, L0_gnn_b1, L0_gnn_W2, L0_gnn_b2, L0_gnn_W3, L0_gnn_b3, L0_gnn_W4, L0_gnn_b4)
    h = jnp.maximum(_layernorm(x, axis=-1), 0.0)
    x = x + _L1_gnn_ref(h, adj, L1_gnn_rel_pair_index, L1_gnn_Wq, L1_gnn_bq, L1_gnn_Wk, L1_gnn_bk)
    return x

_drawn_inputs = setup_inputs


def setup_inputs(seed=0):
    import zlib

    import numpy as np

    out = dict(_drawn_inputs(seed))
    spreads = {'L0_gnn_b1': (0.0, 0.488),
     'L0_gnn_b2': (0.0, 0.287),
     'L0_gnn_b3': (0.0, 0.1),
     'L0_gnn_b4': (0.0, 0.1),
     'L1_gnn_bq': (0.0, 2.0),
     'L1_gnn_bk': (0.0, 2.0)}
    factors = {'L0_gnn_a1': 192.181, 'L0_gnn_a2': 7.978, 'L1_gnn_Wq': 200.0, 'L1_gnn_Wk': 200.0}
    for name, (base, spread) in spreads.items():
        noise = np.random.default_rng([zlib.crc32(name.encode()), seed]).standard_normal(out[name].shape)
        drawn = base * np.exp(spread * noise) if base else spread * noise
        out[name] = jnp.asarray(drawn.astype(out[name].dtype))
    for name, factor in factors.items():
        out[name] = (out[name] * factor).astype(out[name].dtype)
    return out
```

```python
from contextlib import ExitStack

import concourse.bass as bass
from concourse import mybir
from concourse.alu_op_type import AluOpType as ALU

ACT = mybir.ActivationFunctionType
F32 = mybir.dt.float32
I32 = mybir.dt.int32
U32 = mybir.dt.uint32
X_AXIS = mybir.AxisListType.X

P = 128
N = 4096
D = 512
TILES = N // P
HEADS = 8
DH = D // HEADS
KC = D // P
SEG = 8
SEGW = N // SEG
SEGP = SEGW + 8
SLOTS = 16
CH = 5
EDGES = CH * P
PAIR = 2
STEPS = TILES // PAIR
EC = PAIR * CH
GC = EC + PAIR
ROW = D + HEADS
NPAIR = 10000
PP = 125
PCOL = NPAIR // PP
PG = 8
VW = 26
OFFC, ROWC, SRCC = SLOTS, SLOTS + 1, SLOTS + 2
FAR = 5000.0
NEGBIG = 1.0e30
ALPHA = 0.2
EPS = 1e-5
START_TICKS, FRONT_TICKS, MID_TICKS, ROWS_TICKS, EDGE_TICKS, TAIL_TICKS = 24, 34, 46, 10, 10, 6
ROWS1_TICKS, HIT_TICKS, SOFT_TICKS, EDGE1_TICKS = 3, 8, 7, 13
ARENA = 22720
SELF_SCORE = 1e-7


class Steps:

    def __init__(self, eng, sem, per, run):
        self.eng, self.sem, self.base, self.per, self.k = eng, sem, run * per, per, 0

    def __call__(self, instruction):
        instruction.then_inc(self.sem, 1)
        self.k += 1
        return self.k

    def after(self, k):
        self.eng.wait_ge(self.sem, self.base + k)

    def link(self, instruction):
        self.after(self(instruction))

    def end(self):
        assert self.k == self.per, (self.k, self.per)


def lone_wait(eng, met, sem, value):
    if not isinstance(value, int):
        eng.compute_val(value)
    eng.wait_ge(met, 1)
    eng.wait_ge(sem, value)


def gnn_kernel(nc, x, adj, w0, a1, a2, w1t, b1, w2t, b2, w3t, b3, w4t, b4, pairs, wqt, bq, wkt, bk, out):
    table0 = nc.dram_tensor("table0", [N, ROW], F32, kind="Internal").ap()
    table1 = nc.dram_tensor("table1", [N, D], F32, kind="Internal").ap()
    keys_dram = nc.dram_tensor("keys_dram", [N, SLOTS], F32, kind="Internal").ap()
    score_dram = nc.dram_tensor("score_dram", [N * SLOTS, HEADS], F32, kind="Internal").ap()

    adj_flat = adj.rearrange("n m -> (n m)").unsqueeze(1)
    adj_rows = adj.rearrange("n (s c) -> n s c", s=SEG)
    score_rows = score_dram.rearrange("(n k) h -> n (k h)", k=SLOTS)

    with ExitStack() as ctx:
        def sb(name, shape, dt=F32):
            return ctx.enter_context(nc.sbuf_tensor(name, shape, dt))

        def sem(name):
            return ctx.enter_context(nc.semaphore(name))

        iota = sb("iota", [P, EDGES])
        ident = sb("ident", [P, P])
        before = sb("before", [P, P])
        ones = sb("ones", [P, P])
        zeros = sb("zeros", [P, D])
        seg_base = sb("seg_base", [P, SEG, 8])
        self_key = sb("self_key", [P, TILES])
        edge_pos = sb("edge_pos", [P, PAIR, CH])
        iota16 = iota[:, 0:SLOTS]
        iota_row1 = iota[:, 1:P + 1]

        a_fold = sb("a_fold", [P, KC, 2 * HEADS])
        w1_sb = sb("w1_sb", [P, 4, 256])
        w2_sb = sb("w2_sb", [P, 2, 128])
        w3_sb = sb("w3_sb", [P, 256])
        w4_sb = sb("w4_sb", [P, 2, D])
        b1_sb = sb("b1_sb", [P, 2])
        b2_sb = sb("b2_sb", [P, 1])
        b3_sb = sb("b3_sb", [P, 2])
        b4_row = sb("b4_row", [P, D])

        x_all = sb("x_all", [P, TILES, D])
        node = sb("node", [P, TILES, VW])
        src_dst = sb("src_dst", [P, TILES, 2 * HEADS])
        seg_last = sb("seg_last", [P, TILES, SEG])
        end = sb("end", [P, TILES])
        tile_edges = sb("tile_edges", [P, TILES])
        count = sb("count", [P, TILES])
        slot_bias = sb("slot_bias", [P, TILES, SLOTS + 1])
        row_id = sb("row_id", [P, STEPS, EC])
        slot_id = sb("slot_id", [P, STEPS, EC])
        idx_all = sb("idx_all", [P, STEPS, EC], U32)

        arena = sb("arena", [P, ARENA])

        def carver():
            at = [0]

            def carve(shape, dt=F32):
                size = 1
                for n in shape:
                    size *= n
                view = arena[:, at[0]:at[0] + size]
                at[0] += size
                assert at[0] <= ARENA, at[0]
                names = "abc"[:len(shape)]
                if dt is not F32:
                    view = view.bitcast(dt)
                if len(shape) == 1:
                    return view
                return view.rearrange(f"p ({' '.join(names)}) -> p {' '.join(names)}", **dict(zip(names, shape)))

            return carve

        both = range(2)
        front = carver()
        adj_sb = [front([SEG, SEGP]) for u in both]
        ones8 = sb("ones8", [P, 8])
        found = [sb(f"found{u}", [P, SEG, 8], U32) for u in both]
        key_raw = [sb(f"key_raw{u}", [P, SEG, 8]) for u in both]
        key_any = [sb(f"key_any{u}", [P, SEG, 8]) for u in both]
        key_nbr = [sb(f"key_nbr{u}", [P, SEG * 8]) for u in both]
        key_left = [sb(f"key_left{u}", [P, SEG * 8]) for u in both]
        key16 = [sb(f"key16{u}", [P, SLOTS]) for u in both]
        stats = [sb(f"stats{u}", [P, 6]) for u in both]
        mean_var = [sb(f"mean_var{u}", [P, 2]) for u in both]
        ln_scale = [sb(f"ln_scale{u}", [P, 1]) for u in both]
        ln_shift = [sb(f"ln_shift{u}", [P, 1]) for u in both]
        h_sb = [front([D]) for u in both]
        hT = [front([KC, P]) for u in both]
        wh_row = [front([ROW]) for u in both]
        w0_sb = front([KC, D])
        a_rows = front([2, D])
        fold_tmp = front([D])

        pair_sb = sb("pair_sb", [PP, PCOL, 2], I32)
        pair_flat = sb("pair_flat", [PP, PCOL])
        pair_ne = sb("pair_ne", [PP, PCOL])
        pair_idx = sb("pair_idx", [PP, PCOL], U32)
        idx8 = sb("idx8", [PP, PG], U32)
        adj8 = sb("adj8", [PP, PG])
        pair_adj = sb("pair_adj", [PP, PCOL])
        hit_key = sb("hit_key", [P, PCOL])
        hit8 = sb("hit8", [P, 8])
        hit_valid = sb("hit_valid", [P, 8])
        hit8_m1 = sb("hit8_m1", [P, 8], I32)
        hit_sub_i = sb("hit_sub_i", [P, 8], I32)
        hit_obj_i = sb("hit_obj_i", [P, 8], I32)
        hit_node = sb("hit_node", [P, 17])
        hit_end = sb("hit_end", [P, 2])
        hit_rows = sb("hit_rows", [P, P])
        hit_cmp = sb("hit_cmp", [P, P])
        hit_e = sb("hit_e", [P, 17])
        hit_slot = sb("hit_slot", [P, 1])
        hit_sel = sb("hit_sel", [P, 8])
        hit_tmp = sb("hit_tmp", [P, 8])
        hit_sub1 = sb("hit_sub1", [P, 1])
        hit_obj1 = sb("hit_obj1", [P, 1])
        hit_f = sb("hit_f", [P, 4])
        hit_sub = sb("hit_sub", [P, 1], U32)
        hit_obj = sb("hit_obj", [P, 1], U32)
        hit_dst = sb("hit_dst", [P, 1], U32)
        hit_keys = sb("hit_keys", [P, SLOTS])
        hit_att = sb("hit_att", [P, HEADS])
        flag_f = sb("flag_f", [P, 8])
        flag_i = sb("flag_i", [P, 1], I32)
        diag = sb("diag", [P, TILES])

        edge = carver()
        gath = [edge([GC, ROW]) for q in both]
        row_hot = [edge([PAIR, EDGES]) for q in both]
        row_cmp = edge([PAIR, EDGES])
        edge_info = [sb(f"edge_info{q}", [P, EC, VW]) for q in both]
        slot_hot = [sb(f"slot_hot{q}", [P, EC, SLOTS]) for q in both]
        nbr_tmp = sb("nbr_tmp", [P, EC, SLOTS])
        nbr_key = sb("nbr_key", [P, 3, EC])
        edge_idx = [sb(f"edge_idx{q}", [P, EC], U32) for q in both]
        edge_hot = [sb(f"edge_hot{q}", [P, EC, P]) for q in both]
        placed = edge([EC, SLOTS, HEADS])
        masked = edge([PAIR, SLOTS, HEADS])
        row_max = [sb(f"row_max{q}", [P, PAIR, HEADS]) for q in both]
        max_tmp = sb("max_tmp", [P, 3, PAIR, HEADS])
        edge_e = sb("edge_e", [P, 3, GC, HEADS])
        prob = [sb(f"prob{q}", [P, GC, HEADS]) for q in both]
        inv_sum = sb("inv_sum", [P, PAIR, HEADS])
        att = edge([PAIR, D])
        att_exp = edge([PAIR, D])
        att_relu = edge([PAIR, D])
        encT = edge([KC, PAIR * P])
        z1 = edge([2, PAIR * P])
        z2 = edge([PAIR * P])
        z3 = z1

        late = carver()
        late([2 * GC * ROW + 3 * PAIR * EDGES])
        wq_sb = late([KC, D])
        wk_sb = late([KC, D])
        hit_h = [late([D]) for s in both]
        hit_hT = late([KC, P])
        hit_q = late([D])
        hit_k = hit_h[0]
        bq_row, bk_row = b4_row, zeros
        w1_flat = w1_sb[:].rearrange("p a b -> p (a b)")
        score_in = [w1_flat[:, 256 * q:256 * (q + 1)].rearrange("p (u c) -> p u c", u=PAIR) for q in both]
        soft = w1_flat[:, 512:784].rearrange("p (u k h) -> p u k h", u=PAIR, h=HEADS)
        soft_max = max_tmp[:, 0]
        soft_sum = max_tmp[:, 1]
        weight = [sb(f"weight{q}", [P, PAIR, SLOTS + 1]) for q in both]
        edge_w = sb("edge_w", [P, EC])
        self_hot = [sb(f"self_hot{u}", [P, P]) for u in both]
        out_sb = [att[:, u, :] for u in both]
        bank = [ctx.enter_context(nc.psum_tensor(f"bank{i}", [P, 512], F32)) for i in range(8)]

        consts_made = sem("consts_made")
        weights0_in = sem("weights0_in")
        weights1_in = sem("weights1_in")
        weights2_in = sem("weights2_in")
        adj_in = [sem(f"adj_in{u}") for u in both]
        x_in = [sem(f"x_in{u}") for u in both]
        adj_searched = sem("adj_searched")
        dve_start = sem("dve_start")
        dve_front = sem("dve_front")
        fold_ready = sem("fold_ready")
        ln_ready = sem("ln_ready")
        h_made = sem("h_made")
        h_turned = sem("h_turned")
        hT_ready = sem("hT_ready")
        wh_summed = sem("wh_summed")
        wh_copied = sem("wh_copied")
        wh_stored = [sem(f"wh_stored{u}") for u in both]
        b4_added = sem("b4_added")
        pair_in = sem("pair_in")
        pairs_ready = sem("pairs_ready")
        pool_pair = sem("pool_pair")
        pair_adj_in = sem("pair_adj_in")
        diag_in = sem("diag_in")
        dve_mid = sem("dve_mid")
        counts_ready = sem("counts_ready")
        offsets_summed = sem("offsets_summed")
        node_ready = sem("node_ready")
        flags_ready = sem("flags_ready")
        flags_summed = sem("flags_summed")
        hit_rows_ready = sem("hit_rows_ready")
        hit_summed = sem("hit_summed")
        keys_stored = sem("keys_stored")
        score_zeroed = sem("score_zeroed")
        dve_rows = sem("dve_rows")
        rows_ready = sem("rows_ready")
        info_summed = sem("info_summed")
        info_ready = sem("info_ready")
        idx_ready = sem("idx_ready")
        hot_ready = sem("hot_ready")
        gath_in = [sem(f"gath_in{q}") for q in both]
        self_in = [sem(f"self_in{q}") for q in both]
        dve_edge = sem("dve_edge")
        placed_ready = sem("placed_ready")
        slots_summed = sem("slots_summed")
        row_max_ready = sem("row_max_ready")
        edge_max_summed = sem("edge_max_summed")
        exponent_ready = sem("exponent_ready")
        prob_ready = sem("prob_ready")
        scaled = sem("scaled")
        agg_summed = sem("agg_summed")
        att_ready = sem("att_ready")
        elu_parts = sem("elu_parts")
        enc_ready = sem("enc_ready")
        enc_turned = sem("enc_turned")
        encT_ready = sem("encT_ready")
        mlp_summed = sem("mlp_summed")
        mlp_relu = sem("mlp_relu")
        dve_tail = sem("dve_tail")
        ln2_ready = sem("ln2_ready")
        h2_made = sem("h2_made")
        h2_stored = [sem(f"h2_stored{u}") for u in both]
        hit_in = sem("hit_in")
        hit_turned = sem("hit_turned")
        hit_hT_ready = sem("hit_hT_ready")
        hit_proj = sem("hit_proj")
        dve_hit = sem("dve_hit")
        hit_att_ready = sem("hit_att_ready")
        hit_stored = sem("hit_stored")
        late_in = sem("late_in")
        dve_rows1 = sem("dve_rows1")
        rows1_ready = sem("rows1_ready")
        idx1_ready = sem("idx1_ready")
        gath1_in = [sem(f"gath1_in{q}") for q in both]
        self1_in = [sem(f"self1_in{q}") for q in both]
        score_in_sem = [sem(f"score_in{q}") for q in both]
        dve_soft = sem("dve_soft")
        soft_ready = sem("soft_ready")
        soft_exp = sem("soft_exp")
        weight_ready = sem("weight_ready")
        edge_w_summed = sem("edge_w_summed")
        dve_edge1 = sem("dve_edge1")
        hot1_ready = sem("hot1_ready")
        agg1_summed = sem("agg1_summed")
        out_ready = sem("out_ready")
        out_stored = [sem(f"out_stored{u}") for u in both]

        neg_one = sb("neg_one", [P, 1])
        eps_col = sb("eps_col", [P, 1])
        std = [sb(f"std{u}", [P, 1]) for u in both]
        var_ready = sem("var_ready")
        std_ready = sem("std_ready")
        var2_ready = sem("var2_ready")
        std2_ready = sem("std2_ready")
        N_CONSTS = 10
        x_rows = x.rearrange("(t p) d -> t p d", p=P)
        out_rows = out.rearrange("(t p) d -> t p d", p=P)
        adj_tiles = adj_rows.rearrange("(t p) s c -> t p s c", p=P)
        table0_rows = table0.rearrange("(t p) d -> t p d", p=P)
        table0_steps = table0.rearrange("(j u p) d -> j p u d", u=PAIR, p=P)
        table1_rows = table1.rearrange("(t p) d -> t p d", p=P)
        table1_steps = table1.rearrange("(j u p) d -> j p u d", u=PAIR, p=P)
        score_steps = score_rows.rearrange("(j u p) c -> j p u c", u=PAIR, p=P)
        step_bias = slot_bias[:].rearrange("p (j u) k -> p j u k", u=PAIR)
        step_src_dst = src_dst[:].rearrange("p (j u) c -> p j u c", u=PAIR)

        def step_node(j):
            return node[:].rearrange("p (j u) v -> p j u v", u=PAIR)[:, j]


        wide = carver()
        d_whole = [wide([N]) for _ in range(4)]
        d_score, d_adj, d_turned, d_dst = d_whole
        d_head = wide([TILES, DH])
        d_diag = wide([KC, P])
        d_out = wide([D])
        d_agg = d_dst
        d_pair_att = wide([PCOL, HEADS])
        d_pair_att_flat = d_pair_att.rearrange("p c h -> p (c h)")
        d_h2 = arena[:, 2 * N:4 * N].rearrange("p (j d) -> p j d", d=D)
        half = TILES // 2
        d_weight = [arena[:, 0:KC * D].rearrange("p (k n) -> p k n", k=KC),
                    arena[:, KC * D:2 * KC * D].rearrange("p (k n) -> p k n", k=KC)]
        d_pair_h = [arena[0:PP, N + n * D:N + (n + 1) * D] for n in both]
        d_pair_hT = [arena[:, N + (2 + n) * D:N + (3 + n) * D].rearrange("p (k n) -> p k n", k=KC) for n in both]
        d_pair_q = [arena[0:PP, N + (4 + n) * D:N + (5 + n) * D] for n in both]
        d_bias = [arena[:, N + (6 + n) * D:N + (7 + n) * D] for n in both]
        d_max = sb("d_max", [P, 2])
        d_sum = sb("d_sum", [P, 2])
        d_idx = sb("d_idx", [PP, 2], U32)
        d_val = sb("d_val", [PP, 1])
        off_diag, on_diag = self_hot[0], self_hot[1]
        att_dram = nc.dram_tensor("att_dram", [N, D], F32, kind="Internal").ap()
        full_dram = nc.dram_tensor("full_dram", [N, N], F32, kind="Internal").ap()
        agg_dram = nc.dram_tensor("agg_dram", [N, N], F32, kind="Internal").ap()
        full_flat = full_dram.rearrange("n m -> (n m)").unsqueeze(1)
        full_rows = full_dram.rearrange("(t p) m -> t p m", p=P)
        agg_rows = agg_dram.rearrange("(t p) m -> t p m", p=P)
        whole_rows = adj.rearrange("(t p) m -> t p m", p=P)
        att_rows = att_dram.rearrange("(t p) d -> t p d", p=P)
        att_steps = att_dram.rearrange("(j u p) d -> j p u d", u=PAIR, p=P)
        table0_heads = table0.rearrange("(t p) c -> p t c", p=P)
        table1_halves = table1.rearrange("(g t p) d -> g p t d", g=2, p=P)

        g_head_in = sem("g_head_in")
        g_diag_ready = sem("g_diag_ready")
        g_dst_summed = sem("g_dst_summed")
        g_dst_ready = sem("g_dst_ready")
        g_adj_in = sem("g_adj_in")
        g_dve = sem("g_dve")
        g_max_ready = sem("g_max_ready")
        g_exp_ready = sem("g_exp_ready")
        g_turned = sem("g_turned")
        g_turned_ready = sem("g_turned_ready")
        g_summed = sem("g_summed")
        g_out_ready = sem("g_out_ready")
        g_stored = sem("g_stored")
        g_att_in = sem("g_att_in")
        e_weights_in = sem("e_weights_in")
        e_idx_ready = sem("e_idx_ready")
        e_rows_in = sem("e_rows_in")
        e_turned = sem("e_turned")
        e_turned_ready = sem("e_turned_ready")
        e_proj = sem("e_proj")
        e_pair_dve = sem("e_pair_dve")
        e_pair_ready = sem("e_pair_ready")
        e_zero_ready = sem("e_zero_ready")
        e_zeroed = sem("e_zeroed")
        e_agg_zeroed = sem("e_agg_zeroed")
        e_pool = sem("e_pool")
        e_final = sem("e_final")
        e_val_ready = sem("e_val_ready")
        e_scattered = sem("e_scattered")
        e_in = sem("e_in")
        e_dve = sem("e_dve")
        e_max_ready = sem("e_max_ready")
        e_exp_ready = sem("e_exp_ready")
        e_agg_ready = sem("e_agg_ready")
        e_agg_stored = sem("e_agg_stored")
        e_agg_in = sem("e_agg_in")
        e_agg_turned = sem("e_agg_turned")
        e_aggT_ready = sem("e_aggT_ready")
        e_half_in = sem("e_half_in")
        e_summed = sem("e_summed")
        e_out_ready = sem("e_out_ready")
        e_out_stored = sem("e_out_stored")

        def read_flag(eng):
            eng.wait_ge(node_ready, 1)
            return eng.value_load(flag_i[0:1, 0:1], min_val=0, max_val=1)

        def dense0_sync(sp):
            with sp.Fori(0, HEADS) as h:
                sp.dma_start(d_head, table0_heads[:, :, bass.ds(h * DH, DH)]).then_inc(g_head_in, 16)
                with sp.Fori(0, TILES) as t:
                    n = h * TILES + t
                    sp.dma_start(d_adj, whole_rows[t]).then_inc(g_adj_in, 16)
                    sp.wait_ge(g_out_ready, n + 1)
                    sp.dma_start(att_rows[t][:, bass.ds(h * DH, DH)], d_out[:, 0:DH]).then_inc(g_stored, 16)
                    lone_wait(sp, node_ready, g_stored, 16 * (n + 1))

        def dense0_vector(dve):
            v = nc.vector
            with dve.Fori(0, HEADS) as h:
                with dve.Fori(0, TILES // KC) as c:
                    m = h * (TILES // KC) + c
                    v.tensor_tensor(d_diag, ident[:].unsqueeze(1).to_broadcast([P, KC, P]),
                                    src_dst[:].rearrange("p (c k) s -> p c k s", k=KC)[:, c, :, bass.ds(h + HEADS, 1)]
                                    .to_broadcast([P, KC, P]), ALU.mult).then_inc(g_diag_ready, 1)
                    dve.wait_ge(g_dst_summed, m + 1)
                    v.tensor_copy(d_dst.rearrange("p (c n) -> p c n", n=D)[:, c, :], bank[0][:]).then_inc(g_dst_ready, 1)
                    dve.wait_ge(g_dst_ready, m + 1)
                with dve.Fori(0, TILES) as t:
                    n = h * TILES + t
                    st = Steps(dve, g_dve, 10, n)
                    st.link(v.tensor_scalar(d_score, d_dst,
                                            src_dst[:].rearrange("p t s -> p (t s)")[:, bass.ds(t * 2 * HEADS + h, 1)],
                                            None, ALU.add))
                    st.link(v.scalar_tensor_tensor(out=d_score, in0=d_score, scalar=ALPHA, in1=d_score,
                                                   op0=ALU.mult, op1=ALU.max))
                    dve.wait_ge(g_adj_in, 16 * (n + 1))
                    st.link(v.tensor_scalar(d_adj, d_adj, 0.0, None, ALU.is_gt))
                    st.link(v.tensor_tensor(d_score, d_score, d_adj, ALU.mult))
                    st.link(v.tensor_scalar(d_adj, d_adj, 1.0, 9.0e15, ALU.subtract, ALU.mult))
                    st.link(v.tensor_tensor(d_score, d_score, d_adj, ALU.add))
                    st.link(v.tensor_reduce(d_max[:, 0:1], d_score, X_AXIS, ALU.max))
                    v.tensor_scalar(d_max[:, 1:2], d_max[:, 0:1], -1.0, None, ALU.mult).then_inc(g_max_ready, 1)
                    dve.wait_ge(g_exp_ready, n + 1)
                    st.link(v.reciprocal(d_sum[:, 1:2], d_sum[:, 0:1]))
                    dve.wait_ge(g_turned, n + 1)
                    for b in range(8):
                        last = v.tensor_copy(d_turned[:, b * D:(b + 1) * D], bank[b][:])
                        if b == 0:
                            st(last)
                    last.then_inc(g_turned_ready, 1)
                    dve.wait_ge(g_summed, n + 1)
                    v.tensor_scalar(d_out[:, 0:DH], bank[0][:, 0:DH], d_sum[:, 1:2], None, ALU.mult
                                    ).then_inc(g_out_ready, 1)
                    dve.wait_ge(g_stored, 16 * (n + 1))
                    st(v.tensor_copy(d_sum[:, 0:1], d_sum[:, 1:2]))
                    st.end()

        def dense0_scalar(act):
            with act.Fori(0, HEADS * TILES) as n:
                act.wait_ge(g_max_ready, n + 1)
                nc.scalar.activation(d_score, d_score, ACT.Exp, bias=d_max[:, 1:2], accum_out=d_sum[:, 0:1]
                                     ).then_inc(g_exp_ready, 1)

        def dense0_tensor(pe):
            with pe.Fori(0, HEADS) as h:
                with pe.Fori(0, TILES // KC) as c:
                    pe.wait_ge(g_diag_ready, h * (TILES // KC) + c + 1)
                    nc.tensor.matmul(bank[0][:], ones[:], d_diag.rearrange("p k n -> p (k n)"), start=True, stop=True
                                     ).then_inc(g_dst_summed, 1)
                with pe.Fori(0, TILES) as t:
                    n = h * TILES + t
                    pe.wait_ge(g_exp_ready, n + 1)
                    for b in range(TILES):
                        last = nc.tensor.transpose(bank[b // KC][:, b % KC * P:(b % KC + 1) * P],
                                                   d_score[:, b * P:(b + 1) * P], ident[:])
                    last.then_inc(g_turned, 1)
                    pe.wait_ge(g_head_in, 16 * (h + 1))
                    pe.wait_ge(g_turned_ready, n + 1)
                    for b in range(TILES):
                        last = nc.tensor.matmul(bank[0][:, 0:DH], d_turned[:, b * P:(b + 1) * P], d_head[:, b, :],
                                                start=(b == 0), stop=(b == TILES - 1))
                    last.then_inc(g_summed, 1)

        def dense1_sync(sp):
            for dst, src in ((d_weight[0], wqt.rearrange("(k p) n -> p k n", p=P)),
                             (d_weight[1], wkt.rearrange("(k p) n -> p k n", p=P)),
                             (d_bias[0], bq.partition_broadcast(P)), (d_bias[1], bk.partition_broadcast(P))):
                sp.dma_start(dst, src).then_inc(e_weights_in, 16)
            sp.wait_ge(e_zero_ready, 1)
            with sp.Fori(0, TILES) as t:
                for c in range(N // D):
                    sp.dma_start(agg_rows[t][:, c * D:(c + 1) * D], d_out).then_inc(e_agg_zeroed, 16)
            sp.wait_ge(e_agg_zeroed, 16 * 8 * TILES)
            with sp.Fori(0, HEADS) as h:
                with sp.Fori(0, TILES) as t:
                    for c in range(N // D):
                        sp.dma_start(full_rows[t][:, c * D:(c + 1) * D], d_out).then_inc(e_zeroed, 16)
                    lone_wait(sp, node_ready, e_zeroed, 16 * 8 * (h * TILES + t + 1))
                with sp.Fori(0, TILES) as t:
                    n = h * TILES + t
                    sp.wait_ge(e_scattered, 16 * PCOL * (h + 1))
                    sp.dma_start(d_score, full_rows[t]).then_inc(e_in, 16)
                    sp.dma_start(d_adj, whole_rows[t]).then_inc(e_in, 16)
                    sp.dma_start(d_agg, agg_rows[t]).then_inc(e_in, 16)
                    sp.wait_ge(e_agg_ready, n + 1)
                    sp.dma_start(agg_rows[t], d_agg).then_inc(e_agg_stored, 16)
                    lone_wait(sp, node_ready, e_agg_stored, 16 * (n + 1))
            with sp.Fori(0, TILES) as t:
                sp.dma_start(d_score, agg_rows[t]).then_inc(e_agg_in, 16)
                for g in both:
                    if g == 1:
                        sp.wait_ge(e_summed, 2 * t + 1)
                    sp.dma_start(d_h2, table1_halves[g]).then_inc(e_half_in, 16)
                sp.wait_ge(e_out_ready, t + 1)
                sp.dma_start(out_rows[t], d_out).then_inc(e_out_stored, 16)
                lone_wait(sp, node_ready, e_out_stored, 16 * (t + 1))

        def dense1_gpsimd(pool):
            g = nc.gpsimd
            with pool.Fori(0, PCOL) as c:
                g.tensor_copy(d_idx[:], pair_sb[:, c, :]).then_inc(e_pool, 1)
                lone_wait(pool, pairs_ready, e_pool, c + 1)
                for n in both:
                    g.indirect_dma_start(d_pair_h[n], None, table1,
                                         bass.IndirectOffsetOnAxis(ap=d_idx[:, n:n + 1], axis=0),
                                         bounds_check=N - 1, oob_is_err=False).then_inc(e_rows_in, 16)
                pool.wait_ge(e_pair_ready, c + 1)
            with pool.Fori(0, HEADS) as h:
                lone_wait(pool, node_ready, e_zeroed, 16 * 8 * TILES * (h + 1))
                with pool.Fori(0, PCOL) as c:
                    n = h * PCOL + c
                    g.tensor_copy(d_idx[:, 0:1], pair_idx[:, bass.ds(c, 1)]).then_inc(e_pool, 1)
                    g.tensor_copy(d_val[:], d_pair_att_flat[0:PP, bass.ds(c * HEADS + h, 1)]).then_inc(e_pool, 1)
                    lone_wait(pool, pairs_ready, e_pool, 2 * n + PCOL + 2)
                    g.indirect_dma_start(full_flat, bass.IndirectOffsetOnAxis(ap=d_idx[:, 0:1], axis=0), d_val[:], None,
                                         bounds_check=N * N - 1, oob_is_err=False).then_inc(e_scattered, 16)
                    pool.wait_ge(e_scattered, 16 * (n + 1))

        def dense1_scalar(act):
            with act.Fori(0, HEADS * TILES) as n:
                act.wait_ge(e_max_ready, n + 1)
                nc.scalar.activation(d_score, d_score, ACT.Exp, bias=d_max[:, 1:2], accum_out=d_sum[:, 0:1]
                                     ).then_inc(e_exp_ready, 1)

        def dense1_tensor(pe):
            pe.wait_ge(e_weights_in, 64)
            with pe.Fori(0, PCOL) as c:
                pe.wait_ge(e_rows_in, 32 * (c + 1))
                for n in both:
                    for k in range(KC):
                        last = nc.tensor.transpose(bank[n][:, k * P:k * P + PP], d_pair_h[n][:, k * P:(k + 1) * P],
                                                   ident[0:PP, 0:PP])
                last.then_inc(e_turned, 1)
                pe.wait_ge(e_turned_ready, c + 1)
                for n in both:
                    for k in range(KC):
                        last = nc.tensor.matmul(bank[2 + n][0:PP, :], d_pair_hT[n][:, k, 0:PP], d_weight[n][:, k, :],
                                                start=(k == 0), stop=(k == KC - 1))
                last.then_inc(e_proj, 1)
            with pe.Fori(0, TILES) as t:
                pe.wait_ge(e_agg_in, 16 * (t + 1))
                for b in range(TILES):
                    last = nc.tensor.transpose(bank[b // KC][:, b % KC * P:(b % KC + 1) * P],
                                               d_score[:, b * P:(b + 1) * P], ident[:])
                last.then_inc(e_agg_turned, 1)
                pe.wait_ge(e_aggT_ready, t + 1)
                for b in range(TILES):
                    if b % half == 0:
                        pe.wait_ge(e_half_in, 16 * (2 * t + b // half + 1))
                    last = nc.tensor.matmul(bank[0][:], d_adj[:, b * P:(b + 1) * P], d_h2[:, b % half, :],
                                            start=(b == 0), stop=(b == TILES - 1))
                    if b % half == half - 1:
                        last.then_inc(e_summed, 1)

        def dense1_vector(dve):
            v = nc.vector
            v.memset(d_out, 0.0).then_inc(e_zero_ready, 1)
            v.tensor_scalar(off_diag[:], ident[:], 0.0, None, ALU.is_equal).then_inc(e_final, 1)
            v.tensor_scalar(on_diag[:], ident[:], SELF_SCORE, None, ALU.mult).then_inc(e_final, 1)
            dve.wait_ge(e_final, 2)
            dve.wait_ge(e_weights_in, 64)
            with dve.Fori(0, PCOL) as c:
                st = Steps(dve, e_pair_dve, 5, c)
                dve.wait_ge(e_turned, c + 1)
                for n in both:
                    last = v.tensor_copy(d_pair_hT[n][:, :, 0:PP],
                                         bank[n][:].rearrange("p (k n) -> p k n", k=KC)[:, :, 0:PP])
                    if n == 0:
                        st(last)
                last.then_inc(e_turned_ready, 1)
                dve.wait_ge(e_proj, c + 1)
                for n in both:
                    st.link(v.tensor_tensor(d_pair_q[n], bank[2 + n][0:PP, :], d_bias[n][0:PP, :], ALU.add))
                st.link(v.tensor_tensor(d_pair_q[0], d_pair_q[0], d_pair_q[1], ALU.mult))
                st.link(v.tensor_reduce(d_pair_att[0:PP, c, :], d_pair_q[0].rearrange("p (h d) -> p h d", h=HEADS),
                                        X_AXIS, ALU.add))
                v.tensor_scalar(d_pair_att[0:PP, c, :], d_pair_att[0:PP, c, :], DH ** -0.5, None, ALU.mult
                                ).then_inc(e_pair_ready, 1)
                st.end()
            with dve.Fori(0, HEADS) as h:
                with dve.Fori(0, TILES) as t:
                    n = h * TILES + t
                    st = Steps(dve, e_dve, 8, n)
                    dve.wait_ge(e_in, 48 * (n + 1))
                    st.link(v.tensor_scalar(d_adj, d_adj, 1.0, None, ALU.is_equal))
                    st.link(v.tensor_tensor(d_score, d_score, d_adj, ALU.mult))
                    st.link(v.tensor_scalar(d_adj, d_adj, 1.0, NEGBIG, ALU.subtract, ALU.mult))
                    st.link(v.tensor_tensor(d_score, d_score, d_adj, ALU.add))
                    block_own = d_score[:, bass.ds(t * P, P)]
                    st.link(v.tensor_tensor(block_own, block_own, off_diag[:], ALU.mult))
                    st.link(v.tensor_tensor(block_own, block_own, on_diag[:], ALU.add))
                    st.link(v.tensor_reduce(d_max[:, 0:1], d_score, X_AXIS, ALU.max))
                    v.tensor_scalar(d_max[:, 1:2], d_max[:, 0:1], -1.0, None, ALU.mult).then_inc(e_max_ready, 1)
                    dve.wait_ge(e_exp_ready, n + 1)
                    st.link(v.reciprocal(d_sum[:, 1:2], d_sum[:, 0:1]))
                    v.tensor_scalar(d_sum[:, 1:2], d_sum[:, 1:2], 1.0 / HEADS, None, ALU.mult).then_inc(e_final, 1)
                    dve.wait_ge(e_final, n + 3)
                    v.scalar_tensor_tensor(out=d_agg, in0=d_score, scalar=d_sum[:, 1:2], in1=d_agg,
                                           op0=ALU.mult, op1=ALU.add).then_inc(e_agg_ready, 1)
                    dve.wait_ge(e_agg_ready, n + 1)
                    st.end()
            with dve.Fori(0, TILES) as t:
                dve.wait_ge(e_agg_turned, t + 1)
                for b in range(8):
                    last = v.tensor_copy(d_adj[:, b * D:(b + 1) * D], bank[b][:])
                last.then_inc(e_aggT_ready, 1)
                dve.wait_ge(e_summed, 2 * t + 2)
                v.tensor_tensor(d_out, bank[0][:], x_all[:, t, :], ALU.add).then_inc(e_out_ready, 1)
                dve.wait_ge(e_out_stored, 16 * (t + 1))
        block = ctx.enter_context(nc.Block())

        @block.sync
        def _(sp):
            sp.dma_start(pair_sb[:], pairs.rearrange("(p c) two -> p c two", c=PCOL)).then_inc(pair_in, 16)
            sp.dma_start(w0_sb, w0.rearrange("(k p) n -> p k n", p=P)).then_inc(weights0_in, 16)
            sp.dma_start(a_rows[:, 0, :], a1.partition_broadcast(P)).then_inc(weights0_in, 16)
            sp.dma_start(a_rows[:, 1, :], a2.partition_broadcast(P)).then_inc(weights0_in, 16)
            sp.dma_start(b4_row[:], b4.partition_broadcast(P)).then_inc(weights1_in, 16)

            def front(i, first):
                for u in both:
                    if not first:
                        sp.wait_ge(adj_searched, 2 * i + u - 1)
                    sp.dma_start(x_all[:, 2 * i + u, :], x_rows[2 * i + u]).then_inc(x_in[u], 16)
                    sp.dma_start(adj_sb[u][:, :, 0:SEGW], adj_tiles[2 * i + u]).then_inc(adj_in[u], 16)

            front(0, True)
            sp.dma_start(diag[:], bass.AP(tensor=adj.tensor, offset=0, ap=[[N + 1, P], [(N + 1) * P, TILES]]),
                         allow_slow_non_contiguous=True).then_inc(diag_in, 16)
            with sp.Fori(1, STEPS) as i:
                front(i, False)
            sp.dma_start(w1_sb[:], w1t.rearrange("(k p) n -> p k n", p=P)).then_inc(weights2_in, 16)
            sp.dma_start(w2_sb[:], w2t.rearrange("(k p) n -> p k n", p=P)).then_inc(weights2_in, 16)
            sp.dma_start(w3_sb[:], w3t).then_inc(weights2_in, 16)
            sp.dma_start(w4_sb[:], w4t.rearrange("(k p) n -> p k n", p=P)).then_inc(weights2_in, 16)
            sp.dma_start(b1_sb[:], b1).then_inc(weights2_in, 16)
            sp.dma_start(b2_sb[:], b2).then_inc(weights2_in, 16)
            sp.dma_start(b3_sb[:], b3).then_inc(weights2_in, 16)
            sp.wait_ge(consts_made, N_CONSTS)
            for n in range(8):
                sp.dma_start(score_dram.rearrange("(n p r) h -> n p (r h)", n=8, p=P)[n], zeros[:]
                             ).then_inc(score_zeroed, 16)
            sp.wait_ge(node_ready, 1)
            sp.dma_start(keys_dram.rearrange("(t p) k -> p t k", p=P), node[:, :, 0:SLOTS]).then_inc(keys_stored, 16)

            for u in both:
                sp.wait_ge(wh_stored[u], 16 * STEPS)
            flag = read_flag(sp)
            with sp.If(flag > 0):
                dense0_sync(sp)

            def dense_att(j):
                with sp.If(flag > 0):
                    sp.wait_ge(att_ready, 2 * j + 2)
                    sp.dma_start(att, att_steps[j]).then_inc(g_att_in, 16)

            def self_rows(jj, q, first):
                if not first:
                    sp.wait_ge(agg_summed, 4 * jj + 2 * q - 2)
                sp.dma_start(gath[q][:, EC:GC, :], table0_steps[2 * jj + q]).then_inc(self_in[q], 16)

            for q in both:
                self_rows(0, q, True)
            with sp.Fori(1, STEPS // 2) as jj:
                for q in both:
                    self_rows(jj, q, False)
                    dense_att(2 * jj + q - 2)
            for q in both:
                dense_att(STEPS - 2 + q)

            sp.wait_ge(score_zeroed, 16 * 8)
            for u in both:
                sp.wait_ge(h2_stored[u], 16 * STEPS)
            sp.wait_ge(b4_added, TILES)
            sp.dma_start(wq_sb, wqt.rearrange("(k p) n -> p k n", p=P)).then_inc(late_in, 16)
            sp.dma_start(wk_sb, wkt.rearrange("(k p) n -> p k n", p=P)).then_inc(late_in, 16)
            sp.dma_start(bq_row[:], bq.partition_broadcast(P)).then_inc(late_in, 16)
            sp.dma_start(bk_row[:], bk.partition_broadcast(P)).then_inc(late_in, 16)

            def late_rows(jj, q, first):
                if not first:
                    sp.wait_ge(agg1_summed, 4 * jj + 2 * q - 2)
                    sp.wait_ge(weight_ready, 2 * jj + q - 1)
                sp.dma_start(gath[q][:, EC:GC, 0:D], table1_steps[2 * jj + q]).then_inc(self1_in[q], 16)
                if first and q == 0:
                    sp.wait_ge(hit_stored, 16)
                sp.dma_start(score_in[q], score_steps[2 * jj + q]).then_inc(score_in_sem[q], 16)

            def store_out(jj, q):
                for u in both:
                    sp.wait_ge(out_ready, 4 * jj + 2 * q + u + 1)
                    sp.dma_start(out_rows[4 * jj + 2 * q + u], out_sb[u]).then_inc(out_stored[u], 16)

            for q in both:
                late_rows(0, q, True)
            with sp.Fori(1, STEPS // 2) as jj:
                for q in both:
                    late_rows(jj, q, False)
                    store_out(jj - 1, q)
            for q in both:
                store_out(STEPS // 2 - 1, q)
            for u in both:
                sp.wait_ge(out_stored[u], 16 * STEPS)
            with sp.If(flag > 0):
                dense1_sync(sp)

        @block.gpsimd
        def _(pool):
            g = nc.gpsimd
            g.iota(iota[:], pattern=[[1, EDGES]], base=0, channel_multiplier=0,
                   allow_small_or_imprecise_dtypes=True).then_inc(consts_made, 1)
            g.memset(ident[:], 0.0).then_inc(consts_made, 1)
            g.memset(before[:], 1.0).then_inc(consts_made, 1)
            g.memset(ones[:], 1.0).then_inc(consts_made, 1)
            g.memset(zeros[:], 0.0).then_inc(consts_made, 1)
            pool.wait_ge(consts_made, 5)
            g.affine_select(out=ident[:], in_=ident[:], compare_op=ALU.not_equal, fill=1.0, base=0,
                            pattern=[[1, P]], channel_multiplier=-1).then_inc(consts_made, 1)
            g.affine_select(out=before[:], in_=before[:], compare_op=ALU.is_gt, fill=0.0, base=0,
                            pattern=[[1, P]], channel_multiplier=-1).then_inc(consts_made, 1)
            g.iota(seg_base[:], pattern=[[SEGW, SEG], [0, 8]], base=1, channel_multiplier=0,
                   allow_small_or_imprecise_dtypes=True).then_inc(consts_made, 1)
            g.iota(self_key[:], pattern=[[P, TILES]], base=1, channel_multiplier=1,
                   allow_small_or_imprecise_dtypes=True).then_inc(consts_made, 1)
            g.iota(edge_pos[:], pattern=[[0, PAIR], [P, CH]], base=0, channel_multiplier=1,
                   allow_small_or_imprecise_dtypes=True).then_inc(consts_made, 1)

            pool.wait_ge(pairs_ready, 1)
            with pool.Fori(0, PCOL // PG) as n:
                g.tensor_copy(idx8[:], pair_idx[:].rearrange("p (n c) -> p n c", c=PG)[:, n, :]).then_inc(pool_pair, 1)
                lone_wait(pool, pairs_ready, pool_pair, 2 * n + 1)
                for c in range(PG):
                    g.indirect_dma_start(adj8[:, c:c + 1], None, adj_flat,
                                         bass.IndirectOffsetOnAxis(ap=idx8[:, c:c + 1], axis=0),
                                         bounds_check=N * N - 1, oob_is_err=False).then_inc(pair_adj_in, 16)
                pool.wait_ge(pair_adj_in, 16 * PG * (n + 1))
                g.tensor_copy(pair_adj[:].rearrange("p (n c) -> p n c", c=PG)[:, n, :], adj8[:]).then_inc(pool_pair, 1)
            pool.wait_ge(weights1_in, 16)
            with pool.Fori(0, TILES) as t:
                pool.wait_ge(h_made, t + 1)
                g.tensor_tensor(x_all[:, t, :], x_all[:, t, :], b4_row[:], ALU.add).then_inc(b4_added, 1)

            for u in both:
                pool.wait_ge(wh_stored[u], 16 * STEPS)
            flag = read_flag(pool)
            with pool.If(flag > 0):
                pool.wait_ge(g_stored, 16 * HEADS * TILES)

            def gather(table, width, jj, q, first, ready, used, into):
                if not first:
                    pool.wait_ge(used, 4 * jj + 2 * q - 2)
                lone_wait(pool, pairs_ready, ready, 2 * jj + q + 1)
                for c in range(EC):
                    g.indirect_dma_start(gath[q][:, c, 0:width], None, table,
                                         bass.IndirectOffsetOnAxis(ap=edge_idx[q][:, c:c + 1], axis=0),
                                         bounds_check=N - 1, oob_is_err=False).then_inc(into[q], 16)

            for q in both:
                gather(table0, ROW, 0, q, True, idx_ready, agg_summed, gath_in)
            with pool.Fori(1, STEPS // 2) as jj:
                for q in both:
                    gather(table0, ROW, jj, q, False, idx_ready, agg_summed, gath_in)

            for u in both:
                pool.wait_ge(h2_stored[u], 16 * STEPS)
            pool.wait_ge(keys_stored, 16)
            g.memset(hit_keys[:], 0.0).then_inc(pool_pair, 1)
            pool.wait_ge(pool_pair, 2 * (PCOL // PG) + 1)
            pool.wait_ge(hit_summed, 1)
            pool.wait_ge(dve_mid, MID_TICKS)
            for dst, table, idx in ((hit_h[0], table1, hit_sub), (hit_h[1], table1, hit_obj),
                                    (hit_keys[:], keys_dram, hit_sub)):
                g.indirect_dma_start(dst, None, table, bass.IndirectOffsetOnAxis(ap=idx[:, 0:1], axis=0),
                                     bounds_check=N - 1, oob_is_err=False).then_inc(hit_in, 16)
            gather(table1, D, 0, 0, True, idx1_ready, agg1_summed, gath1_in)
            pool.wait_ge(hit_att_ready, 1)
            g.indirect_dma_start(score_dram, bass.IndirectOffsetOnAxis(ap=hit_dst[:, 0:1], axis=0), hit_att[:], None,
                                 bounds_check=N * SLOTS - 1, oob_is_err=False).then_inc(hit_stored, 16)
            gather(table1, D, 0, 1, True, idx1_ready, agg1_summed, gath1_in)
            with pool.Fori(1, STEPS // 2) as jj:
                for q in both:
                    gather(table1, D, jj, q, False, idx1_ready, agg1_summed, gath1_in)
            for u in both:
                pool.wait_ge(out_stored[u], 16 * STEPS)
            with pool.If(flag > 0):
                dense1_gpsimd(pool)

        @block.scalar
        def _(act):
            s = nc.scalar

            def front(i, first):
                for u in both:
                    act.wait_ge(var_ready, 2 * i + u + 1)
                    s.activation(std[u][:], mean_var[u][:, 1:2], ACT.Sqrt, bias=eps_col[:, 0:1]).then_inc(std_ready, 1)
                    act.wait_ge(ln_ready, 2 * i + u + 1)
                    if not first:
                        act.wait_ge(h_turned, 2 * i + u - 1)
                    s.activation(h_sb[u], x_all[:, 2 * i + u, :], ACT.Relu, bias=ln_shift[u][:, 0:1],
                                 scale=ln_scale[u][:, 0:1]).then_inc(h_made, 1)
                for u in both:
                    act.wait_ge(h_turned, 2 * i + u + 1)
                    if not first:
                        act.wait_ge(wh_summed, 2 * i + u - 1)
                    s.copy(hT[u].rearrange("p k n -> p (k n)"), bank[u][:]).then_inc(hT_ready, 1)
                for u in both:
                    act.wait_ge(wh_summed, 2 * i + u + 1)
                    if not first:
                        act.wait_ge(wh_stored[u], 16 * i)
                    s.copy(wh_row[u][:, 0:D], bank[2 + u][:]).then_inc(wh_copied, 1)
                    s.copy(wh_row[u][:, D:ROW], bank[4 + u][:, HEADS:2 * HEADS]).then_inc(wh_copied, 1)
                    s.copy(src_dst[:, 2 * i + u, :], bank[4 + u][:, 0:2 * HEADS]).then_inc(wh_copied, 1)
                    act.wait_ge(wh_copied, 6 * i + 3 * u + 2)
                    act.dma_start(table0_rows[2 * i + u], wh_row[u]).then_inc(wh_stored[u], 16)

            front(0, True)
            with act.Fori(1, STEPS) as i:
                front(i, False)

            def info(j, q):
                act.wait_ge(info_summed, j + 1)
                if not isinstance(j, int) or j >= 2:
                    act.wait_ge(exponent_ready, j - 1)
                s.copy(edge_info[q][:].rearrange("p c v -> p (c v)"), bank[0][:, 0:EC * VW]).then_inc(info_ready, 1)

            def edges(j, q):
                act.wait_ge(exponent_ready, j + 1)
                if not isinstance(j, int) or j >= 2:
                    act.wait_ge(agg_summed, 2 * j - 2)
                s.activation(prob[q][:], edge_e[:, 2], ACT.Exp).then_inc(prob_ready, 1)

            def tail(j, q):
                with act.If(flag > 0):
                    lone_wait(act, node_ready, g_att_in, 16 * (j + 1))
                act.wait_ge(att_ready, 2 * j + 2)
                if not isinstance(j, int) or j >= 1:
                    act.wait_ge(enc_turned, 2 * j)
                    for u in both:
                        act.wait_ge(h2_stored[u], 16 * j)
                s.activation(att_exp, att, ACT.Exp).then_inc(elu_parts, 1)
                s.activation(att_relu, att, ACT.Relu).then_inc(elu_parts, 1)
                for u in both:
                    act.wait_ge(enc_turned, 2 * j + u + 1)
                    s.activation(encT[:, :, u * P:(u + 1) * P], bank[4 + u][:].rearrange("p (k n) -> p k n", k=KC),
                                 ACT.Identity, bias=neg_one[:, 0:1]).then_inc(encT_ready, 1)
                act.wait_ge(mlp_summed, 5 * j + 1)
                for m in range(2):
                    s.activation(z1[:, m, :], bank[6][:, 256 * m:256 * (m + 1)], ACT.Relu,
                                 bias=b1_sb[:, m:m + 1]).then_inc(mlp_relu, 1)
                act.wait_ge(mlp_summed, 5 * j + 2)
                s.activation(z2, bank[7][:, 0:PAIR * P], ACT.Relu, bias=b2_sb[:, 0:1]).then_inc(mlp_relu, 1)
                act.wait_ge(mlp_summed, 5 * j + 3)
                for m in range(2):
                    s.activation(z3[:, m, :], bank[6][:, 256 * m:256 * (m + 1)], ACT.Relu,
                                 bias=b3_sb[:, m:m + 1]).then_inc(mlp_relu, 1)
                for u in both:
                    act.wait_ge(var2_ready, 2 * j + u + 1)
                    s.activation(std[u][:], mean_var[u][:, 1:2], ACT.Sqrt, bias=eps_col[:, 0:1]).then_inc(std2_ready, 1)
                for u in both:
                    act.wait_ge(ln2_ready, 2 * j + u + 1)
                    s.activation(att_relu[:, u, :], x_all[:, 2 * j + u, :], ACT.Relu, bias=ln_shift[u][:, 0:1],
                                 scale=ln_scale[u][:, 0:1]).then_inc(h2_made, 1)
                    act.wait_ge(h2_made, 2 * j + u + 1)
                    act.dma_start(table1_rows[2 * j + u], att_relu[:, u, :]).then_inc(h2_stored[u], 16)

            act.wait_ge(weights2_in, 7 * 16)
            flag = read_flag(act)
            with act.If(flag > 0):
                dense0_scalar(act)
            info(0, 0)

            def step(j, q, last=False):
                if not last:
                    info(j + 1, 1 - q)
                edges(j, q)
                tail(j, q)

            step(0, 0)
            step(1, 1)
            with act.Fori(1, STEPS // 2 - 1) as jj:
                for q in both:
                    step(2 * jj + q, q)
            step(STEPS - 2, 0)
            step(STEPS - 1, 1, last=True)

            for n in both:
                act.wait_ge(hit_turned, n + 1)
                if n:
                    act.wait_ge(hit_proj, 1)
                s.copy(hit_hT.rearrange("p k n -> p (k n)"), bank[n][:]).then_inc(hit_hT_ready, 1)
            with act.Fori(0, STEPS) as j:
                act.wait_ge(soft_ready, j + 1)
                s.activation(soft, soft, ACT.Exp).then_inc(soft_exp, 1)
            with act.If(flag > 0):
                dense1_scalar(act)

        @block.tensor
        def _(pe):
            mm = nc.tensor.matmul
            turn = nc.tensor.transpose
            pe.wait_ge(consts_made, N_CONSTS)
            pe.wait_ge(weights0_in, 48)
            pe.wait_ge(fold_ready, 1)

            def front(i, first):
                for u in both:
                    pe.wait_ge(h_made, 2 * i + u + 1)
                    for k in range(KC):
                        last = turn(bank[u][:, k * P:(k + 1) * P], h_sb[u][:, k * P:(k + 1) * P], ident[:])
                    last.then_inc(h_turned, 1)
                for u in both:
                    pe.wait_ge(hT_ready, 2 * i + u + 1)
                    if not first:
                        pe.wait_ge(wh_copied, 6 * i + 3 * u - 3)
                    for k in range(KC):
                        mm(bank[2 + u][:], hT[u][:, k, :], w0_sb[:, k, :], start=(k == 0), stop=(k == KC - 1))
                    for k in range(KC):
                        last = mm(bank[4 + u][:, 0:2 * HEADS], hT[u][:, k, :], a_fold[:, k, :],
                                  start=(k == 0), stop=(k == KC - 1))
                    last.then_inc(wh_summed, 1)

            front(0, True)
            with pe.Fori(1, STEPS) as i:
                front(i, False)

            pe.wait_ge(counts_ready, 1)
            mm(bank[6][:, 0:TILES], before[:], count[:], start=True, stop=True)
            mm(bank[6][:, TILES:2 * TILES], ones[:], count[:], start=True, stop=True)
            mm(bank[6][:, 64:65], before[:], hit_end[:, 0:1], start=True, stop=True)
            mm(bank[6][:, 65:66], ones[:], hit_end[:, 0:1], start=True, stop=True).then_inc(offsets_summed, 1)
            pe.wait_ge(hit_rows_ready, 1)
            mm(bank[7][:, 0:17], hit_rows[:], hit_node[:], start=True, stop=True).then_inc(hit_summed, 1)
            pe.wait_ge(flags_ready, 1)
            mm(bank[3][:, 0:1], ones[:], flag_f[:, 0:1], start=True, stop=True).then_inc(flags_summed, 1)

            def info(j, q):
                for u in both:
                    pe.wait_ge(rows_ready, 2 * j + u + 1)
                    if u == 0 and (not isinstance(j, int) or j >= 1):
                        pe.wait_ge(info_ready, j)
                    for c in range(CH):
                        last = mm(bank[0][:, (u * CH + c) * VW:(u * CH + c + 1) * VW],
                                  row_hot[q][:, u, c * P:(c + 1) * P], step_node(j)[:, u, :], start=True, stop=True)
                last.then_inc(info_summed, 1)

            def slots(j, q):
                pe.wait_ge(placed_ready, j + 1)
                pe.wait_ge(hot_ready, j + 1)
                if not isinstance(j, int) or j >= 1:
                    pe.wait_ge(exponent_ready, j)
                for u in both:
                    for c in range(CH):
                        last = mm(bank[1][:, u * P:(u + 1) * P], edge_hot[q][:, u * CH + c, :],
                                  placed[:, u * CH + c].rearrange("p k h -> p (k h)"),
                                  start=(c == 0), stop=(c == CH - 1))
                last.then_inc(slots_summed, 1)
                pe.wait_ge(row_max_ready, j + 1)
                for u in both:
                    for c in range(CH):
                        n = u * CH + c
                        last = mm(bank[0][:, EC * VW + n * HEADS:EC * VW + (n + 1) * HEADS],
                                  row_hot[q][:, u, c * P:(c + 1) * P], row_max[q][:, u, :], start=True, stop=True)
                last.then_inc(edge_max_summed, 1)

            def aggregate(j, q):
                pe.wait_ge(prob_ready, j + 1)
                if not isinstance(j, int) or j >= 1:
                    pe.wait_ge(att_ready, 2 * j)
                for u in both:
                    for c in range(CH + 1):
                        n = u * CH + c if c < CH else EC + u
                        hot = edge_hot[q][:, n, :] if c < CH else ident[:]
                        mm(bank[1][:, 2 * P + u * HEADS:2 * P + (u + 1) * HEADS], hot, prob[q][:, n, :],
                           start=(c == 0), stop=(c == CH))
                for u in both:
                    for c in range(CH + 1):
                        n = u * CH + c if c < CH else EC + u
                        hot = edge_hot[q][:, n, :] if c < CH else ident[:]
                        if c in (0, 2, CH):
                            pe.wait_ge(scaled, 5 * j + (3 if c == CH else 1 + c // 2 + 3 * u))
                        last = mm(bank[2 + u][:], hot, gath[q][:, n, 0:D], start=(c == 0), stop=(c == CH))
                    last.then_inc(agg_summed, 1)

            def tail(j, q):
                pe.wait_ge(enc_ready, j + 1)
                if not isinstance(j, int) or j >= 1:
                    pe.wait_ge(ln2_ready, 2 * j)
                for u in both:
                    for k in range(KC):
                        last = turn(bank[4 + u][:, k * P:(k + 1) * P], att_exp[:, u, k * P:(k + 1) * P], ident[:])
                    last.then_inc(enc_turned, 1)
                pe.wait_ge(encT_ready, 2 * j + 2)
                for m in range(2):
                    for k in range(KC):
                        last = mm(bank[6][:, 256 * m:256 * (m + 1)], w1_sb[:, k, m * P:(m + 1) * P], encT[:, k, :],
                                  start=(k == 0), stop=(k == KC - 1))
                last.then_inc(mlp_summed, 1)
                pe.wait_ge(mlp_relu, 5 * j + 2)
                for k in range(2):
                    last = mm(bank[7][:, 0:PAIR * P], w2_sb[:, k, :], z1[:, k, :], start=(k == 0), stop=(k == 1))
                last.then_inc(mlp_summed, 1)
                pe.wait_ge(mlp_relu, 5 * j + 3)
                for m in range(2):
                    last = mm(bank[6][:, 256 * m:256 * (m + 1)], w3_sb[:, m * P:(m + 1) * P], z2, start=True, stop=True)
                last.then_inc(mlp_summed, 1)
                pe.wait_ge(mlp_relu, 5 * j + 5)
                for u in both:
                    for k in range(2):
                        last = mm(bank[4 + u][:], z3[:, k, u * P:(u + 1) * P], w4_sb[:, k, :],
                                  start=(k == 0), stop=(k == 1))
                    last.then_inc(mlp_summed, 1)

            flag = read_flag(pe)
            with pe.If(flag > 0):
                dense0_tensor(pe)
            info(0, 0)

            def step(j, q, last=False):
                if not last:
                    info(j + 1, 1 - q)
                slots(j, q)
                aggregate(j, q)
                tail(j, q)

            pe.wait_ge(weights2_in, 7 * 16)
            step(0, 0)
            step(1, 1)
            with pe.Fori(1, STEPS // 2 - 1) as jj:
                for q in both:
                    step(2 * jj + q, q)
            step(STEPS - 2, 0)
            step(STEPS - 1, 1, last=True)

            pe.wait_ge(hit_in, 48)
            for n in both:
                for k in range(KC):
                    last = turn(bank[n][:, k * P:(k + 1) * P], hit_h[n][:, k * P:(k + 1) * P], ident[:])
                last.then_inc(hit_turned, 1)
            pe.wait_ge(late_in, 64)
            for n in both:
                pe.wait_ge(hit_hT_ready, n + 1)
                for k in range(KC):
                    last = mm(bank[6 + n][:], hit_hT[:, k, :], (wq_sb, wk_sb)[n][:, k, :],
                              start=(k == 0), stop=(k == KC - 1))
                last.then_inc(hit_proj, 1)

            def late(jj, q, first):
                j = 2 * jj + q
                if not first:
                    pe.wait_ge(out_ready, 2 * j - 2)
                pe.wait_ge(rows1_ready, j + 1)
                pe.wait_ge(weight_ready, j + 1)
                for n in range(EC):
                    last = mm(bank[0][:, n * SLOTS:(n + 1) * SLOTS], row_hot[q][:, n // CH, n % CH * P:(n % CH + 1) * P],
                              weight[q][:, n // CH, 0:SLOTS], start=True, stop=True)
                last.then_inc(edge_w_summed, 1)
                pe.wait_ge(hot1_ready, j + 1)
                pe.wait_ge(gath1_in[q], 16 * EC * (jj + 1))
                pe.wait_ge(self1_in[q], 16 * (jj + 1))
                for u in both:
                    for c in range(CH + 1):
                        n = u * CH + c if c < CH else EC + u
                        hot = edge_hot[q][:, n, :] if c < CH else self_hot[u][:]
                        last = mm(bank[2 + 2 * q + u][:], hot, gath[q][:, n, 0:D], start=(c == 0), stop=(c == CH))
                    last.then_inc(agg1_summed, 1)

            for q in both:
                late(0, q, True)
            with pe.Fori(1, STEPS // 2) as jj:
                for q in both:
                    late(jj, q, False)
            for u in both:
                pe.wait_ge(out_stored[u], 16 * STEPS)
            with pe.If(flag > 0):
                dense1_tensor(pe)

        @block.vector
        def _(dve):
            v = nc.vector

            st = Steps(dve, dve_start, START_TICKS, 0)
            for u in both:
                st(v.memset(adj_sb[u][:, :, SEGW:SEGP], 1.0))
            st(v.memset(ones8[:], 1.0))
            st(v.memset(neg_one[:], -1.0))
            st(v.memset(eps_col[:], EPS))
            st(v.memset(hit_key[:], 0.0))
            st(v.memset(slot_bias[:, :, SLOTS:SLOTS + 1], 0.0))
            dve.wait_ge(pair_in, 16)
            st(v.scalar_tensor_tensor(out=pair_flat[:], in0=pair_sb[:, :, 0], scalar=float(N), in1=pair_sb[:, :, 1],
                                      op0=ALU.mult, op1=ALU.add))
            st.link(v.tensor_tensor(pair_ne[:], pair_sb[:, :, 0], pair_sb[:, :, 1], ALU.not_equal))
            v.tensor_copy(pair_idx[:], pair_flat[:]).then_inc(pairs_ready, 1)
            dve.wait_ge(weights0_in, 48)
            for k in range(KC):
                for a in range(2):
                    st.link(v.tensor_tensor(fold_tmp, w0_sb[:, k, :], a_rows[:, a, :], ALU.mult))
                    last = v.tensor_reduce(a_fold[:, k, a * HEADS:(a + 1) * HEADS],
                                           fold_tmp.rearrange("p (h d) -> p h d", h=HEADS), X_AXIS, ALU.add)
                    if (k, a) != (KC - 1, 1):
                        st.link(last)
            last.then_inc(fold_ready, 1)
            st.end()

            def alone(sem, value):
                lone_wait(dve, fold_ready, sem, value)

            def search(u, g):
                return v.max_index(found[u][:, g, :], ones8[:], adj_sb[u][:, g, :])

            def neighbours(t, u, st, k):
                if k == 0:
                    st(v.tensor_tensor(key_raw[u][:], found[u][:], seg_base[:], ALU.add))
                elif k == 1:
                    st.after(st.k)
                    st(v.scalar_tensor_tensor(out=key_any[u][:], in0=found[u][:], scalar=float(SEGW), in1=key_raw[u][:],
                                              op0=ALU.is_lt, op1=ALU.mult))
                elif k == 2:
                    st.after(st.k)
                    flat = key_any[u][:].rearrange("p s c -> p (s c)")
                    st(v.scalar_tensor_tensor(out=key_nbr[u][:], in0=flat, scalar=self_key[:, bass.ds(t, 1)], in1=flat,
                                              op0=ALU.not_equal, op1=ALU.mult))
                elif k == 3:
                    alone(st.sem, st.base + st.k)
                    st(v.max(key16[u][:, 0:8], key_nbr[u][:]))
                elif k == 4:
                    alone(st.sem, st.base + st.k)
                    st(v.match_replace(key_left[u][:], key16[u][:, 0:8], key_nbr[u][:], 0.0))
                elif k == 5:
                    alone(st.sem, st.base + st.k)
                    st(v.max(key16[u][:, 8:16], key_left[u][:]))
                elif k == 6:
                    st(v.tensor_copy(seg_last[:, t, :], key_any[u][:, :, 7]))
                elif k == 7:
                    st.after(st.k - 1)
                    st(v.tensor_copy(node[:, t, 0:SLOTS], key16[u][:]))

            def front(i, first):
                st = Steps(dve, dve_front, FRONT_TICKS, i)
                for u in both:
                    t = 2 * i + u
                    alone(x_in[u], 16 * (i + 1))
                    stats_at = st(v.bn_stats(stats[u][:], x_all[:, t, :]))
                    alone(adj_in[u], 16 * (i + 1))
                    for g in range(SEG):
                        done = search(u, g)
                        if g == SEG - 1:
                            done.then_inc(adj_searched, 1)
                        else:
                            st(done)
                        if g == 0:
                            alone(st.sem, st.base + stats_at)
                            v.bn_aggr(mean_var[u][:], stats[u][:]).then_inc(var_ready, 1)
                        if g == 3:
                            dve.wait_ge(std_ready, t + 1)
                            if not first:
                                dve.wait_ge(h_made, t - 1)
                            stats_at = st(v.reciprocal(ln_scale[u][:], std[u][:]))
                        if g == 4:
                            st.after(stats_at)
                            v.scalar_tensor_tensor(out=ln_shift[u][:], in0=mean_var[u][:, 0:1], scalar=-1.0,
                                                   in1=ln_scale[u][:], op0=ALU.mult, op1=ALU.mult
                                                   ).then_inc(ln_ready, 1)
                        if u == 1:
                            if g == 0:
                                dve.wait_ge(adj_searched, t)
                            neighbours(2 * i, 0, st, g)
                dve.wait_ge(adj_searched, 2 * i + 2)
                for k in range(8):
                    neighbours(2 * i + 1, 1, st, k)
                st.end()

            dve.wait_ge(consts_made, N_CONSTS)
            front(0, True)
            with dve.Fori(1, STEPS) as i:
                front(i, False)
            dve.wait_ge(dve_front, FRONT_TICKS * STEPS)

            st = Steps(dve, dve_mid, MID_TICKS, 0)
            valid = slot_bias[:, :, 0:SLOTS]
            st.link(v.tensor_scalar(valid, node[:, :, 0:SLOTS], 0.0, None, ALU.is_gt))
            st(v.tensor_reduce(count[:], valid, X_AXIS, ALU.add))
            dve.wait_ge(pool_pair, 2 * (PCOL // PG))
            st.link(v.scalar_tensor_tensor(out=pair_ne[:], in0=pair_adj[:], scalar=1.0, in1=pair_ne[:],
                                           op0=ALU.is_equal, op1=ALU.mult))
            st.link(v.scalar_tensor_tensor(out=hit_key[0:PP, :], in0=pair_flat[:], scalar=1.0, in1=pair_ne[:],
                                           op0=ALU.add, op1=ALU.mult))
            st.link(v.max(hit8[:], hit_key[:]))
            st(v.tensor_scalar(hit8_m1[:], hit8[:], -1.0, None, ALU.add))
            st.link(v.tensor_scalar(hit_valid[:], hit8[:], 0.0, None, ALU.is_gt))
            v.tensor_reduce(hit_end[:, 0:1], hit_valid[:], X_AXIS, ALU.add).then_inc(counts_ready, 1)
            st(v.tensor_scalar(valid, valid, 1.0, NEGBIG, ALU.subtract, ALU.mult))
            st(v.tensor_scalar(hit_sub_i[:], hit8_m1[:], 12, None, ALU.logical_shift_right))
            st.link(v.tensor_scalar(hit_obj_i[:], hit8_m1[:], N - 1, None, ALU.bitwise_and))
            st(v.scalar_tensor_tensor(out=hit_node[:, 0:8], in0=hit_sub_i[:], scalar=1.0, in1=hit_valid[:],
                                      op0=ALU.add, op1=ALU.mult))
            st(v.scalar_tensor_tensor(out=hit_node[:, 8:16], in0=hit_obj_i[:], scalar=1.0, in1=hit_valid[:],
                                      op0=ALU.add, op1=ALU.mult))
            st(v.tensor_reduce(flag_f[:, 1:2], seg_last[:].rearrange("p t s -> p (t s)"), X_AXIS, ALU.max))
            st(v.tensor_reduce(flag_f[:, 2:3], node[:, :, SLOTS - 1], X_AXIS, ALU.max))
            dve.wait_ge(diag_in, 16)
            st(v.tensor_reduce(flag_f[:, 3:4], diag[:], X_AXIS, ALU.min))
            dve.wait_ge(offsets_summed, 1)
            st(v.tensor_copy(node[:, :, OFFC], bank[6][:, 0:TILES]))
            st(v.tensor_tensor(end[:], bank[6][:, 0:TILES], count[:], ALU.add))
            st(v.tensor_copy(node[:, :, ROWC], self_key[:, 0:1].to_broadcast([P, TILES])))
            st(v.tensor_copy(hit_node[:, 16:17], bank[6][:, 64:65]))
            st(v.tensor_tensor(hit_end[:, 1:2], bank[6][:, 64:65], hit_end[:, 0:1], ALU.add))
            st(v.tensor_reduce(flag_f[:, 4:5], bank[6][:, TILES:2 * TILES], X_AXIS, ALU.max))
            st(v.tensor_scalar(flag_f[:, 5:6], bank[6][:, 65:66], float(P), None, ALU.is_gt))
            dve.wait_ge(wh_copied, 6 * STEPS)
            st.link(v.tensor_copy(node[:, :, SRCC:VW], src_dst[:, :, 0:HEADS]))
            st.link(v.tensor_scalar(hit_cmp[:], iota[:, 0:P], hit_node[:, 16:17], None, ALU.is_ge))
            v.scalar_tensor_tensor(out=hit_rows[:], in0=iota[:, 0:P], scalar=hit_end[:, 1:2], in1=hit_cmp[:],
                                   op0=ALU.is_lt, op1=ALU.mult).then_inc(hit_rows_ready, 1)
            st.link(v.tensor_tensor(flag_f[:, 1:2], flag_f[:, 1:2], flag_f[:, 2:3], ALU.max))
            st.link(v.tensor_tensor(flag_f[:, 1:2], flag_f[:, 1:2], hit8[:, 7:8], ALU.max))
            st(v.tensor_scalar(flag_f[:, 1:2], flag_f[:, 1:2], 0.0, None, ALU.is_gt))
            st(v.tensor_scalar(flag_f[:, 3:4], flag_f[:, 3:4], 1.0, None, ALU.not_equal))
            st.link(v.tensor_scalar(flag_f[:, 4:5], flag_f[:, 4:5], float(EDGES), None, ALU.is_gt))
            st.link(v.tensor_tensor(flag_f[:, 1:2], flag_f[:, 1:2], flag_f[:, 3:4], ALU.add))
            st.link(v.tensor_tensor(flag_f[:, 1:2], flag_f[:, 1:2], flag_f[:, 4:5], ALU.add))
            v.tensor_tensor(flag_f[:, 0:1], flag_f[:, 1:2], flag_f[:, 5:6], ALU.add).then_inc(flags_ready, 1)
            dve.wait_ge(hit_summed, 1)
            st(v.tensor_copy(hit_e[:], bank[7][:, 0:17]))
            st.link(v.tensor_tensor(hit_slot[:], edge_pos[:, 0, 0:1], bank[7][:, 16:17], ALU.subtract))
            st.link(v.tensor_scalar(hit_sel[:], iota[:, 0:8], hit_slot[:, 0:1], None, ALU.is_equal))
            for part, node1, idx, f in ((0, hit_sub1, hit_sub, 0), (8, hit_obj1, hit_obj, 2)):
                st.link(v.tensor_tensor(hit_tmp[:], hit_e[:, part:part + 8], hit_sel[:], ALU.mult))
                st.link(v.tensor_reduce(node1[:], hit_tmp[:], X_AXIS, ALU.add))
                st.link(v.tensor_scalar(hit_f[:, f:f + 1], node1[:], 0.0, FAR, ALU.is_equal, ALU.mult))
                st.link(v.scalar_tensor_tensor(out=hit_f[:, f + 1:f + 2], in0=node1[:], scalar=-1.0,
                                               in1=hit_f[:, f:f + 1], op0=ALU.add, op1=ALU.add))
                st.link(v.tensor_copy(idx[:], hit_f[:, f + 1:f + 2]))
            dve.wait_ge(flags_summed, 1)
            st.link(v.tensor_scalar(flag_f[:, 6:7], bank[3][:, 0:1], 1.0, None, ALU.min))
            st.link(v.tensor_copy(flag_i[:], flag_f[:, 6:7]))
            v.tensor_copy(flag_f[:, 7:8], flag_f[:, 6:7]).then_inc(node_ready, 1)
            st.end()

            flag = read_flag(dve)
            with dve.If(flag > 0):
                for u in both:
                    dve.wait_ge(wh_stored[u], 16 * STEPS)
                dense0_vector(dve)

            def row_onehots(st, j, q, ready):
                for u in both:
                    t = 2 * j + u
                    st.link(v.tensor_scalar(row_cmp[:, u, :], iota[:], step_node(j)[:, u, OFFC:OFFC + 1], None, ALU.is_ge))
                    v.scalar_tensor_tensor(out=row_hot[q][:, u, :], in0=iota[:], scalar=end[:, bass.ds(t, 1)],
                                           in1=row_cmp[:, u, :], op0=ALU.is_lt, op1=ALU.mult).then_inc(ready, 1)

            def rows(j, q):
                st = Steps(dve, dve_rows, ROWS_TICKS, j)
                if not isinstance(j, int) or j >= 2:
                    dve.wait_ge(agg_summed, 2 * j - 2)
                row_onehots(st, j, q, rows_ready)
                dve.wait_ge(info_ready, j + 1)
                info = edge_info[q]
                st(v.tensor_copy(row_id[:, j, :], info[:, :, ROWC]))
                st.link(v.tensor_tensor(slot_id[:, j, :], edge_pos[:].rearrange("p u c -> p (u c)"), info[:, :, OFFC],
                                        ALU.subtract))
                st.link(v.tensor_tensor(slot_hot[q][:], iota16.unsqueeze(1).to_broadcast([P, EC, SLOTS]),
                                        slot_id[:, j, :].unsqueeze(2).to_broadcast([P, EC, SLOTS]), ALU.is_equal))
                st(v.tensor_tensor(nbr_tmp[:], slot_hot[q][:], info[:, :, 0:SLOTS], ALU.mult))
                at = st.k
                v.tensor_tensor(edge_hot[q][:], iota_row1.unsqueeze(1).to_broadcast([P, EC, P]),
                                row_id[:, j, :].unsqueeze(2).to_broadcast([P, EC, P]), ALU.is_equal
                                ).then_inc(hot_ready, 1)
                st.after(at)
                st.link(v.tensor_reduce(nbr_key[:, 0, :], nbr_tmp[:], X_AXIS, ALU.add))
                st.link(v.tensor_scalar(nbr_key[:, 1, :], nbr_key[:, 0, :], 0.0, FAR, ALU.is_equal, ALU.mult))
                st.link(v.scalar_tensor_tensor(out=nbr_key[:, 2, :], in0=nbr_key[:, 0, :], scalar=-1.0,
                                               in1=nbr_key[:, 1, :], op0=ALU.add, op1=ALU.add))
                v.tensor_copy(edge_idx[q][:], nbr_key[:, 2, :]).then_inc(idx_ready, 1)
                st(v.tensor_copy(idx_all[:, j, :], nbr_key[:, 2, :]))
                st.end()

            def edges(jj, q):
                j = 2 * jj + q
                st = Steps(dve, dve_edge, EDGE_TICKS, j)
                info, rows_in = edge_info[q], gath[q]
                dst = rows_in[:, 0:EC, D:ROW]
                own = step_src_dst[:, j]
                dve.wait_ge(gath_in[q], 16 * EC * (jj + 1))
                dve.wait_ge(self_in[q], 16 * (jj + 1))
                v.tensor_tensor(placed, slot_hot[q][:].unsqueeze(3).to_broadcast([P, EC, SLOTS, HEADS]),
                                dst.unsqueeze(2).to_broadcast([P, EC, SLOTS, HEADS]), ALU.mult
                                ).then_inc(placed_ready, 1)
                st(v.tensor_tensor(edge_e[:, 0, 0:EC, :], dst, info[:, :, SRCC:VW], ALU.add))
                st.link(v.tensor_tensor(edge_e[:, 0, EC:GC, :], own[:, :, 0:HEADS], own[:, :, HEADS:], ALU.add))
                st(v.scalar_tensor_tensor(out=edge_e[:, 1], in0=edge_e[:, 0], scalar=ALPHA, in1=edge_e[:, 0],
                                          op0=ALU.mult, op1=ALU.max))
                dve.wait_ge(slots_summed, j + 1)
                st.link(v.tensor_tensor(masked, bank[1][:, 0:PAIR * P].rearrange("p (u k h) -> p u k h", u=PAIR, k=SLOTS),
                                        step_bias[:, j, :, 0:SLOTS].unsqueeze(3).to_broadcast([P, PAIR, SLOTS, HEADS]),
                                        ALU.add))
                st.link(v.tensor_reduce(max_tmp[:, 0], masked.rearrange("p u k h -> p u h k"), X_AXIS, ALU.max))
                st.link(v.tensor_tensor(max_tmp[:, 1], max_tmp[:, 0], own[:, :, HEADS:], ALU.max))
                st.link(v.tensor_tensor(max_tmp[:, 2], max_tmp[:, 1], own[:, :, 0:HEADS], ALU.add))
                v.scalar_tensor_tensor(out=row_max[q][:], in0=max_tmp[:, 2], scalar=ALPHA, in1=max_tmp[:, 2],
                                       op0=ALU.mult, op1=ALU.max).then_inc(row_max_ready, 1)
                dve.wait_ge(row_max_ready, j + 1)
                if not isinstance(j, int) or j >= 1:
                    dve.wait_ge(prob_ready, j)
                st(v.tensor_tensor(edge_e[:, 0, EC:GC, :], edge_e[:, 1, EC:GC, :], row_max[q][:], ALU.subtract))
                dve.wait_ge(edge_max_summed, j + 1)
                st.link(v.tensor_tensor(edge_e[:, 0, 0:EC, :], edge_e[:, 1, 0:EC, :],
                                        bank[0][:, EC * VW:EC * (VW + HEADS)].rearrange("p (c h) -> p c h", c=EC),
                                        ALU.subtract))
                v.tensor_scalar(edge_e[:, 2], edge_e[:, 0], 0.0, None, ALU.min).then_inc(exponent_ready, 1)
                dve.wait_ge(prob_ready, j + 1)
                for c0, c1 in ((0, 2), (2, CH), (EC, GC), (CH, CH + 2), (CH + 2, EC)):
                    part = rows_in[:, c0:c1, 0:D].rearrange("p c (h d) -> p c h d", h=HEADS)
                    v.tensor_tensor(part, part, prob[q][:, c0:c1, :].unsqueeze(3).to_broadcast([P, c1 - c0, HEADS, DH]),
                                    ALU.mult).then_inc(scaled, 1)
                dve.wait_ge(agg_summed, 2 * j + 1)
                st.link(v.reciprocal(inv_sum[:].rearrange("p u h -> p (u h)"), bank[1][:, 2 * P:2 * P + 2 * HEADS]))
                for u in both:
                    dve.wait_ge(agg_summed, 2 * j + u + 1)
                    v.tensor_tensor(att[:, u, :].rearrange("p (h d) -> p h d", h=HEADS),
                                    bank[2 + u][:].rearrange("p (h d) -> p h d", h=HEADS),
                                    inv_sum[:, u, :].unsqueeze(2).to_broadcast([P, HEADS, DH]), ALU.mult
                                    ).then_inc(att_ready, 1)
                st.end()

            def tail(j, q):
                st = Steps(dve, dve_tail, TAIL_TICKS, j)
                dve.wait_ge(elu_parts, 2 * j + 2)
                v.scalar_tensor_tensor(out=att_exp, in0=att_exp, scalar=1.0, in1=att_relu,
                                       op0=ALU.min, op1=ALU.add).then_inc(enc_ready, 1)
                for u in both:
                    t = 2 * j + u
                    dve.wait_ge(mlp_summed, 5 * j + 4 + u)
                    if u == 0:
                        dve.wait_ge(b4_added, TILES)
                    st(v.tensor_tensor(x_all[:, t, :], bank[4 + u][:], x_all[:, t, :], ALU.add))
                    alone(st.sem, st.base + st.k)
                    st(v.bn_stats(stats[u][:], x_all[:, t, :]))
                    alone(st.sem, st.base + st.k)
                    v.bn_aggr(mean_var[u][:], stats[u][:]).then_inc(var2_ready, 1)
                for u in both:
                    t = 2 * j + u
                    if not isinstance(j, int) or j >= 1:
                        dve.wait_ge(h2_made, t - 1)
                    dve.wait_ge(std2_ready, t + 1)
                    st.link(v.reciprocal(ln_scale[u][:], std[u][:]))
                    v.scalar_tensor_tensor(out=ln_shift[u][:], in0=mean_var[u][:, 0:1], scalar=-1.0,
                                           in1=ln_scale[u][:], op0=ALU.mult, op1=ALU.mult).then_inc(ln2_ready, 1)
                st.end()

            rows(0, 0)

            def step(jj, q, last=False):
                j = 2 * jj + q
                if not last:
                    rows(j + 1, 1 - q)
                edges(jj, q)
                tail(j, q)

            step(0, 0)
            step(0, 1)
            with dve.Fori(1, STEPS // 2 - 1) as jj:
                for q in both:
                    step(jj, q)
            step(STEPS // 2 - 1, 0)
            step(STEPS // 2 - 1, 1, last=True)

            def rows1(jj, q, first, st):
                j = 2 * jj + q
                if not first:
                    dve.wait_ge(agg1_summed, 2 * j - 2)
                st.link(v.tensor_copy(edge_idx[q][:], idx_all[:, j, :]))
                v.tensor_tensor(slot_hot[q][:], iota16.unsqueeze(1).to_broadcast([P, EC, SLOTS]),
                                slot_id[:, j, :].unsqueeze(2).to_broadcast([P, EC, SLOTS]), ALU.is_equal
                                ).then_inc(idx1_ready, 1)
                row_onehots(st, j, q, rows1_ready)

            st = Steps(dve, dve_rows1, ROWS1_TICKS, 0)
            rows1(0, 0, True, st)
            st.end()
            st = Steps(dve, dve_rows1, ROWS1_TICKS, 1)
            rows1(0, 1, True, st)
            st.end()
            st = Steps(dve, dve_hit, HIT_TICKS, 0)
            dve.wait_ge(hit_in, 48)
            st.link(v.scalar_tensor_tensor(out=hit_keys[:], in0=hit_keys[:], scalar=hit_obj1[:, 0:1], in1=iota16,
                                           op0=ALU.is_equal, op1=ALU.mult))
            st.link(v.tensor_reduce(hit_slot[:], hit_keys[:], X_AXIS, ALU.add))
            st.link(v.scalar_tensor_tensor(out=hit_f[:, 0:1], in0=hit_f[:, 1:2], scalar=float(SLOTS), in1=hit_slot[:],
                                           op0=ALU.mult, op1=ALU.add))
            st(v.tensor_copy(hit_dst[:], hit_f[:, 0:1]))
            dve.wait_ge(hit_proj, 1)
            st(v.tensor_tensor(hit_q, bank[6][:], bq_row[:], ALU.add))
            dve.wait_ge(hit_proj, 2)
            st.link(v.tensor_tensor(hit_k, bank[7][:], bk_row[:], ALU.add))
            st.link(v.tensor_tensor(hit_q, hit_q, hit_k, ALU.mult))
            st.link(v.tensor_reduce(hit_tmp[:], hit_q.rearrange("p (h d) -> p h d", h=HEADS), X_AXIS, ALU.add))
            v.tensor_scalar(hit_att[:], hit_tmp[:], DH ** -0.5, None, ALU.mult).then_inc(hit_att_ready, 1)
            st.end()

            def softmax(jj, q, first):
                j = 2 * jj + q
                st = Steps(dve, dve_soft, SOFT_TICKS, j)
                dve.wait_ge(score_in_sem[q], 16 * (jj + 1))
                st(v.tensor_tensor(soft[:, :, 0:SLOTS, :], score_in[q].rearrange("p u (k h) -> p u k h", k=SLOTS),
                                   step_bias[:, j, :, 0:SLOTS].unsqueeze(3).to_broadcast([P, PAIR, SLOTS, HEADS]),
                                   ALU.add))
                st.link(v.memset(soft[:, :, SLOTS, :], SELF_SCORE))
                by_slot = soft.rearrange("p u k h -> p u h k")
                over_slots = [P, PAIR, SLOTS + 1, HEADS]
                st.link(v.tensor_reduce(soft_max, by_slot, X_AXIS, ALU.max))
                v.tensor_tensor(soft, soft, soft_max.unsqueeze(2).to_broadcast(over_slots), ALU.subtract
                                ).then_inc(soft_ready, 1)
                dve.wait_ge(soft_exp, j + 1)
                st.link(v.tensor_reduce(soft_sum, by_slot, X_AXIS, ALU.add))
                st.link(v.reciprocal(soft_sum, soft_sum))
                st.link(v.tensor_tensor(soft, soft, soft_sum.unsqueeze(2).to_broadcast(over_slots), ALU.mult))
                if not first:
                    dve.wait_ge(agg1_summed, 2 * j - 2)
                st.link(v.tensor_reduce(weight[q][:], soft, X_AXIS, ALU.add))
                v.tensor_scalar(weight[q][:], weight[q][:], 1.0 / HEADS, None, ALU.mult).then_inc(weight_ready, 1)
                st.end()

            def late(jj, q, first, last):
                j = 2 * jj + q
                st = Steps(dve, dve_edge1, EDGE1_TICKS, j)
                dve.wait_ge(edge_w_summed, j + 1)
                st.link(v.tensor_tensor(nbr_tmp[:], slot_hot[q][:],
                                        bank[0][:, 0:EC * SLOTS].rearrange("p (c k) -> p c k", c=EC), ALU.mult))
                st.link(v.tensor_reduce(edge_w[:], nbr_tmp[:], X_AXIS, ALU.add))
                if not (first and q == 0):
                    dve.wait_ge(agg1_summed, 2 * j)
                for n in range(EC):
                    st(v.tensor_scalar(edge_hot[q][:, n, :], iota_row1, row_id[:, j, n:n + 1], edge_w[:, n:n + 1],
                                       ALU.is_equal, ALU.mult))
                st(v.tensor_scalar(self_hot[0][:], ident[:], weight[q][:, 0, SLOTS:SLOTS + 1], None, ALU.mult))
                v.tensor_scalar(self_hot[1][:], ident[:], weight[q][:, 1, SLOTS:SLOTS + 1], None, ALU.mult
                                ).then_inc(hot1_ready, 1)
                if not last:
                    softmax_next(jj, q, first)
                for u in both:
                    dve.wait_ge(agg1_summed, 2 * j + u + 1)
                    if not (first and q == 0):
                        dve.wait_ge(out_stored[u], 16 * j)
                    v.tensor_tensor(out_sb[u], bank[2 + 2 * q + u][:], x_all[:, 2 * j + u, :], ALU.add
                                    ).then_inc(out_ready, 1)
                st.end()

            def softmax_next(jj, q, first):
                if q == 0:
                    softmax(jj, 1, first)
                else:
                    softmax(jj + 1, 0, False)

            def rows1_next(jj, q):
                st = Steps(dve, dve_rows1, ROWS1_TICKS, 2 * jj + q + 2)
                rows1(jj + 1, q, False, st)
                st.end()

            softmax(0, 0, True)
            for q in both:
                late(0, q, True, False)
                rows1_next(0, q)
            with dve.Fori(1, STEPS // 2 - 1) as jj:
                for q in both:
                    late(jj, q, False, False)
                    rows1_next(jj, q)
            late(STEPS // 2 - 1, 0, False, False)
            late(STEPS // 2 - 1, 1, False, True)
            for u in both:
                dve.wait_ge(out_stored[u], 16 * STEPS)
            with dve.If(flag > 0):
                dense1_vector(dve)


def kernel(**inputs):
    import numpy as _np
    import concourse.bacc as _bacc
    from concourse import mybir as _mybir
    from concourse.bass_utils import run_bass_kernel_spmd as _run

    def host(name):
        return _np.asarray(inputs[name])

    laid_out = {
        "x": host("x"),
        "adj": host("adj"),
        "w0": host("L0_gnn_W").transpose(1, 0, 2).reshape(D, D),
        "a1": host("L0_gnn_a1").reshape(D),
        "a2": host("L0_gnn_a2").reshape(D),
        "w1t": host("L0_gnn_W1").T,
        "b1": host("L0_gnn_b1").reshape(-1, P).T,
        "w2t": host("L0_gnn_W2").T,
        "b2": host("L0_gnn_b2").reshape(-1, P).T,
        "w3t": host("L0_gnn_W3").T,
        "b3": host("L0_gnn_b3").reshape(-1, P).T,
        "w4t": host("L0_gnn_W4").T,
        "b4": host("L0_gnn_b4"),
        "pairs": host("L1_gnn_rel_pair_index"),
        "wqt": host("L1_gnn_Wq").T,
        "bq": host("L1_gnn_bq"),
        "wkt": host("L1_gnn_Wk").T,
        "bk": host("L1_gnn_bk"),
    }
    nc = _bacc.Bacc("TRN2", target_bir_lowering=False, num_devices=1)
    arrays, args = {}, []
    for name, a in laid_out.items():
        a = _np.ascontiguousarray(a)
        arrays[f"in_{name}_dram"] = a
        args.append(nc.dram_tensor(f"in_{name}_dram", a.shape, _mybir.dt.from_np(a.dtype), kind="ExternalInput").ap())
    out = nc.dram_tensor("out_dram", (N, D), F32, kind="ExternalOutput").ap()
    gnn_kernel(nc, *args, out)
    r = _run(nc, [arrays], core_ids=[0])
    return r.results[0]["out_dram"]
```

```python
from contextlib import ExitStack

import concourse.bass as bass
from concourse import mybir
from concourse.alu_op_type import AluOpType as ALU

ACT = mybir.ActivationFunctionType
F32 = mybir.dt.float32
I32 = mybir.dt.int32
U32 = mybir.dt.uint32
X_AXIS = mybir.AxisListType.X

P = 128
N = 4096
D = 512
TILES = N // P
HEADS = 8
DH = D // HEADS
KC = D // P
SEG = 8
SEGW = N // SEG
SEGP = SEGW + 8
SLOTS = 16
CH = 5
EDGES = CH * P
BUFS = 4
PAIR = 2
STEPS = TILES // PAIR
EC = PAIR * CH
GC = EC + PAIR
ROW = D + HEADS
NPAIR = 10000
PP = 125
PCOL = NPAIR // PP
PG = 8
VW = 26
OFFC, ROWC, SRCC = SLOTS, SLOTS + 1, SLOTS + 2
FAR = 5000.0
NEGBIG = 1.0e30
ALPHA = 0.2
EPS = 1e-5
START_TICKS, FRONT_TICKS, NBR_TICKS, MID_TICKS, ROWS_TICKS, IDX_TICKS, EDGE_TICKS = 26, 9, 8, 46, 2, 8, 9
ATT_TICKS, NORM_TICKS, ROWS1_TICKS, HIT_TICKS, SOFT_TICKS, EDGE1_TICKS = 1, 4, 3, 10, 8, 11
ARENA = 22720
SELF_SCORE = 1e-7


class Steps:

    def __init__(self, eng, sem, per, run):
        self.eng, self.sem, self.base, self.per, self.k = eng, sem, run * per, per, 0

    def __call__(self, instruction):
        instruction.then_inc(self.sem, 1)
        self.k += 1
        return self.k

    def after(self, k):
        self.eng.wait_ge(self.sem, self.base + k)

    def link(self, instruction):
        self.after(self(instruction))

    def end(self):
        assert self.k == self.per, (self.k, self.per)


def later(j, n):
    return not isinstance(j, int) or j >= n


def lone_wait(eng, met, sem, value):
    if not isinstance(value, int):
        eng.compute_val(value)
    eng.wait_ge(met, 1)
    eng.wait_ge(sem, value)


def gnn_kernel(nc, x, adj, w0, a1, a2, w1t, b1, w2t, b2, w3t, b3, w4t, b4, pairs, wqt, bq, wkt, bk, out):
    table0 = nc.dram_tensor("table0", [N, ROW], F32, kind="Internal").ap()
    table1 = nc.dram_tensor("table1", [N, D], F32, kind="Internal").ap()
    keys_dram = nc.dram_tensor("keys_dram", [N, SLOTS], F32, kind="Internal").ap()
    score_dram = nc.dram_tensor("score_dram", [N * SLOTS, HEADS], F32, kind="Internal").ap()

    adj_flat = adj.rearrange("n m -> (n m)").unsqueeze(1)
    adj_rows = adj.rearrange("n (s c) -> n s c", s=SEG)
    score_rows = score_dram.rearrange("(n k) h -> n (k h)", k=SLOTS)

    with ExitStack() as ctx:
        def sb(name, shape, dt=F32):
            return ctx.enter_context(nc.sbuf_tensor(name, shape, dt))

        def sem(name):
            return ctx.enter_context(nc.semaphore(name))

        iota = sb("iota", [P, EDGES])
        ident = sb("ident", [P, P])
        before = sb("before", [P, P])
        ones = sb("ones", [P, P])
        zeros = sb("zeros", [P, D])
        seg_base = sb("seg_base", [P, SEG, 8])
        self_key = sb("self_key", [P, TILES])
        edge_pos = sb("edge_pos", [P, PAIR, CH])
        iota16 = iota[:, 0:SLOTS]
        iota_row1 = iota[:, 1:P + 1]

        a_fold = sb("a_fold", [P, KC, 2 * HEADS])
        w1_sb = sb("w1_sb", [P, 4, 256])
        w2_sb = sb("w2_sb", [P, 2, 128])
        w3_sb = sb("w3_sb", [P, 256])
        w4_sb = sb("w4_sb", [P, 2, D])
        b1_sb = sb("b1_sb", [P, 2])
        b2_sb = sb("b2_sb", [P, 1])
        b3_sb = sb("b3_sb", [P, 2])
        b4_row = sb("b4_row", [P, D])

        x_all = sb("x_all", [P, TILES, D])
        node = sb("node", [P, TILES, VW])
        src_dst = sb("src_dst", [P, TILES, 2 * HEADS])
        seg_last = sb("seg_last", [P, TILES, SEG])
        end = sb("end", [P, TILES])
        tile_edges = sb("tile_edges", [P, TILES])
        count = sb("count", [P, TILES])
        slot_bias = sb("slot_bias", [P, TILES, SLOTS + 1])
        row_id = sb("row_id", [P, STEPS, EC])
        slot_id = sb("slot_id", [P, STEPS, EC])
        idx_all = sb("idx_all", [P, STEPS, EC], U32)

        arena = sb("arena", [P, ARENA])

        def carver():
            at = [0]

            def carve(shape, dt=F32):
                size = 1
                for n in shape:
                    size *= n
                view = arena[:, at[0]:at[0] + size]
                at[0] += size
                assert at[0] <= ARENA, at[0]
                names = "abc"[:len(shape)]
                if dt is not F32:
                    view = view.bitcast(dt)
                if len(shape) == 1:
                    return view
                return view.rearrange(f"p ({' '.join(names)}) -> p {' '.join(names)}", **dict(zip(names, shape)))

            return carve

        both = range(2)
        bufs = range(BUFS)
        front = carver()
        adj_sb = [front([SEG, SEGP]) for b in bufs]
        ones8 = sb("ones8", [P, 8])
        found = [sb(f"found{u}", [P, SEG, 8], U32) for u in both]
        key_raw = [sb(f"key_raw{u}", [P, SEG, 8]) for u in both]
        key_any = [sb(f"key_any{u}", [P, SEG, 8]) for u in both]
        key_nbr = [sb(f"key_nbr{u}", [P, SEG * 8]) for u in both]
        key_left = [sb(f"key_left{u}", [P, SEG * 8]) for u in both]
        key16 = [sb(f"key16{u}", [P, SLOTS]) for u in both]
        stats = [sb(f"stats{u}", [P, 6]) for u in both]
        mean_var = [sb(f"mean_var{u}", [P, 2]) for u in both]
        ln_scale = [sb(f"ln_scale{u}", [P, 1]) for u in both]
        ln_shift = [sb(f"ln_shift{u}", [P, 1]) for u in both]
        w0_sb = front([KC, D])
        h_sb = [front([D]) for u in both]
        hT = [front([KC, P]) for u in both]
        wh_row = [front([ROW]) for u in both]
        folding = carver()
        folding([BUFS * SEG * SEGP + KC * D])
        a_rows = folding([2, D])
        fold_tmp = folding([D])

        pair_sb = sb("pair_sb", [PP, PCOL, 2], I32)
        pair_flat = sb("pair_flat", [PP, PCOL])
        pair_ne = sb("pair_ne", [PP, PCOL])
        pair_idx = sb("pair_idx", [PP, PCOL], U32)
        idx8 = sb("idx8", [PP, PG], U32)
        adj8 = sb("adj8", [PP, PG])
        pair_adj = sb("pair_adj", [PP, PCOL])
        hit_key = sb("hit_key", [P, PCOL])
        hit8 = sb("hit8", [P, 8])
        hit_valid = sb("hit_valid", [P, 8])
        hit8_m1 = sb("hit8_m1", [P, 8], I32)
        hit_sub_i = sb("hit_sub_i", [P, 8], I32)
        hit_obj_i = sb("hit_obj_i", [P, 8], I32)
        hit_node = sb("hit_node", [P, 17])
        hit_end = sb("hit_end", [P, 2])
        hit_rows = sb("hit_rows", [P, P])
        hit_cmp = sb("hit_cmp", [P, P])
        hit_e = sb("hit_e", [P, 17])
        hit_slot = sb("hit_slot", [P, 1])
        hit_sel = sb("hit_sel", [P, 8])
        hit_tmp = sb("hit_tmp", [P, 8])
        hit_sub1 = sb("hit_sub1", [P, 1])
        hit_obj1 = sb("hit_obj1", [P, 1])
        hit_f = sb("hit_f", [P, 4])
        hit_sub = sb("hit_sub", [P, 1], U32)
        hit_obj = sb("hit_obj", [P, 1], U32)
        hit_dst = sb("hit_dst", [P, 1], U32)
        hit_keys = sb("hit_keys", [P, SLOTS])
        hit_att = sb("hit_att", [P, HEADS])
        flag_f = sb("flag_f", [P, 8])
        flag_i = sb("flag_i", [P, 1], I32)
        diag = sb("diag", [P, TILES])

        edge = carver()
        gath = [edge([GC, ROW]) for q in both]
        row_hot = [edge([PAIR, EDGES]) for q in both]
        row_cmp = edge([EDGES])
        edge_info = [sb(f"edge_info{q}", [P, EC, VW]) for q in both]
        slot_hot = [sb(f"slot_hot{q}", [P, EC, SLOTS]) for q in both]
        nbr_tmp = sb("nbr_tmp", [P, EC, SLOTS])
        nbr_key = sb("nbr_key", [P, 3, EC])
        edge_idx = [sb(f"edge_idx{q}", [P, EC], U32) for q in both]
        edge_hot = [sb(f"edge_hot{q}", [P, EC, P]) for q in both]
        placed = edge([EC, SLOTS, HEADS])
        masked = edge([PAIR, SLOTS, HEADS])
        row_max = [sb(f"row_max{q}", [P, PAIR, HEADS]) for q in both]
        max_tmp = sb("max_tmp", [P, 3, PAIR, HEADS])
        edge_e = sb("edge_e", [P, 3, GC, HEADS])
        prob = [sb(f"prob{q}", [P, GC, HEADS]) for q in both]
        inv_sum = sb("inv_sum", [P, PAIR, HEADS])
        att = edge([PAIR, D])
        att_exp = edge([PAIR, D])
        h2_sb = edge([PAIR, D])
        encT = edge([KC, PAIR * P])
        z1 = edge([2, PAIR * P])
        z2 = edge([PAIR * P])
        z3 = z1

        late = carver()
        late([2 * GC * ROW + 2 * PAIR * EDGES + EDGES])
        wq_sb = late([KC, D])
        wk_sb = late([KC, D])
        hit_h = [late([D]) for s in both]
        hit_hT = late([KC, P])
        hit_q = late([D])
        hit_k = hit_h[0]
        bq_row, bk_row = b4_row, zeros
        w1_flat = w1_sb[:].rearrange("p a b -> p (a b)")
        score_in = [w1_flat[:, 256 * q:256 * (q + 1)].rearrange("p (u c) -> p u c", u=PAIR) for q in both]
        soft = w1_flat[:, 512:784].rearrange("p (u k h) -> p u k h", u=PAIR, h=HEADS)
        soft_max = max_tmp[:, 0]
        soft_sum = max_tmp[:, 1]
        weight = [sb(f"weight{q}", [P, PAIR, SLOTS + 1]) for q in both]
        edge_w = sb("edge_w", [P, EC])
        out_sb = [att, att_exp]
        ln2_scale = sb("ln2_scale", [P, STEPS, PAIR])
        ln2_shift = sb("ln2_shift", [P, STEPS, PAIR])
        own_scale = sb("own_scale", [P, 2, PAIR])
        own_shift = sb("own_shift", [P, 2, PAIR])
        bank = [ctx.enter_context(nc.psum_tensor(f"bank{i}", [P, 512], F32)) for i in range(8)]

        consts_made = sem("consts_made")
        weights0_in = sem("weights0_in")
        weights1_in = sem("weights1_in")
        weights2_in = sem("weights2_in")
        adj_in = [sem(f"adj_in{b}") for b in bufs]
        x_in = [sem(f"x_in{b}") for b in bufs]
        adj_searched = sem("adj_searched")
        dve_start = sem("dve_start")
        dve_front = sem("dve_front")
        dve_nbr = sem("dve_nbr")
        fold_ready = sem("fold_ready")
        ln_ready = sem("ln_ready")
        h_made = sem("h_made")
        h_turned = sem("h_turned")
        hT_ready = sem("hT_ready")
        wh_summed = sem("wh_summed")
        wh_copied = sem("wh_copied")
        wh_stored = [sem(f"wh_stored{u}") for u in both]
        b4_added = sem("b4_added")
        pair_in = sem("pair_in")
        pairs_ready = sem("pairs_ready")
        pool_pair = sem("pool_pair")
        pair_adj_in = sem("pair_adj_in")
        diag_in = sem("diag_in")
        dve_mid = sem("dve_mid")
        counts_ready = sem("counts_ready")
        offsets_summed = sem("offsets_summed")
        node_ready = sem("node_ready")
        flags_ready = sem("flags_ready")
        flags_summed = sem("flags_summed")
        hit_rows_ready = sem("hit_rows_ready")
        hit_summed = sem("hit_summed")
        keys_stored = sem("keys_stored")
        score_zeroed = sem("score_zeroed")
        dve_rows = sem("dve_rows")
        rows_ready = sem("rows_ready")
        info_summed = sem("info_summed")
        info_ready = sem("info_ready")
        idx_ready = sem("idx_ready")
        hot_ready = sem("hot_ready")
        gath_in = [sem(f"gath_in{q}") for q in both]
        self_in = [sem(f"self_in{q}") for q in both]
        dve_edge = sem("dve_edge")
        placed_ready = sem("placed_ready")
        slots_summed = sem("slots_summed")
        row_max_ready = sem("row_max_ready")
        edge_max_summed = sem("edge_max_summed")
        exponent_ready = sem("exponent_ready")
        prob_ready = sem("prob_ready")
        scaled = sem("scaled")
        agg_summed = sem("agg_summed")
        att_ready = sem("att_ready")
        dve_idx = sem("dve_idx")
        dve_att = sem("dve_att")
        x_added = sem("x_added")
        own_ready = sem("own_ready")
        own_made = sem("own_made")
        out_added = sem("out_added")
        dve_norm = sem("dve_norm")
        elu_parts = sem("elu_parts")
        enc_ready = sem("enc_ready")
        enc_turned = sem("enc_turned")
        encT_ready = sem("encT_ready")
        mlp_summed = sem("mlp_summed")
        mlp_relu = sem("mlp_relu")
        ln2_ready = sem("ln2_ready")
        h2_made = sem("h2_made")
        h2_stored = [sem(f"h2_stored{u}") for u in both]
        hit_in = sem("hit_in")
        hit_turned = sem("hit_turned")
        hit_hT_ready = sem("hit_hT_ready")
        hit_proj = sem("hit_proj")
        dve_hit = sem("dve_hit")
        hit_att_ready = sem("hit_att_ready")
        hit_stored = sem("hit_stored")
        late_in = sem("late_in")
        dve_rows1 = sem("dve_rows1")
        rows1_ready = sem("rows1_ready")
        idx1_ready = sem("idx1_ready")
        gath1_in = [sem(f"gath1_in{q}") for q in both]
        score_in_sem = [sem(f"score_in{q}") for q in both]
        dve_soft = sem("dve_soft")
        soft_ready = sem("soft_ready")
        soft_exp = sem("soft_exp")
        weight_ready = sem("weight_ready")
        edge_w_summed = sem("edge_w_summed")
        dve_edge1 = sem("dve_edge1")
        hot1_ready = sem("hot1_ready")
        agg1_summed = sem("agg1_summed")
        out_ready = sem("out_ready")
        out_stored = [sem(f"out_stored{n}") for n in range(4)]

        neg_one = sb("neg_one", [P, 1])
        eps_col = sb("eps_col", [P, 1])
        std = [sb(f"std{u}", [P, 1]) for u in both]
        var_ready = sem("var_ready")
        std_ready = sem("std_ready")
        var2_ready = sem("var2_ready")
        std2_ready = sem("std2_ready")
        N_CONSTS = 10
        x_rows = x.rearrange("(t p) d -> t p d", p=P)
        out_rows = out.rearrange("(t p) d -> t p d", p=P)
        adj_tiles = adj_rows.rearrange("(t p) s c -> t p s c", p=P)
        table0_rows = table0.rearrange("(t p) d -> t p d", p=P)
        table0_steps = table0.rearrange("(j u p) d -> j p u d", u=PAIR, p=P)
        table1_rows = table1.rearrange("(t p) d -> t p d", p=P)
        table1_steps = table1.rearrange("(j u p) d -> j p u d", u=PAIR, p=P)
        score_steps = score_rows.rearrange("(j u p) c -> j p u c", u=PAIR, p=P)
        step_bias = slot_bias[:].rearrange("p (j u) k -> p j u k", u=PAIR)
        step_src_dst = src_dst[:].rearrange("p (j u) c -> p j u c", u=PAIR)

        def step_node(j):
            return node[:].rearrange("p (j u) v -> p j u v", u=PAIR)[:, j]

        def front_slots(eng, slot):
            for b in bufs:
                slot(0, b)
            with eng.Fori(1, TILES // BUFS) as i:
                for b in bufs:
                    slot(i, b)

        def edge_pipeline(eng, body):
            for j in range(2):
                body(j // 2, j % 2)
            with eng.Fori(1, STEPS // 2 - 1) as jj:
                for q in both:
                    body(jj, q)
            for j in range(STEPS - 2, STEPS + 2):
                body(j // 2, j % 2)

        def has(j, low, high):
            return not isinstance(j, int) or low <= j <= high


        wide = carver()
        d_whole = [wide([N]) for _ in range(4)]
        d_score, d_adj, d_turned, d_dst = d_whole
        d_head = wide([TILES, DH])
        d_diag = wide([KC, P])
        d_out = wide([D])
        d_agg = d_dst
        d_pair_att = wide([PCOL, HEADS])
        d_pair_att_flat = d_pair_att.rearrange("p c h -> p (c h)")
        d_h2 = arena[:, 2 * N:4 * N].rearrange("p (j d) -> p j d", d=D)
        half = TILES // 2
        d_weight = [arena[:, 0:KC * D].rearrange("p (k n) -> p k n", k=KC),
                    arena[:, KC * D:2 * KC * D].rearrange("p (k n) -> p k n", k=KC)]
        d_pair_h = [arena[0:PP, N + n * D:N + (n + 1) * D] for n in both]
        d_pair_hT = [arena[:, N + (2 + n) * D:N + (3 + n) * D].rearrange("p (k n) -> p k n", k=KC) for n in both]
        d_pair_q = [arena[0:PP, N + (4 + n) * D:N + (5 + n) * D] for n in both]
        d_bias = [arena[:, N + (6 + n) * D:N + (7 + n) * D] for n in both]
        d_max = sb("d_max", [P, 2])
        d_sum = sb("d_sum", [P, 2])
        d_idx = sb("d_idx", [PP, 2], U32)
        d_val = sb("d_val", [PP, 1])
        off_diag, on_diag = edge_hot[0][:, 0, :], edge_hot[0][:, 1, :]
        att_dram = nc.dram_tensor("att_dram", [N, D], F32, kind="Internal").ap()
        full_dram = nc.dram_tensor("full_dram", [N, N], F32, kind="Internal").ap()
        agg_dram = nc.dram_tensor("agg_dram", [N, N], F32, kind="Internal").ap()
        full_flat = full_dram.rearrange("n m -> (n m)").unsqueeze(1)
        full_rows = full_dram.rearrange("(t p) m -> t p m", p=P)
        agg_rows = agg_dram.rearrange("(t p) m -> t p m", p=P)
        whole_rows = adj.rearrange("(t p) m -> t p m", p=P)
        att_rows = att_dram.rearrange("(t p) d -> t p d", p=P)
        att_steps = att_dram.rearrange("(j u p) d -> j p u d", u=PAIR, p=P)
        table0_heads = table0.rearrange("(t p) c -> p t c", p=P)
        table1_halves = table1.rearrange("(g t p) d -> g p t d", g=2, p=P)

        g_head_in = sem("g_head_in")
        g_diag_ready = sem("g_diag_ready")
        g_dst_summed = sem("g_dst_summed")
        g_dst_ready = sem("g_dst_ready")
        g_adj_in = sem("g_adj_in")
        g_dve = sem("g_dve")
        g_max_ready = sem("g_max_ready")
        g_exp_ready = sem("g_exp_ready")
        g_turned = sem("g_turned")
        g_turned_ready = sem("g_turned_ready")
        g_summed = sem("g_summed")
        g_out_ready = sem("g_out_ready")
        g_stored = sem("g_stored")
        g_att_in = sem("g_att_in")
        e_weights_in = sem("e_weights_in")
        e_idx_ready = sem("e_idx_ready")
        e_rows_in = sem("e_rows_in")
        e_turned = sem("e_turned")
        e_turned_ready = sem("e_turned_ready")
        e_proj = sem("e_proj")
        e_pair_dve = sem("e_pair_dve")
        e_pair_ready = sem("e_pair_ready")
        e_zero_ready = sem("e_zero_ready")
        e_zeroed = sem("e_zeroed")
        e_agg_zeroed = sem("e_agg_zeroed")
        e_pool = sem("e_pool")
        e_final = sem("e_final")
        e_val_ready = sem("e_val_ready")
        e_scattered = sem("e_scattered")
        e_in = sem("e_in")
        e_dve = sem("e_dve")
        e_max_ready = sem("e_max_ready")
        e_exp_ready = sem("e_exp_ready")
        e_agg_ready = sem("e_agg_ready")
        e_agg_stored = sem("e_agg_stored")
        e_agg_in = sem("e_agg_in")
        e_agg_turned = sem("e_agg_turned")
        e_aggT_ready = sem("e_aggT_ready")
        e_half_in = sem("e_half_in")
        e_summed = sem("e_summed")
        e_out_ready = sem("e_out_ready")
        e_out_stored = sem("e_out_stored")

        def read_flag(eng):
            eng.wait_ge(node_ready, 1)
            return eng.value_load(flag_i[0:1, 0:1], min_val=0, max_val=1)

        def dense0_sync(sp):
            with sp.Fori(0, HEADS) as h:
                sp.dma_start(d_head, table0_heads[:, :, bass.ds(h * DH, DH)]).then_inc(g_head_in, 16)
                with sp.Fori(0, TILES) as t:
                    n = h * TILES + t
                    sp.dma_start(d_adj, whole_rows[t]).then_inc(g_adj_in, 16)
                    sp.wait_ge(g_out_ready, n + 1)
                    sp.dma_start(att_rows[t][:, bass.ds(h * DH, DH)], d_out[:, 0:DH]).then_inc(g_stored, 16)
                    lone_wait(sp, node_ready, g_stored, 16 * (n + 1))

        def dense0_vector(dve):
            v = nc.vector
            with dve.Fori(0, HEADS) as h:
                with dve.Fori(0, TILES // KC) as c:
                    m = h * (TILES // KC) + c
                    v.tensor_tensor(d_diag, ident[:].unsqueeze(1).to_broadcast([P, KC, P]),
                                    src_dst[:].rearrange("p (c k) s -> p c k s", k=KC)[:, c, :, bass.ds(h + HEADS, 1)]
                                    .to_broadcast([P, KC, P]), ALU.mult).then_inc(g_diag_ready, 1)
                    dve.wait_ge(g_dst_summed, m + 1)
                    v.tensor_copy(d_dst.rearrange("p (c n) -> p c n", n=D)[:, c, :], bank[0][:]).then_inc(g_dst_ready, 1)
                    dve.wait_ge(g_dst_ready, m + 1)
                with dve.Fori(0, TILES) as t:
                    n = h * TILES + t
                    st = Steps(dve, g_dve, 10, n)
                    st.link(v.tensor_scalar(d_score, d_dst,
                                            src_dst[:].rearrange("p t s -> p (t s)")[:, bass.ds(t * 2 * HEADS + h, 1)],
                                            None, ALU.add))
                    st.link(v.scalar_tensor_tensor(out=d_score, in0=d_score, scalar=ALPHA, in1=d_score,
                                                   op0=ALU.mult, op1=ALU.max))
                    dve.wait_ge(g_adj_in, 16 * (n + 1))
                    st.link(v.tensor_scalar(d_adj, d_adj, 0.0, None, ALU.is_gt))
                    st.link(v.tensor_tensor(d_score, d_score, d_adj, ALU.mult))
                    st.link(v.tensor_scalar(d_adj, d_adj, 1.0, 9.0e15, ALU.subtract, ALU.mult))
                    st.link(v.tensor_tensor(d_score, d_score, d_adj, ALU.add))
                    st.link(v.tensor_reduce(d_max[:, 0:1], d_score, X_AXIS, ALU.max))
                    v.tensor_scalar(d_max[:, 1:2], d_max[:, 0:1], -1.0, None, ALU.mult).then_inc(g_max_ready, 1)
                    dve.wait_ge(g_exp_ready, n + 1)
                    st.link(v.reciprocal(d_sum[:, 1:2], d_sum[:, 0:1]))
                    dve.wait_ge(g_turned, n + 1)
                    for b in range(8):
                        last = v.tensor_copy(d_turned[:, b * D:(b + 1) * D], bank[b][:])
                        if b == 0:
                            st(last)
                    last.then_inc(g_turned_ready, 1)
                    dve.wait_ge(g_summed, n + 1)
                    v.tensor_scalar(d_out[:, 0:DH], bank[0][:, 0:DH], d_sum[:, 1:2], None, ALU.mult
                                    ).then_inc(g_out_ready, 1)
                    dve.wait_ge(g_stored, 16 * (n + 1))
                    st(v.tensor_copy(d_sum[:, 0:1], d_sum[:, 1:2]))
                    st.end()

        def dense0_scalar(act):
            with act.Fori(0, HEADS * TILES) as n:
                act.wait_ge(g_max_ready, n + 1)
                nc.scalar.activation(d_score, d_score, ACT.Exp, bias=d_max[:, 1:2], accum_out=d_sum[:, 0:1]
                                     ).then_inc(g_exp_ready, 1)

        def dense0_tensor(pe):
            with pe.Fori(0, HEADS) as h:
                with pe.Fori(0, TILES // KC) as c:
                    pe.wait_ge(g_diag_ready, h * (TILES // KC) + c + 1)
                    nc.tensor.matmul(bank[0][:], ones[:], d_diag.rearrange("p k n -> p (k n)"), start=True, stop=True
                                     ).then_inc(g_dst_summed, 1)
                with pe.Fori(0, TILES) as t:
                    n = h * TILES + t
                    pe.wait_ge(g_exp_ready, n + 1)
                    for b in range(TILES):
                        last = nc.tensor.transpose(bank[b // KC][:, b % KC * P:(b % KC + 1) * P],
                                                   d_score[:, b * P:(b + 1) * P], ident[:])
                    last.then_inc(g_turned, 1)
                    pe.wait_ge(g_head_in, 16 * (h + 1))
                    pe.wait_ge(g_turned_ready, n + 1)
                    for b in range(TILES):
                        last = nc.tensor.matmul(bank[0][:, 0:DH], d_turned[:, b * P:(b + 1) * P], d_head[:, b, :],
                                                start=(b == 0), stop=(b == TILES - 1))
                    last.then_inc(g_summed, 1)

        def dense1_sync(sp):
            for dst, src in ((d_weight[0], wqt.rearrange("(k p) n -> p k n", p=P)),
                             (d_weight[1], wkt.rearrange("(k p) n -> p k n", p=P)),
                             (d_bias[0], bq.partition_broadcast(P)), (d_bias[1], bk.partition_broadcast(P))):
                sp.dma_start(dst, src).then_inc(e_weights_in, 16)
            sp.wait_ge(e_zero_ready, 1)
            with sp.Fori(0, TILES) as t:
                for c in range(N // D):
                    sp.dma_start(agg_rows[t][:, c * D:(c + 1) * D], d_out).then_inc(e_agg_zeroed, 16)
            sp.wait_ge(e_agg_zeroed, 16 * 8 * TILES)
            with sp.Fori(0, HEADS) as h:
                with sp.Fori(0, TILES) as t:
                    for c in range(N // D):
                        sp.dma_start(full_rows[t][:, c * D:(c + 1) * D], d_out).then_inc(e_zeroed, 16)
                    lone_wait(sp, node_ready, e_zeroed, 16 * 8 * (h * TILES + t + 1))
                with sp.Fori(0, TILES) as t:
                    n = h * TILES + t
                    sp.wait_ge(e_scattered, 16 * PCOL * (h + 1))
                    sp.dma_start(d_score, full_rows[t]).then_inc(e_in, 16)
                    sp.dma_start(d_adj, whole_rows[t]).then_inc(e_in, 16)
                    sp.dma_start(d_agg, agg_rows[t]).then_inc(e_in, 16)
                    sp.wait_ge(e_agg_ready, n + 1)
                    sp.dma_start(agg_rows[t], d_agg).then_inc(e_agg_stored, 16)
                    lone_wait(sp, node_ready, e_agg_stored, 16 * (n + 1))
            with sp.Fori(0, TILES) as t:
                sp.dma_start(d_score, agg_rows[t]).then_inc(e_agg_in, 16)
                for g in both:
                    if g == 1:
                        sp.wait_ge(e_summed, 2 * t + 1)
                    sp.dma_start(d_h2, table1_halves[g]).then_inc(e_half_in, 16)
                sp.wait_ge(e_out_ready, t + 1)
                sp.dma_start(out_rows[t], d_out).then_inc(e_out_stored, 16)
                lone_wait(sp, node_ready, e_out_stored, 16 * (t + 1))

        def dense1_gpsimd(pool):
            g = nc.gpsimd
            with pool.Fori(0, PCOL) as c:
                g.tensor_copy(d_idx[:], pair_sb[:, c, :]).then_inc(e_pool, 1)
                lone_wait(pool, pairs_ready, e_pool, c + 1)
                for n in both:
                    g.indirect_dma_start(d_pair_h[n], None, table1,
                                         bass.IndirectOffsetOnAxis(ap=d_idx[:, n:n + 1], axis=0),
                                         bounds_check=N - 1, oob_is_err=False).then_inc(e_rows_in, 16)
                pool.wait_ge(e_pair_ready, c + 1)
            with pool.Fori(0, HEADS) as h:
                lone_wait(pool, node_ready, e_zeroed, 16 * 8 * TILES * (h + 1))
                with pool.Fori(0, PCOL) as c:
                    n = h * PCOL + c
                    g.tensor_copy(d_idx[:, 0:1], pair_idx[:, bass.ds(c, 1)]).then_inc(e_pool, 1)
                    g.tensor_copy(d_val[:], d_pair_att_flat[0:PP, bass.ds(c * HEADS + h, 1)]).then_inc(e_pool, 1)
                    lone_wait(pool, pairs_ready, e_pool, 2 * n + PCOL + 2)
                    g.indirect_dma_start(full_flat, bass.IndirectOffsetOnAxis(ap=d_idx[:, 0:1], axis=0), d_val[:], None,
                                         bounds_check=N * N - 1, oob_is_err=False).then_inc(e_scattered, 16)
                    pool.wait_ge(e_scattered, 16 * (n + 1))

        def dense1_scalar(act):
            with act.Fori(0, HEADS * TILES) as n:
                act.wait_ge(e_max_ready, n + 1)
                nc.scalar.activation(d_score, d_score, ACT.Exp, bias=d_max[:, 1:2], accum_out=d_sum[:, 0:1]
                                     ).then_inc(e_exp_ready, 1)

        def dense1_tensor(pe):
            pe.wait_ge(e_weights_in, 64)
            with pe.Fori(0, PCOL) as c:
                pe.wait_ge(e_rows_in, 32 * (c + 1))
                for n in both:
                    for k in range(KC):
                        last = nc.tensor.transpose(bank[n][:, k * P:k * P + PP], d_pair_h[n][:, k * P:(k + 1) * P],
                                                   ident[0:PP, 0:PP])
                last.then_inc(e_turned, 1)
                pe.wait_ge(e_turned_ready, c + 1)
                for n in both:
                    for k in range(KC):
                        last = nc.tensor.matmul(bank[2 + n][0:PP, :], d_pair_hT[n][:, k, 0:PP], d_weight[n][:, k, :],
                                                start=(k == 0), stop=(k == KC - 1))
                last.then_inc(e_proj, 1)
            with pe.Fori(0, TILES) as t:
                pe.wait_ge(e_agg_in, 16 * (t + 1))
                for b in range(TILES):
                    last = nc.tensor.transpose(bank[b // KC][:, b % KC * P:(b % KC + 1) * P],
                                               d_score[:, b * P:(b + 1) * P], ident[:])
                last.then_inc(e_agg_turned, 1)
                pe.wait_ge(e_aggT_ready, t + 1)
                for b in range(TILES):
                    if b % half == 0:
                        pe.wait_ge(e_half_in, 16 * (2 * t + b // half + 1))
                    last = nc.tensor.matmul(bank[0][:], d_adj[:, b * P:(b + 1) * P], d_h2[:, b % half, :],
                                            start=(b == 0), stop=(b == TILES - 1))
                    if b % half == half - 1:
                        last.then_inc(e_summed, 1)

        def dense1_vector(dve):
            v = nc.vector
            v.memset(d_out, 0.0).then_inc(e_zero_ready, 1)
            v.tensor_scalar(off_diag, ident[:], 0.0, None, ALU.is_equal).then_inc(e_final, 1)
            v.tensor_scalar(on_diag, ident[:], SELF_SCORE, None, ALU.mult).then_inc(e_final, 1)
            dve.wait_ge(e_final, 2)
            dve.wait_ge(e_weights_in, 64)
            with dve.Fori(0, PCOL) as c:
                st = Steps(dve, e_pair_dve, 5, c)
                dve.wait_ge(e_turned, c + 1)
                for n in both:
                    last = v.tensor_copy(d_pair_hT[n][:, :, 0:PP],
                                         bank[n][:].rearrange("p (k n) -> p k n", k=KC)[:, :, 0:PP])
                    if n == 0:
                        st(last)
                last.then_inc(e_turned_ready, 1)
                dve.wait_ge(e_proj, c + 1)
                for n in both:
                    st.link(v.tensor_tensor(d_pair_q[n], bank[2 + n][0:PP, :], d_bias[n][0:PP, :], ALU.add))
                st.link(v.tensor_tensor(d_pair_q[0], d_pair_q[0], d_pair_q[1], ALU.mult))
                st.link(v.tensor_reduce(d_pair_att[0:PP, c, :], d_pair_q[0].rearrange("p (h d) -> p h d", h=HEADS),
                                        X_AXIS, ALU.add))
                v.tensor_scalar(d_pair_att[0:PP, c, :], d_pair_att[0:PP, c, :], DH ** -0.5, None, ALU.mult
                                ).then_inc(e_pair_ready, 1)
                st.end()
            with dve.Fori(0, HEADS) as h:
                with dve.Fori(0, TILES) as t:
                    n = h * TILES + t
                    st = Steps(dve, e_dve, 8, n)
                    dve.wait_ge(e_in, 48 * (n + 1))
                    st.link(v.tensor_scalar(d_adj, d_adj, 1.0, None, ALU.is_equal))
                    st.link(v.tensor_tensor(d_score, d_score, d_adj, ALU.mult))
                    st.link(v.tensor_scalar(d_adj, d_adj, 1.0, NEGBIG, ALU.subtract, ALU.mult))
                    st.link(v.tensor_tensor(d_score, d_score, d_adj, ALU.add))
                    block_own = d_score[:, bass.ds(t * P, P)]
                    st.link(v.tensor_tensor(block_own, block_own, off_diag, ALU.mult))
                    st.link(v.tensor_tensor(block_own, block_own, on_diag, ALU.add))
                    st.link(v.tensor_reduce(d_max[:, 0:1], d_score, X_AXIS, ALU.max))
                    v.tensor_scalar(d_max[:, 1:2], d_max[:, 0:1], -1.0, None, ALU.mult).then_inc(e_max_ready, 1)
                    dve.wait_ge(e_exp_ready, n + 1)
                    st.link(v.reciprocal(d_sum[:, 1:2], d_sum[:, 0:1]))
                    v.tensor_scalar(d_sum[:, 1:2], d_sum[:, 1:2], 1.0 / HEADS, None, ALU.mult).then_inc(e_final, 1)
                    dve.wait_ge(e_final, n + 3)
                    v.scalar_tensor_tensor(out=d_agg, in0=d_score, scalar=d_sum[:, 1:2], in1=d_agg,
                                           op0=ALU.mult, op1=ALU.add).then_inc(e_agg_ready, 1)
                    dve.wait_ge(e_agg_ready, n + 1)
                    st.end()
            with dve.Fori(0, TILES) as t:
                dve.wait_ge(e_agg_turned, t + 1)
                for b in range(8):
                    last = v.tensor_copy(d_adj[:, b * D:(b + 1) * D], bank[b][:])
                last.then_inc(e_aggT_ready, 1)
                dve.wait_ge(e_summed, 2 * t + 2)
                v.tensor_tensor(d_out, bank[0][:], x_all[:, t, :], ALU.add).then_inc(e_out_ready, 1)
                dve.wait_ge(e_out_stored, 16 * (t + 1))
        block = ctx.enter_context(nc.Block())

        @block.sync
        def _(sp):
            sp.dma_start(pair_sb[:], pairs.rearrange("(p c) two -> p c two", c=PCOL)).then_inc(pair_in, 16)
            sp.dma_start(w0_sb, w0.rearrange("(k p) n -> p k n", p=P)).then_inc(weights0_in, 16)
            sp.dma_start(a_rows[:, 0, :], a1.partition_broadcast(P)).then_inc(weights0_in, 16)
            sp.dma_start(a_rows[:, 1, :], a2.partition_broadcast(P)).then_inc(weights0_in, 16)

            def load(i, b):
                t = BUFS * i + b
                if later(t, BUFS):
                    sp.wait_ge(adj_searched, t - BUFS + 1)
                sp.dma_start(x_all[:, t, :], x_rows[t]).then_inc(x_in[b], 16)
                sp.dma_start(adj_sb[b][:, :, 0:SEGW], adj_tiles[t]).then_inc(adj_in[b], 16)

            front_slots(sp, load)
            sp.dma_start(b4_row[:], b4.partition_broadcast(P)).then_inc(weights1_in, 16)
            sp.dma_start(diag[:], bass.AP(tensor=adj.tensor, offset=0, ap=[[N + 1, P], [(N + 1) * P, TILES]]),
                         allow_slow_non_contiguous=True).then_inc(diag_in, 16)
            sp.dma_start(w1_sb[:], w1t.rearrange("(k p) n -> p k n", p=P)).then_inc(weights2_in, 16)
            sp.dma_start(w2_sb[:], w2t.rearrange("(k p) n -> p k n", p=P)).then_inc(weights2_in, 16)
            sp.dma_start(w3_sb[:], w3t).then_inc(weights2_in, 16)
            sp.dma_start(w4_sb[:], w4t.rearrange("(k p) n -> p k n", p=P)).then_inc(weights2_in, 16)
            sp.dma_start(b1_sb[:], b1).then_inc(weights2_in, 16)
            sp.dma_start(b2_sb[:], b2).then_inc(weights2_in, 16)
            sp.dma_start(b3_sb[:], b3).then_inc(weights2_in, 16)
            sp.wait_ge(consts_made, N_CONSTS)
            for n in range(8):
                sp.dma_start(score_dram.rearrange("(n p r) h -> n p (r h)", n=8, p=P)[n], zeros[:]
                             ).then_inc(score_zeroed, 16)
            sp.wait_ge(node_ready, 1)
            sp.dma_start(keys_dram.rearrange("(t p) k -> p t k", p=P), node[:, :, 0:SLOTS]).then_inc(keys_stored, 16)

            for u in both:
                sp.wait_ge(wh_stored[u], 16 * STEPS)
            flag = read_flag(sp)
            with sp.If(flag > 0):
                dense0_sync(sp)

            def dense_att(j):
                with sp.If(flag > 0):
                    sp.wait_ge(att_ready, 2 * j + 2)
                    sp.dma_start(att, att_steps[j]).then_inc(g_att_in, 16)

            def self_rows(jj, q, first):
                if not first:
                    sp.wait_ge(agg_summed, 4 * jj + 2 * q - 2)
                sp.dma_start(gath[q][:, EC:GC, :], table0_steps[2 * jj + q]).then_inc(self_in[q], 16)

            for q in both:
                self_rows(0, q, True)
            with sp.Fori(1, STEPS // 2) as jj:
                for q in both:
                    self_rows(jj, q, False)
                    dense_att(2 * jj + q - 2)
            for q in both:
                dense_att(STEPS - 2 + q)

            sp.wait_ge(score_zeroed, 16 * 8)
            for u in both:
                sp.wait_ge(h2_stored[u], 16 * STEPS)
            sp.wait_ge(b4_added, TILES)
            sp.dma_start(wq_sb, wqt.rearrange("(k p) n -> p k n", p=P)).then_inc(late_in, 16)
            sp.dma_start(wk_sb, wkt.rearrange("(k p) n -> p k n", p=P)).then_inc(late_in, 16)
            sp.dma_start(bq_row[:], bq.partition_broadcast(P)).then_inc(late_in, 16)
            sp.dma_start(bk_row[:], bk.partition_broadcast(P)).then_inc(late_in, 16)

            def late_rows(jj, q, first):
                if not first:
                    sp.wait_ge(weight_ready, 2 * jj + q - 1)
                if first and q == 0:
                    sp.wait_ge(hit_stored, 16)
                sp.dma_start(score_in[q], score_steps[2 * jj + q]).then_inc(score_in_sem[q], 16)

            def store_out(jj, q):
                for u in both:
                    sp.wait_ge(out_ready, 4 * jj + 2 * q + u + 1)
                    sp.dma_start(out_rows[4 * jj + 2 * q + u], out_sb[q][:, u, :]).then_inc(out_stored[2 * q + u], 16)

            for q in both:
                late_rows(0, q, True)
            with sp.Fori(1, STEPS // 2) as jj:
                for q in both:
                    late_rows(jj, q, False)
                    store_out(jj - 1, q)
            for q in both:
                store_out(STEPS // 2 - 1, q)
            for stored in out_stored:
                sp.wait_ge(stored, 8 * STEPS)
            with sp.If(flag > 0):
                dense1_sync(sp)

        @block.gpsimd
        def _(pool):
            g = nc.gpsimd
            g.iota(iota[:], pattern=[[1, EDGES]], base=0, channel_multiplier=0,
                   allow_small_or_imprecise_dtypes=True).then_inc(consts_made, 1)
            g.memset(ident[:], 0.0).then_inc(consts_made, 1)
            g.memset(before[:], 1.0).then_inc(consts_made, 1)
            g.memset(ones[:], 1.0).then_inc(consts_made, 1)
            g.memset(zeros[:], 0.0).then_inc(consts_made, 1)
            pool.wait_ge(consts_made, 5)
            g.affine_select(out=ident[:], in_=ident[:], compare_op=ALU.not_equal, fill=1.0, base=0,
                            pattern=[[1, P]], channel_multiplier=-1).then_inc(consts_made, 1)
            g.affine_select(out=before[:], in_=before[:], compare_op=ALU.is_gt, fill=0.0, base=0,
                            pattern=[[1, P]], channel_multiplier=-1).then_inc(consts_made, 1)
            g.iota(seg_base[:], pattern=[[SEGW, SEG], [0, 8]], base=1, channel_multiplier=0,
                   allow_small_or_imprecise_dtypes=True).then_inc(consts_made, 1)
            g.iota(self_key[:], pattern=[[P, TILES]], base=1, channel_multiplier=1,
                   allow_small_or_imprecise_dtypes=True).then_inc(consts_made, 1)
            g.iota(edge_pos[:], pattern=[[0, PAIR], [P, CH]], base=0, channel_multiplier=1,
                   allow_small_or_imprecise_dtypes=True).then_inc(consts_made, 1)

            pool.wait_ge(pairs_ready, 1)
            with pool.Fori(0, PCOL // PG) as n:
                g.tensor_copy(idx8[:], pair_idx[:].rearrange("p (n c) -> p n c", c=PG)[:, n, :]).then_inc(pool_pair, 1)
                lone_wait(pool, pairs_ready, pool_pair, 2 * n + 1)
                for c in range(PG):
                    g.indirect_dma_start(adj8[:, c:c + 1], None, adj_flat,
                                         bass.IndirectOffsetOnAxis(ap=idx8[:, c:c + 1], axis=0),
                                         bounds_check=N * N - 1, oob_is_err=False).then_inc(pair_adj_in, 16)
                pool.wait_ge(pair_adj_in, 16 * PG * (n + 1))
                g.tensor_copy(pair_adj[:].rearrange("p (n c) -> p n c", c=PG)[:, n, :], adj8[:]).then_inc(pool_pair, 1)
            pool.wait_ge(weights1_in, 16)
            with pool.Fori(0, TILES) as t:
                pool.wait_ge(h_made, t + 1)
                g.tensor_tensor(x_all[:, t, :], x_all[:, t, :], b4_row[:], ALU.add).then_inc(b4_added, 1)

            for u in both:
                pool.wait_ge(wh_stored[u], 16 * STEPS)
            flag = read_flag(pool)
            with pool.If(flag > 0):
                pool.wait_ge(g_stored, 16 * HEADS * TILES)

            def gather(table, width, jj, q, first, ready, used, into):
                lone_wait(pool, pairs_ready, ready, 2 * jj + q + 1)
                for c in range(EC):
                    if not first and c % CH == 0:
                        lone_wait(pool, pairs_ready, used, 4 * jj + 2 * q - 3 + c // CH)
                    g.indirect_dma_start(gath[q][:, c, 0:width], None, table,
                                         bass.IndirectOffsetOnAxis(ap=edge_idx[q][:, c:c + 1], axis=0),
                                         bounds_check=N - 1, oob_is_err=False).then_inc(into[q], 16)

            for q in both:
                gather(table0, ROW, 0, q, True, idx_ready, agg_summed, gath_in)
            with pool.Fori(1, STEPS // 2) as jj:
                for q in both:
                    gather(table0, ROW, jj, q, False, idx_ready, agg_summed, gath_in)

            for u in both:
                pool.wait_ge(h2_stored[u], 16 * STEPS)
            pool.wait_ge(keys_stored, 16)
            g.memset(hit_keys[:], 0.0).then_inc(pool_pair, 1)
            pool.wait_ge(pool_pair, 2 * (PCOL // PG) + 1)
            pool.wait_ge(hit_summed, 1)
            pool.wait_ge(dve_mid, MID_TICKS)
            for dst, table, idx in ((hit_h[0], table1, hit_sub), (hit_h[1], table1, hit_obj),
                                    (hit_keys[:], keys_dram, hit_sub)):
                g.indirect_dma_start(dst, None, table, bass.IndirectOffsetOnAxis(ap=idx[:, 0:1], axis=0),
                                     bounds_check=N - 1, oob_is_err=False).then_inc(hit_in, 16)
            gather(table1, D, 0, 0, True, idx1_ready, agg1_summed, gath1_in)
            pool.wait_ge(hit_att_ready, 1)
            g.indirect_dma_start(score_dram, bass.IndirectOffsetOnAxis(ap=hit_dst[:, 0:1], axis=0), hit_att[:], None,
                                 bounds_check=N * SLOTS - 1, oob_is_err=False).then_inc(hit_stored, 16)
            gather(table1, D, 0, 1, True, idx1_ready, agg1_summed, gath1_in)
            with pool.Fori(1, STEPS // 2) as jj:
                for q in both:
                    gather(table1, D, jj, q, False, idx1_ready, agg1_summed, gath1_in)
            for stored in out_stored:
                pool.wait_ge(stored, 8 * STEPS)
            with pool.If(flag > 0):
                dense1_gpsimd(pool)

        @block.scalar
        def _(act):
            s = nc.scalar

            def turn_copy(t, u):
                act.wait_ge(h_turned, t + 1)
                if later(t, 2):
                    act.wait_ge(wh_summed, t - 1)
                s.copy(hT[u].rearrange("p k n -> p (k n)"), bank[u][:]).then_inc(hT_ready, 1)

            def copy_table(t, u, stored_before):
                act.wait_ge(wh_summed, t + 1)
                if later(t, 2):
                    act.wait_ge(wh_stored[u], 16 * stored_before)
                s.copy(wh_row[u][:, 0:D], bank[2 + u][:]).then_inc(wh_copied, 1)
                s.copy(wh_row[u][:, D:ROW], bank[4 + u][:, HEADS:2 * HEADS]).then_inc(wh_copied, 1)
                s.copy(src_dst[:, t, :], bank[4 + u][:, 0:2 * HEADS]).then_inc(wh_copied, 1)
                act.wait_ge(wh_copied, 3 * t + 2)
                act.dma_start(table0_rows[t], wh_row[u]).then_inc(wh_stored[u], 16)

            def front(i, b):
                t, u = BUFS * i + b, b % 2
                act.wait_ge(var_ready, t + 1)
                s.activation(std[u][:], mean_var[u][:, 1:2], ACT.Sqrt, bias=eps_col[:, 0:1]).then_inc(std_ready, 1)
                if later(t, 1):
                    turn_copy(t - 1, 1 - u)
                act.wait_ge(ln_ready, t + 1)
                if later(t, 2):
                    act.wait_ge(h_turned, t - 1)
                s.activation(h_sb[u], x_all[:, t, :], ACT.Relu, bias=ln_shift[u][:, 0:1],
                             scale=ln_scale[u][:, 0:1]).then_inc(h_made, 1)
                if later(t, 2):
                    copy_table(t - 2, u, 2 * i + b // 2 - 1)

            front_slots(act, front)
            turn_copy(TILES - 1, 1)
            copy_table(TILES - 2, 0, STEPS - 1)
            copy_table(TILES - 1, 1, STEPS - 1)

            def info(j, q):
                act.wait_ge(info_summed, j + 1)
                if later(j, 2):
                    act.wait_ge(exponent_ready, j - 1)
                s.copy(edge_info[q][:].rearrange("p c v -> p (c v)"), bank[0][:, 0:EC * VW]).then_inc(info_ready, 1)

            def probabilities(j, q):
                act.wait_ge(exponent_ready, j + 1)
                if later(j, 2):
                    act.wait_ge(agg_summed, 2 * j - 2)
                s.activation(prob[q][:], edge_e[:, 2], ACT.Exp).then_inc(prob_ready, 1)

            def elu_parts_of(j, u):
                with act.If(flag > 0):
                    lone_wait(act, node_ready, g_att_in, 16 * (j + 1))
                act.wait_ge(att_ready, 2 * j + u + 1)
                s.activation(att_exp[:, u, :], att[:, u, :], ACT.Exp).then_inc(elu_parts, 1)
                act.wait_ge(elu_parts, 4 * j + 2 * u + 1)
                s.activation(att[:, u, :], att[:, u, :], ACT.Relu).then_inc(elu_parts, 1)

            def mlp_bias_relu(j, layer):
                act.wait_ge(mlp_summed, 5 * j + layer)
                if layer == 2:
                    s.activation(z2, bank[7][:, 0:PAIR * P], ACT.Relu, bias=b2_sb[:, 0:1]).then_inc(mlp_relu, 1)
                else:
                    for m in range(2):
                        s.activation((z1, z3)[layer // 2][:, m, :], bank[6][:, 256 * m:256 * (m + 1)], ACT.Relu,
                                     bias=(b1_sb, b3_sb)[layer // 2][:, m:m + 1]).then_inc(mlp_relu, 1)

            def layer1_input(j):
                for u in both:
                    act.wait_ge(ln2_ready, 2 * j + u + 1)
                    if later(j, 1):
                        act.wait_ge(h2_stored[u], 16 * j)
                    s.activation(h2_sb[:, u, :], x_all[:, 2 * j + u, :], ACT.Relu, bias=ln2_shift[:, j, u:u + 1],
                                 scale=ln2_scale[:, j, u:u + 1]).then_inc(h2_made, 1)
                    act.wait_ge(h2_made, 2 * j + u + 1)
                    act.dma_start(table1_rows[2 * j + u], h2_sb[:, u, :]).then_inc(h2_stored[u], 16)

            act.wait_ge(weights2_in, 7 * 16)
            flag = read_flag(act)
            with act.If(flag > 0):
                dense0_scalar(act)
            info(0, 0)
            info(1, 1)
            probabilities(0, 0)

            def body(jj, q):
                j = 2 * jj + q
                if has(j, 1, STEPS):
                    for u in both:
                        act.wait_ge(enc_turned, 2 * j + u - 1)
                        s.activation(encT[:, :, u * P:(u + 1) * P], bank[4 + u][:].rearrange("p (k n) -> p k n", k=KC),
                                     ACT.Identity, bias=neg_one[:, 0:1]).then_inc(encT_ready, 1)
                if has(j, 0, STEPS - 3):
                    info(j + 2, q)
                if has(j, 0, STEPS - 1):
                    for u in both:
                        elu_parts_of(j, u)
                if has(j, 1, STEPS):
                    mlp_bias_relu(j - 1, 1)
                if has(j, 2, STEPS + 1):
                    for u in both:
                        act.wait_ge(var2_ready, 2 * j + u - 3)
                        s.activation(std[u][:], mean_var[u][:, 1:2], ACT.Sqrt, bias=eps_col[:, 0:1]
                                     ).then_inc(std2_ready, 1)
                if has(j, 1, STEPS):
                    mlp_bias_relu(j - 1, 2)
                    mlp_bias_relu(j - 1, 3)
                if has(j, 0, STEPS - 2):
                    probabilities(j + 1, 1 - q)
                if has(j, 2, STEPS + 1):
                    layer1_input(j - 2)

            edge_pipeline(act, body)

            for n in both:
                act.wait_ge(hit_turned, n + 1)
                if n:
                    act.wait_ge(hit_proj, 1)
                s.copy(hit_hT.rearrange("p k n -> p (k n)"), bank[n][:]).then_inc(hit_hT_ready, 1)

            def late_exp(j):
                act.wait_ge(soft_ready, j + 1)
                s.activation(soft, soft, ACT.Exp).then_inc(soft_exp, 1)

            def own_part(j, q):
                act.wait_ge(own_ready, j + 1)
                if later(j, 2):
                    act.wait_ge(out_ready, 2 * j - 2)
                for u in both:
                    s.activation(gath[q][:, EC + u, 0:D], x_all[:, 2 * j + u, :], ACT.Relu,
                                 bias=own_shift[:, q, u:u + 1], scale=own_scale[:, q, u:u + 1]).then_inc(own_made, 1)

            def late_body(jj, q):
                j = 2 * jj + q
                late_exp(j)
                own_part(j, q)

            for q in both:
                late_body(0, q)
            with act.Fori(1, STEPS // 2) as jj:
                for q in both:
                    late_body(jj, q)
            with act.If(flag > 0):
                dense1_scalar(act)

        @block.tensor
        def _(pe):
            mm = nc.tensor.matmul
            turn = nc.tensor.transpose
            pe.wait_ge(consts_made, N_CONSTS)
            pe.wait_ge(weights0_in, 48)
            pe.wait_ge(fold_ready, 1)

            def project(t, u):
                pe.wait_ge(hT_ready, t + 1)
                if later(t, 2):
                    pe.wait_ge(wh_copied, 3 * t - 3)
                for k in range(KC):
                    mm(bank[2 + u][:], hT[u][:, k, :], w0_sb[:, k, :], start=(k == 0), stop=(k == KC - 1))
                for k in range(KC):
                    last = mm(bank[4 + u][:, 0:2 * HEADS], hT[u][:, k, :], a_fold[:, k, :],
                              start=(k == 0), stop=(k == KC - 1))
                last.then_inc(wh_summed, 1)

            def front(i, b):
                t, u = BUFS * i + b, b % 2
                if later(t, 1):
                    project(t - 1, 1 - u)
                pe.wait_ge(h_made, t + 1)
                if later(t, 2):
                    pe.wait_ge(hT_ready, t - 1)
                for k in range(KC):
                    last = turn(bank[u][:, k * P:(k + 1) * P], h_sb[u][:, k * P:(k + 1) * P], ident[:])
                last.then_inc(h_turned, 1)

            front_slots(pe, front)
            project(TILES - 1, 1)

            pe.wait_ge(counts_ready, 1)
            mm(bank[6][:, 0:TILES], before[:], count[:], start=True, stop=True)
            mm(bank[6][:, TILES:2 * TILES], ones[:], count[:], start=True, stop=True)
            mm(bank[6][:, 64:65], before[:], hit_end[:, 0:1], start=True, stop=True)
            mm(bank[6][:, 65:66], ones[:], hit_end[:, 0:1], start=True, stop=True).then_inc(offsets_summed, 1)
            pe.wait_ge(hit_rows_ready, 1)
            mm(bank[7][:, 0:17], hit_rows[:], hit_node[:], start=True, stop=True).then_inc(hit_summed, 1)
            pe.wait_ge(flags_ready, 1)
            mm(bank[3][:, 0:1], ones[:], flag_f[:, 0:1], start=True, stop=True).then_inc(flags_summed, 1)

            def info(j, q):
                if later(j, 2):
                    pe.wait_ge(exponent_ready, j - 1)
                if later(j, 1):
                    pe.wait_ge(info_ready, j)
                for u in both:
                    pe.wait_ge(rows_ready, 2 * j + u + 1)
                    for c in range(CH):
                        last = mm(bank[0][:, (u * CH + c) * VW:(u * CH + c + 1) * VW],
                                  row_hot[q][:, u, c * P:(c + 1) * P], step_node(j)[:, u, :], start=True, stop=True)
                last.then_inc(info_summed, 1)

            def slots(j, q):
                pe.wait_ge(placed_ready, j + 1)
                pe.wait_ge(hot_ready, j + 1)
                if later(j, 1):
                    pe.wait_ge(att_ready, 2 * j)
                for u in both:
                    for c in range(CH):
                        last = mm(bank[1][:, u * P:(u + 1) * P], edge_hot[q][:, u * CH + c, :],
                                  placed[:, u * CH + c].rearrange("p k h -> p (k h)"),
                                  start=(c == 0), stop=(c == CH - 1))
                last.then_inc(slots_summed, 1)

            def edge_max(j, q, copied):
                pe.wait_ge(row_max_ready, j + 1)
                pe.wait_ge(info_ready, copied)
                for u in both:
                    for c in range(CH):
                        n = u * CH + c
                        last = mm(bank[0][:, EC * VW + n * HEADS:EC * VW + (n + 1) * HEADS],
                                  row_hot[q][:, u, c * P:(c + 1) * P], row_max[q][:, u, :], start=True, stop=True)
                last.then_inc(edge_max_summed, 1)

            def hot_of(q, u, c):
                return (edge_hot[q][:, u * CH + c, :], u * CH + c) if c < CH else (ident[:], EC + u)

            def exp_sums(j, q):
                pe.wait_ge(prob_ready, j + 1)
                for u in both:
                    for c in range(CH + 1):
                        hot, n = hot_of(q, u, c)
                        mm(bank[1][:, 2 * P + u * HEADS:2 * P + (u + 1) * HEADS], hot, prob[q][:, n, :],
                           start=(c == 0), stop=(c == CH))

            def aggregate(j, q, u):
                if later(j, 1):
                    pe.wait_ge(att_ready, 2 * j + u - 1)
                for c in range(CH + 1):
                    hot, n = hot_of(q, u, c)
                    if c in (0, 2, CH):
                        pe.wait_ge(scaled, 5 * j + (3 if c == CH else 1 + c // 2 + 3 * u))
                    last = mm(bank[2 + u][:], hot, gath[q][:, n, 0:D], start=(c == 0), stop=(c == CH))
                last.then_inc(agg_summed, 1)

            def turn_enc(j):
                pe.wait_ge(enc_ready, 2 * j + 2)
                for u in both:
                    for k in range(KC):
                        last = turn(bank[4 + u][:, k * P:(k + 1) * P], att_exp[:, u, k * P:(k + 1) * P], ident[:])
                    last.then_inc(enc_turned, 1)

            def mlp(j, layer):
                if layer == 1:
                    pe.wait_ge(encT_ready, 2 * j + 2)
                    if later(j, 1):
                        pe.wait_ge(x_added, 2 * j)
                    for m in range(2):
                        for k in range(KC):
                            last = mm(bank[6][:, 256 * m:256 * (m + 1)], w1_sb[:, k, m * P:(m + 1) * P],
                                      encT[:, k, :], start=(k == 0), stop=(k == KC - 1))
                elif layer == 2:
                    pe.wait_ge(mlp_relu, 5 * j + 2)
                    for k in range(2):
                        last = mm(bank[7][:, 0:PAIR * P], w2_sb[:, k, :], z1[:, k, :], start=(k == 0), stop=(k == 1))
                elif layer == 3:
                    pe.wait_ge(mlp_relu, 5 * j + 3)
                    for m in range(2):
                        last = mm(bank[6][:, 256 * m:256 * (m + 1)], w3_sb[:, m * P:(m + 1) * P], z2,
                                  start=True, stop=True)
                else:
                    pe.wait_ge(mlp_relu, 5 * j + 5)
                    for u in both:
                        for k in range(2):
                            last = mm(bank[7 - u][:], z3[:, k, u * P:(u + 1) * P], w4_sb[:, k, :],
                                      start=(k == 0), stop=(k == 1))
                        if u == 0:
                            last.then_inc(mlp_summed, 1)
                last.then_inc(mlp_summed, 1)

            flag = read_flag(pe)
            with pe.If(flag > 0):
                dense0_tensor(pe)
            pe.wait_ge(weights2_in, 7 * 16)
            info(0, 0)
            info(1, 1)
            slots(0, 0)
            edge_max(0, 0, 2)

            def body(jj, q):
                j = 2 * jj + q
                if has(j, 0, STEPS - 1):
                    exp_sums(j, q)
                    aggregate(j, q, 0)
                if has(j, 1, STEPS):
                    turn_enc(j - 1)
                if has(j, 0, STEPS - 3):
                    info(j + 2, q)
                if has(j, 0, STEPS - 1):
                    aggregate(j, q, 1)
                if has(j, 1, STEPS):
                    mlp(j - 1, 1)
                if has(j, 0, STEPS - 2):
                    slots(j + 1, 1 - q)
                if has(j, 1, STEPS):
                    mlp(j - 1, 2)
                    mlp(j - 1, 3)
                if has(j, 0, STEPS - 2):
                    edge_max(j + 1, 1 - q, STEPS if isinstance(j, int) and j == STEPS - 2 else j + 3)
                if has(j, 1, STEPS):
                    mlp(j - 1, 4)

            edge_pipeline(pe, body)

            pe.wait_ge(hit_in, 48)
            for n in both:
                for k in range(KC):
                    last = turn(bank[n][:, k * P:(k + 1) * P], hit_h[n][:, k * P:(k + 1) * P], ident[:])
                last.then_inc(hit_turned, 1)
            pe.wait_ge(late_in, 64)
            for n in both:
                pe.wait_ge(hit_hT_ready, n + 1)
                for k in range(KC):
                    last = mm(bank[6 + n][:], hit_hT[:, k, :], (wq_sb, wk_sb)[n][:, k, :],
                              start=(k == 0), stop=(k == KC - 1))
                last.then_inc(hit_proj, 1)

            def edge_weights(j, q):
                pe.wait_ge(rows1_ready, 2 * j + 2)
                pe.wait_ge(weight_ready, j + 1)
                if later(j, 1):
                    pe.wait_ge(hot1_ready, j)
                for n in range(EC):
                    last = mm(bank[0][:, n * SLOTS:(n + 1) * SLOTS], row_hot[q][:, n // CH, n % CH * P:(n % CH + 1) * P],
                              weight[q][:, n // CH, 0:SLOTS], start=True, stop=True)
                last.then_inc(edge_w_summed, 1)

            def late(jj, q, first, last_step=False):
                j = 2 * jj + q
                if not last_step:
                    edge_weights(j + 1, 1 - q)
                if not first:
                    pe.wait_ge(out_ready, 2 * j - 2)
                pe.wait_ge(hot1_ready, j + 1)
                pe.wait_ge(gath1_in[q], 16 * EC * (jj + 1))
                for u in both:
                    for c in range(CH):
                        last = mm(bank[2 + 2 * q + u][:], edge_hot[q][:, u * CH + c, :], gath[q][:, u * CH + c, 0:D],
                                  start=(c == 0), stop=(c == CH - 1))
                    last.then_inc(agg1_summed, 1)

            edge_weights(0, 0)
            for q in both:
                late(0, q, True)
            with pe.Fori(1, STEPS // 2 - 1) as jj:
                for q in both:
                    late(jj, q, False)
            late(STEPS // 2 - 1, 0, False)
            late(STEPS // 2 - 1, 1, False, True)
            for stored in out_stored:
                pe.wait_ge(stored, 8 * STEPS)
            with pe.If(flag > 0):
                dense1_tensor(pe)

        @block.vector
        def _(dve):
            v = nc.vector

            st = Steps(dve, dve_start, START_TICKS, 0)
            for b in bufs:
                st(v.memset(adj_sb[b][:, :, SEGW:SEGP], 1.0))
            st(v.memset(ones8[:], 1.0))
            st(v.memset(neg_one[:], -1.0))
            st(v.memset(eps_col[:], EPS))
            st(v.memset(hit_key[:], 0.0))
            st(v.memset(slot_bias[:, :, SLOTS:SLOTS + 1], 0.0))
            dve.wait_ge(pair_in, 16)
            st(v.scalar_tensor_tensor(out=pair_flat[:], in0=pair_sb[:, :, 0], scalar=float(N), in1=pair_sb[:, :, 1],
                                      op0=ALU.mult, op1=ALU.add))
            st.link(v.tensor_tensor(pair_ne[:], pair_sb[:, :, 0], pair_sb[:, :, 1], ALU.not_equal))
            v.tensor_copy(pair_idx[:], pair_flat[:]).then_inc(pairs_ready, 1)
            dve.wait_ge(weights0_in, 48)
            for k in range(KC):
                for a in range(2):
                    st.link(v.tensor_tensor(fold_tmp, w0_sb[:, k, :], a_rows[:, a, :], ALU.mult))
                    last = v.tensor_reduce(a_fold[:, k, a * HEADS:(a + 1) * HEADS],
                                           fold_tmp.rearrange("p (h d) -> p h d", h=HEADS), X_AXIS, ALU.add)
                    if (k, a) != (KC - 1, 1):
                        st.link(last)
            last.then_inc(fold_ready, 1)
            st.end()

            def alone(sem, value):
                lone_wait(dve, fold_ready, sem, value)


            def neighbours(t, u, st, k):
                if k == 0:
                    st(v.tensor_tensor(key_raw[u][:], found[u][:], seg_base[:], ALU.add))
                elif k == 1:
                    st.after(st.k)
                    st(v.scalar_tensor_tensor(out=key_any[u][:], in0=found[u][:], scalar=float(SEGW), in1=key_raw[u][:],
                                              op0=ALU.is_lt, op1=ALU.mult))
                elif k == 2:
                    st.after(st.k)
                    flat = key_any[u][:].rearrange("p s c -> p (s c)")
                    st(v.scalar_tensor_tensor(out=key_nbr[u][:], in0=flat, scalar=self_key[:, bass.ds(t, 1)], in1=flat,
                                              op0=ALU.not_equal, op1=ALU.mult))
                elif k == 3:
                    alone(st.sem, st.base + st.k)
                    st(v.max(key16[u][:, 0:8], key_nbr[u][:]))
                elif k == 4:
                    alone(st.sem, st.base + st.k)
                    st(v.match_replace(key_left[u][:], key16[u][:, 0:8], key_nbr[u][:], 0.0))
                elif k == 5:
                    alone(st.sem, st.base + st.k)
                    st(v.max(key16[u][:, 8:16], key_left[u][:]))
                elif k == 6:
                    st(v.tensor_copy(seg_last[:, t, :], key_any[u][:, :, 7]))
                elif k == 7:
                    st.after(st.k - 1)
                    st(v.tensor_copy(node[:, t, 0:SLOTS], key16[u][:]))

            def front(i, b):
                t, u = BUFS * i + b, b % 2
                st = Steps(dve, dve_front, FRONT_TICKS, t)
                nbr = Steps(dve, dve_nbr, NBR_TICKS, t - 1)
                alone(x_in[b], 16 * (i + 1))
                stats_at = st(v.bn_stats(stats[u][:], x_all[:, t, :]))
                alone(adj_in[b], 16 * (i + 1))
                for g in range(SEG):
                    done = v.max_index(found[u][:, g, :], ones8[:], adj_sb[b][:, g, :])
                    if g == SEG - 1:
                        done.then_inc(adj_searched, 1)
                    else:
                        st(done)
                    if g == 0:
                        alone(st.sem, st.base + stats_at)
                        v.bn_aggr(mean_var[u][:], stats[u][:]).then_inc(var_ready, 1)
                    if g == 5:
                        dve.wait_ge(std_ready, t + 1)
                        if later(t, 2):
                            dve.wait_ge(h_made, t - 1)
                        stats_at = st(v.reciprocal(ln_scale[u][:], std[u][:]))
                    if g == 6:
                        st.after(stats_at)
                        v.scalar_tensor_tensor(out=ln_shift[u][:], in0=mean_var[u][:, 0:1], scalar=-1.0,
                                               in1=ln_scale[u][:], op0=ALU.mult, op1=ALU.mult
                                               ).then_inc(ln_ready, 1)
                    if later(t, 1):
                        if g == 0:
                            dve.wait_ge(adj_searched, t)
                        neighbours(t - 1, 1 - u, nbr, g)
                st.end()

            dve.wait_ge(consts_made, N_CONSTS)
            front_slots(dve, front)
            dve.wait_ge(adj_searched, TILES)
            nbr = Steps(dve, dve_nbr, NBR_TICKS, TILES - 1)
            for k in range(NBR_TICKS):
                neighbours(TILES - 1, 1, nbr, k)
            nbr.end()
            dve.wait_ge(dve_nbr, NBR_TICKS * TILES)

            st = Steps(dve, dve_mid, MID_TICKS, 0)
            valid = slot_bias[:, :, 0:SLOTS]
            st.link(v.tensor_scalar(valid, node[:, :, 0:SLOTS], 0.0, None, ALU.is_gt))
            st(v.tensor_reduce(count[:], valid, X_AXIS, ALU.add))
            dve.wait_ge(pool_pair, 2 * (PCOL // PG))
            st.link(v.scalar_tensor_tensor(out=pair_ne[:], in0=pair_adj[:], scalar=1.0, in1=pair_ne[:],
                                           op0=ALU.is_equal, op1=ALU.mult))
            st.link(v.scalar_tensor_tensor(out=hit_key[0:PP, :], in0=pair_flat[:], scalar=1.0, in1=pair_ne[:],
                                           op0=ALU.add, op1=ALU.mult))
            st.link(v.max(hit8[:], hit_key[:]))
            st(v.tensor_scalar(hit8_m1[:], hit8[:], -1.0, None, ALU.add))
            st.link(v.tensor_scalar(hit_valid[:], hit8[:], 0.0, None, ALU.is_gt))
            v.tensor_reduce(hit_end[:, 0:1], hit_valid[:], X_AXIS, ALU.add).then_inc(counts_ready, 1)
            st(v.tensor_scalar(valid, valid, 1.0, NEGBIG, ALU.subtract, ALU.mult))
            st(v.tensor_scalar(hit_sub_i[:], hit8_m1[:], 12, None, ALU.logical_shift_right))
            st.link(v.tensor_scalar(hit_obj_i[:], hit8_m1[:], N - 1, None, ALU.bitwise_and))
            st(v.scalar_tensor_tensor(out=hit_node[:, 0:8], in0=hit_sub_i[:], scalar=1.0, in1=hit_valid[:],
                                      op0=ALU.add, op1=ALU.mult))
            st(v.scalar_tensor_tensor(out=hit_node[:, 8:16], in0=hit_obj_i[:], scalar=1.0, in1=hit_valid[:],
                                      op0=ALU.add, op1=ALU.mult))
            st(v.tensor_reduce(flag_f[:, 1:2], seg_last[:].rearrange("p t s -> p (t s)"), X_AXIS, ALU.max))
            st(v.tensor_reduce(flag_f[:, 2:3], node[:, :, SLOTS - 1], X_AXIS, ALU.max))
            dve.wait_ge(diag_in, 16)
            st(v.tensor_reduce(flag_f[:, 3:4], diag[:], X_AXIS, ALU.min))
            dve.wait_ge(offsets_summed, 1)
            st(v.tensor_copy(node[:, :, OFFC], bank[6][:, 0:TILES]))
            st(v.tensor_tensor(end[:], bank[6][:, 0:TILES], count[:], ALU.add))
            st(v.tensor_copy(node[:, :, ROWC], self_key[:, 0:1].to_broadcast([P, TILES])))
            st(v.tensor_copy(hit_node[:, 16:17], bank[6][:, 64:65]))
            st(v.tensor_tensor(hit_end[:, 1:2], bank[6][:, 64:65], hit_end[:, 0:1], ALU.add))
            st(v.tensor_reduce(flag_f[:, 4:5], bank[6][:, TILES:2 * TILES], X_AXIS, ALU.max))
            st(v.tensor_scalar(flag_f[:, 5:6], bank[6][:, 65:66], float(P), None, ALU.is_gt))
            dve.wait_ge(wh_copied, 6 * STEPS)
            st.link(v.tensor_copy(node[:, :, SRCC:VW], src_dst[:, :, 0:HEADS]))
            st.link(v.tensor_scalar(hit_cmp[:], iota[:, 0:P], hit_node[:, 16:17], None, ALU.is_ge))
            v.scalar_tensor_tensor(out=hit_rows[:], in0=iota[:, 0:P], scalar=hit_end[:, 1:2], in1=hit_cmp[:],
                                   op0=ALU.is_lt, op1=ALU.mult).then_inc(hit_rows_ready, 1)
            st.link(v.tensor_tensor(flag_f[:, 1:2], flag_f[:, 1:2], flag_f[:, 2:3], ALU.max))
            st.link(v.tensor_tensor(flag_f[:, 1:2], flag_f[:, 1:2], hit8[:, 7:8], ALU.max))
            st(v.tensor_scalar(flag_f[:, 1:2], flag_f[:, 1:2], 0.0, None, ALU.is_gt))
            st(v.tensor_scalar(flag_f[:, 3:4], flag_f[:, 3:4], 1.0, None, ALU.not_equal))
            st.link(v.tensor_scalar(flag_f[:, 4:5], flag_f[:, 4:5], float(EDGES), None, ALU.is_gt))
            st.link(v.tensor_tensor(flag_f[:, 1:2], flag_f[:, 1:2], flag_f[:, 3:4], ALU.add))
            st.link(v.tensor_tensor(flag_f[:, 1:2], flag_f[:, 1:2], flag_f[:, 4:5], ALU.add))
            v.tensor_tensor(flag_f[:, 0:1], flag_f[:, 1:2], flag_f[:, 5:6], ALU.add).then_inc(flags_ready, 1)
            dve.wait_ge(hit_summed, 1)
            st(v.tensor_copy(hit_e[:], bank[7][:, 0:17]))
            st.link(v.tensor_tensor(hit_slot[:], edge_pos[:, 0, 0:1], bank[7][:, 16:17], ALU.subtract))
            st.link(v.tensor_scalar(hit_sel[:], iota[:, 0:8], hit_slot[:, 0:1], None, ALU.is_equal))
            for part, node1, idx, f in ((0, hit_sub1, hit_sub, 0), (8, hit_obj1, hit_obj, 2)):
                st.link(v.tensor_tensor(hit_tmp[:], hit_e[:, part:part + 8], hit_sel[:], ALU.mult))
                st.link(v.tensor_reduce(node1[:], hit_tmp[:], X_AXIS, ALU.add))
                st.link(v.tensor_scalar(hit_f[:, f:f + 1], node1[:], 0.0, FAR, ALU.is_equal, ALU.mult))
                st.link(v.scalar_tensor_tensor(out=hit_f[:, f + 1:f + 2], in0=node1[:], scalar=-1.0,
                                               in1=hit_f[:, f:f + 1], op0=ALU.add, op1=ALU.add))
                st.link(v.tensor_copy(idx[:], hit_f[:, f + 1:f + 2]))
            dve.wait_ge(flags_summed, 1)
            st.link(v.tensor_scalar(flag_f[:, 6:7], bank[3][:, 0:1], 1.0, None, ALU.min))
            st.link(v.tensor_copy(flag_i[:], flag_f[:, 6:7]))
            v.tensor_copy(flag_f[:, 7:8], flag_f[:, 6:7]).then_inc(node_ready, 1)
            st.end()

            flag = read_flag(dve)
            with dve.If(flag > 0):
                for u in both:
                    dve.wait_ge(wh_stored[u], 16 * STEPS)
                dense0_vector(dve)

            def row_onehots(st, j, q, ready):
                for u in both:
                    t = 2 * j + u
                    st.link(v.tensor_scalar(row_cmp, iota[:], step_node(j)[:, u, OFFC:OFFC + 1], None, ALU.is_ge))
                    v.scalar_tensor_tensor(out=row_hot[q][:, u, :], in0=iota[:], scalar=end[:, bass.ds(t, 1)],
                                           in1=row_cmp, op0=ALU.is_lt, op1=ALU.mult).then_inc(ready, 1)
                    dve.wait_ge(ready, t + 1)

            def rows(j, q):
                st = Steps(dve, dve_rows, ROWS_TICKS, j)
                row_onehots(st, j, q, rows_ready)
                st.end()

            def indices(j, q):
                st = Steps(dve, dve_idx, IDX_TICKS, j)
                dve.wait_ge(info_ready, j + 1)
                info = edge_info[q]
                st(v.tensor_copy(row_id[:, j, :], info[:, :, ROWC]))
                st.link(v.tensor_tensor(slot_id[:, j, :], edge_pos[:].rearrange("p u c -> p (u c)"), info[:, :, OFFC],
                                        ALU.subtract))
                st.link(v.tensor_tensor(slot_hot[q][:], iota16.unsqueeze(1).to_broadcast([P, EC, SLOTS]),
                                        slot_id[:, j, :].unsqueeze(2).to_broadcast([P, EC, SLOTS]), ALU.is_equal))
                st.link(v.tensor_tensor(nbr_tmp[:], slot_hot[q][:], info[:, :, 0:SLOTS], ALU.mult))
                st.link(v.tensor_reduce(nbr_key[:, 0, :], nbr_tmp[:], X_AXIS, ALU.add))
                st.link(v.tensor_scalar(nbr_key[:, 1, :], nbr_key[:, 0, :], 0.0, FAR, ALU.is_equal, ALU.mult))
                st.link(v.scalar_tensor_tensor(out=nbr_key[:, 2, :], in0=nbr_key[:, 0, :], scalar=-1.0,
                                               in1=nbr_key[:, 1, :], op0=ALU.add, op1=ALU.add))
                v.tensor_copy(edge_idx[q][:], nbr_key[:, 2, :]).then_inc(idx_ready, 1)
                st(v.tensor_copy(idx_all[:, j, :], nbr_key[:, 2, :]))
                st.end()

            def edge_onehots(j, q):
                v.tensor_tensor(edge_hot[q][:], iota_row1.unsqueeze(1).to_broadcast([P, EC, P]),
                                row_id[:, j, :].unsqueeze(2).to_broadcast([P, EC, P]), ALU.is_equal
                                ).then_inc(hot_ready, 1)

            def edge_scores(st, jj, q):
                j = 2 * jj + q
                dst = gath[q][:, 0:EC, D:ROW]
                own = step_src_dst[:, j]
                dve.wait_ge(gath_in[q], 16 * EC * (jj + 1))
                if later(j, 1):
                    dve.wait_ge(slots_summed, j)
                v.tensor_tensor(placed, slot_hot[q][:].unsqueeze(3).to_broadcast([P, EC, SLOTS, HEADS]),
                                dst.unsqueeze(2).to_broadcast([P, EC, SLOTS, HEADS]), ALU.mult
                                ).then_inc(placed_ready, 1)
                st(v.tensor_tensor(edge_e[:, 0, 0:EC, :], dst, edge_info[q][:, :, SRCC:VW], ALU.add))
                st.link(v.tensor_tensor(edge_e[:, 0, EC:GC, :], own[:, :, 0:HEADS], own[:, :, HEADS:], ALU.add))
                return st(v.scalar_tensor_tensor(out=edge_e[:, 1], in0=edge_e[:, 0], scalar=ALPHA, in1=edge_e[:, 0],
                                                 op0=ALU.mult, op1=ALU.max))

            def row_maxima(st, j, q):
                own = step_src_dst[:, j]
                dve.wait_ge(slots_summed, j + 1)
                st.link(v.tensor_tensor(masked, bank[1][:, 0:PAIR * P].rearrange("p (u k h) -> p u k h", u=PAIR, k=SLOTS),
                                        step_bias[:, j, :, 0:SLOTS].unsqueeze(3).to_broadcast([P, PAIR, SLOTS, HEADS]),
                                        ALU.add))
                st.link(v.tensor_reduce(max_tmp[:, 0], masked.rearrange("p u k h -> p u h k"), X_AXIS, ALU.max))
                st.link(v.tensor_tensor(max_tmp[:, 1], max_tmp[:, 0], own[:, :, HEADS:], ALU.max))
                st.link(v.tensor_tensor(max_tmp[:, 2], max_tmp[:, 1], own[:, :, 0:HEADS], ALU.add))
                v.scalar_tensor_tensor(out=row_max[q][:], in0=max_tmp[:, 2], scalar=ALPHA, in1=max_tmp[:, 2],
                                       op0=ALU.mult, op1=ALU.max).then_inc(row_max_ready, 1)

            def exponents(st, j, q):
                dve.wait_ge(row_max_ready, j + 1)
                if later(j, 1):
                    dve.wait_ge(prob_ready, j)
                st(v.tensor_tensor(edge_e[:, 0, EC:GC, :], edge_e[:, 1, EC:GC, :], row_max[q][:], ALU.subtract))
                dve.wait_ge(edge_max_summed, j + 1)
                st.link(v.tensor_tensor(edge_e[:, 0, 0:EC, :], edge_e[:, 1, 0:EC, :],
                                        bank[0][:, EC * VW:EC * (VW + HEADS)].rearrange("p (c h) -> p c h", c=EC),
                                        ALU.subtract))
                v.tensor_scalar(edge_e[:, 2], edge_e[:, 0], 0.0, None, ALU.min).then_inc(exponent_ready, 1)

            def scale(q, parts):
                for c0, c1 in parts:
                    part = gath[q][:, c0:c1, 0:D].rearrange("p c (h d) -> p c h d", h=HEADS)
                    v.tensor_tensor(part, part, prob[q][:, c0:c1, :].unsqueeze(3).to_broadcast([P, c1 - c0, HEADS, DH]),
                                    ALU.mult).then_inc(scaled, 1)

            def normalise(j, u):
                if u == 0:
                    dve.wait_ge(agg_summed, 2 * j + 1)
                    st = Steps(dve, dve_att, ATT_TICKS, j)
                    st.link(v.reciprocal(inv_sum[:].rearrange("p u h -> p (u h)"), bank[1][:, 2 * P:2 * P + 2 * HEADS]))
                    st.end()
                dve.wait_ge(agg_summed, 2 * j + u + 1)
                v.tensor_tensor(att[:, u, :].rearrange("p (h d) -> p h d", h=HEADS),
                                bank[2 + u][:].rearrange("p (h d) -> p h d", h=HEADS),
                                inv_sum[:, u, :].unsqueeze(2).to_broadcast([P, HEADS, DH]), ALU.mult
                                ).then_inc(att_ready, 1)

            def elu(j, u):
                dve.wait_ge(elu_parts, 4 * j + 2 * u + 2)
                v.scalar_tensor_tensor(out=att_exp[:, u, :], in0=att_exp[:, u, :], scalar=1.0, in1=att[:, u, :],
                                       op0=ALU.min, op1=ALU.add).then_inc(enc_ready, 1)

            def add_to_x(j):
                for u in both:
                    dve.wait_ge(mlp_summed, 5 * j + 4 + u)
                    v.tensor_tensor(x_all[:, 2 * j + u, :], bank[7 - u][:], x_all[:, 2 * j + u, :], ALU.add
                                    ).then_inc(x_added, 1)

            def norm_stats(st, j):
                for u in both:
                    alone(x_added, 2 * j + u + 1)
                    st(v.bn_stats(stats[u][:], x_all[:, 2 * j + u, :]))
                at = st.k
                for u in both:
                    alone(st.sem, st.base + at - 1 + u)
                    v.bn_aggr(mean_var[u][:], stats[u][:]).then_inc(var2_ready, 1)

            def norm_scale(st, j):
                for u in both:
                    dve.wait_ge(std2_ready, 2 * j + u + 1)
                    st(v.reciprocal(ln2_scale[:, j, u:u + 1], std[u][:]))
                for u in both:
                    st.after(st.k - 1 + u)
                    v.scalar_tensor_tensor(out=ln2_shift[:, j, u:u + 1], in0=mean_var[u][:, 0:1], scalar=-1.0,
                                           in1=ln2_scale[:, j, u:u + 1], op0=ALU.mult, op1=ALU.mult
                                           ).then_inc(ln2_ready, 1)

            def begin(jj, q):
                st = Steps(dve, dve_edge, EDGE_TICKS, 2 * jj + q)
                edge_scores(st, jj, q)
                row_maxima(st, 2 * jj + q, q)
                exponents(st, 2 * jj + q, q)
                st.end()

            for q in both:
                rows(q, q)
                indices(q, q)
                edge_onehots(q, q)
            begin(0, 0)

            def body(jj, q):
                j = 2 * jj + q
                norm = Steps(dve, dve_norm, NORM_TICKS, j - 2)
                if has(j, 0, STEPS - 1):
                    dve.wait_ge(prob_ready, j + 1)
                    dve.wait_ge(self_in[q], 16 * (jj + 1))
                    scale(q, ((0, 2), (2, CH), (EC, GC)))
                if has(j, 2, STEPS + 1):
                    add_to_x(j - 2)
                if has(j, 0, STEPS - 1):
                    scale(q, ((CH, CH + 2), (CH + 2, EC)))
                if has(j, 0, STEPS - 3):
                    rows(j + 2, q)
                if has(j, 0, STEPS - 1):
                    normalise(j, 0)
                if has(j, 0, STEPS - 3):
                    indices(j + 2, q)
                if has(j, 2, STEPS + 1):
                    norm_stats(norm, j - 2)
                if has(j, 0, STEPS - 1):
                    normalise(j, 1)
                    elu(j, 0)
                if has(j, 0, STEPS - 2):
                    st = Steps(dve, dve_edge, EDGE_TICKS, j + 1)
                    edge_scores(st, jj + q, 1 - q)
                if has(j, 0, STEPS - 3):
                    edge_onehots(j + 2, q)
                if has(j, 0, STEPS - 1):
                    elu(j, 1)
                if has(j, 0, STEPS - 2):
                    row_maxima(st, j + 1, 1 - q)
                if has(j, 2, STEPS + 1):
                    norm_scale(norm, j - 2)
                    norm.end()
                if has(j, 0, STEPS - 2):
                    exponents(st, j + 1, 1 - q)
                    st.end()

            dve.wait_ge(b4_added, TILES)
            edge_pipeline(dve, body)

            def rows1(jj, q, first, st):
                j = 2 * jj + q
                if not first:
                    dve.wait_ge(gath1_in[q], 16 * EC * jj)
                    dve.wait_ge(edge_w_summed, j - 1)
                st.link(v.tensor_copy(edge_idx[q][:], idx_all[:, j, :]))
                v.tensor_tensor(slot_hot[q][:], iota16.unsqueeze(1).to_broadcast([P, EC, SLOTS]),
                                slot_id[:, j, :].unsqueeze(2).to_broadcast([P, EC, SLOTS]), ALU.is_equal
                                ).then_inc(idx1_ready, 1)
                row_onehots(st, j, q, rows1_ready)

            for q in both:
                st = Steps(dve, dve_rows1, ROWS1_TICKS, q)
                rows1(0, q, True, st)
                st.end()
            st = Steps(dve, dve_hit, HIT_TICKS, 0)
            dve.wait_ge(hit_in, 48)
            st.link(v.scalar_tensor_tensor(out=hit_keys[:], in0=hit_keys[:], scalar=hit_obj1[:, 0:1],
                                           in1=iota[:, 1:SLOTS + 1], op0=ALU.is_equal, op1=ALU.mult))
            st.link(v.tensor_reduce(hit_slot[:], hit_keys[:], X_AXIS, ALU.add))
            st(v.tensor_scalar(hit_f[:, 2:3], hit_slot[:], 0.0, float(2 * N * SLOTS), ALU.is_equal, ALU.mult))
            st.link(v.scalar_tensor_tensor(out=hit_f[:, 0:1], in0=hit_f[:, 1:2], scalar=float(SLOTS), in1=hit_slot[:],
                                           op0=ALU.mult, op1=ALU.add))
            st.link(v.scalar_tensor_tensor(out=hit_f[:, 0:1], in0=hit_f[:, 0:1], scalar=-1.0, in1=hit_f[:, 2:3],
                                           op0=ALU.add, op1=ALU.add))
            st(v.tensor_copy(hit_dst[:], hit_f[:, 0:1]))
            dve.wait_ge(hit_proj, 1)
            st(v.tensor_tensor(hit_q, bank[6][:], bq_row[:], ALU.add))
            dve.wait_ge(hit_proj, 2)
            st.link(v.tensor_tensor(hit_k, bank[7][:], bk_row[:], ALU.add))
            st.link(v.tensor_tensor(hit_q, hit_q, hit_k, ALU.mult))
            st.link(v.tensor_reduce(hit_tmp[:], hit_q.rearrange("p (h d) -> p h d", h=HEADS), X_AXIS, ALU.add))
            v.tensor_scalar(hit_att[:], hit_tmp[:], DH ** -0.5, None, ALU.mult).then_inc(hit_att_ready, 1)
            st.end()

            def softmax(jj, q, first):
                j = 2 * jj + q
                st = Steps(dve, dve_soft, SOFT_TICKS, j)
                dve.wait_ge(score_in_sem[q], 16 * (jj + 1))
                st(v.tensor_tensor(soft[:, :, 0:SLOTS, :], score_in[q].rearrange("p u (k h) -> p u k h", k=SLOTS),
                                   step_bias[:, j, :, 0:SLOTS].unsqueeze(3).to_broadcast([P, PAIR, SLOTS, HEADS]),
                                   ALU.add))
                st.link(v.memset(soft[:, :, SLOTS, :], SELF_SCORE))
                by_slot = soft.rearrange("p u k h -> p u h k")
                over_slots = [P, PAIR, SLOTS + 1, HEADS]
                st.link(v.tensor_reduce(soft_max, by_slot, X_AXIS, ALU.max))
                v.tensor_tensor(soft, soft, soft_max.unsqueeze(2).to_broadcast(over_slots), ALU.subtract
                                ).then_inc(soft_ready, 1)
                dve.wait_ge(soft_exp, j + 1)
                st.link(v.tensor_reduce(soft_sum, by_slot, X_AXIS, ALU.add))
                st.link(v.reciprocal(soft_sum, soft_sum))
                st.link(v.tensor_tensor(soft, soft, soft_sum.unsqueeze(2).to_broadcast(over_slots), ALU.mult))
                if not first:
                    dve.wait_ge(edge_w_summed, j - 1)
                    dve.wait_ge(own_made, 2 * j - 2)
                st.link(v.tensor_reduce(weight[q][:], soft, X_AXIS, ALU.add))
                v.tensor_scalar(weight[q][:], weight[q][:], 1.0 / HEADS, None, ALU.mult).then_inc(weight_ready, 1)
                dve.wait_ge(weight_ready, j + 1)
                own = weight[q][:, :, SLOTS]
                st(v.tensor_tensor(own_scale[:, q, :], ln2_scale[:, j, :], own, ALU.mult))
                v.tensor_tensor(own_shift[:, q, :], ln2_shift[:, j, :], own, ALU.mult).then_inc(own_ready, 1)
                st.end()

            def weighted_onehots(jj, q):
                j = 2 * jj + q
                st = Steps(dve, dve_edge1, EDGE1_TICKS, j)
                dve.wait_ge(edge_w_summed, j + 1)
                st.link(v.tensor_tensor(nbr_tmp[:], slot_hot[q][:],
                                        bank[0][:, 0:EC * SLOTS].rearrange("p (c k) -> p c k", c=EC), ALU.mult))
                st.link(v.tensor_reduce(edge_w[:], nbr_tmp[:], X_AXIS, ALU.add))
                if later(j, 2):
                    dve.wait_ge(agg1_summed, 2 * j - 2)
                for n in range(EC):
                    last = v.tensor_scalar(edge_hot[q][:, n, :], iota_row1, row_id[:, j, n:n + 1], edge_w[:, n:n + 1],
                                           ALU.is_equal, ALU.mult)
                    if n < EC - 1:
                        st(last)
                last.then_inc(hot1_ready, 1)
                dve.wait_ge(hot1_ready, j + 1)
                st.end()

            def outputs(jj, q):
                j = 2 * jj + q
                for u in both:
                    dve.wait_ge(agg1_summed, 2 * j + u + 1)
                    if later(j, 2):
                        dve.wait_ge(out_stored[2 * q + u], 16 * jj)
                    v.tensor_tensor(out_sb[q][:, u, :], bank[2 + 2 * q + u][:], x_all[:, 2 * j + u, :], ALU.add
                                    ).then_inc(out_added, 1)
                for u in both:
                    dve.wait_ge(own_made, 2 * j + u + 1)
                    dve.wait_ge(out_added, 2 * j + u + 1)
                    v.tensor_tensor(out_sb[q][:, u, :], out_sb[q][:, u, :], gath[q][:, EC + u, 0:D], ALU.add
                                    ).then_inc(out_ready, 1)

            def late(jj, q, following=2):
                if following >= 1:
                    weighted_onehots(jj + q, 1 - q)
                if following >= 2:
                    st = Steps(dve, dve_rows1, ROWS1_TICKS, 2 * jj + q + 2)
                    rows1(jj + 1, q, False, st)
                    st.end()
                    softmax(jj + 1, q, False)
                outputs(jj, q)

            softmax(0, 0, True)
            softmax(0, 1, True)
            weighted_onehots(0, 0)
            for q in both:
                late(0, q)
            with dve.Fori(1, STEPS // 2 - 1) as jj:
                for q in both:
                    late(jj, q)
            late(STEPS // 2 - 1, 0, 1)
            late(STEPS // 2 - 1, 1, 0)
            for stored in out_stored:
                dve.wait_ge(stored, 8 * STEPS)
            with dve.If(flag > 0):
                dense1_vector(dve)


def kernel(**inputs):
    import numpy as _np
    import concourse.bacc as _bacc
    from concourse import mybir as _mybir
    from concourse.bass_utils import run_bass_kernel_spmd as _run

    def host(name):
        return _np.asarray(inputs[name])

    laid_out = {
        "x": host("x"),
        "adj": host("adj"),
        "w0": host("L0_gnn_W").transpose(1, 0, 2).reshape(D, D),
        "a1": host("L0_gnn_a1").reshape(D),
        "a2": host("L0_gnn_a2").reshape(D),
        "w1t": host("L0_gnn_W1").T,
        "b1": host("L0_gnn_b1").reshape(-1, P).T,
        "w2t": host("L0_gnn_W2").T,
        "b2": host("L0_gnn_b2").reshape(-1, P).T,
        "w3t": host("L0_gnn_W3").T,
        "b3": host("L0_gnn_b3").reshape(-1, P).T,
        "w4t": host("L0_gnn_W4").T,
        "b4": host("L0_gnn_b4"),
        "pairs": host("L1_gnn_rel_pair_index"),
        "wqt": host("L1_gnn_Wq").T,
        "bq": host("L1_gnn_bq"),
        "wkt": host("L1_gnn_Wk").T,
        "bk": host("L1_gnn_bk"),
    }
    nc = _bacc.Bacc("TRN2", target_bir_lowering=False, num_devices=1)
    arrays, args = {}, []
    for name, a in laid_out.items():
        a = _np.ascontiguousarray(a)
        arrays[f"in_{name}_dram"] = a
        args.append(nc.dram_tensor(f"in_{name}_dram", a.shape, _mybir.dt.from_np(a.dtype), kind="ExternalInput").ap())
    out = nc.dram_tensor("out_dram", (N, D), F32, kind="ExternalOutput").ap()
    gnn_kernel(nc, *args, out)
    r = _run(nc, [arrays], core_ids=[0])
    return r.results[0]["out_dram"]
```

```python
from contextlib import ExitStack

import concourse.bass as bass
from concourse import mybir
from concourse.alu_op_type import AluOpType as ALU

ACT = mybir.ActivationFunctionType
F32 = mybir.dt.float32
F32R = mybir.dt.float32r
I32 = mybir.dt.int32
U32 = mybir.dt.uint32
X_AXIS = mybir.AxisListType.X

P = 128
N = 4096
D = 512
TILES = N // P
HEADS = 8
DH = D // HEADS
KC = D // P
SEG = 8
SEGW = N // SEG
SEGP = SEGW + 8
SLOTS = 16
CH = 5
EDGES = CH * P
BUFS = 4
PAIR = 2
STEPS = TILES // PAIR
EC = PAIR * CH
GC = EC + PAIR
ROW = D + HEADS
NPAIR = 10000
PP = 125
PCOL = NPAIR // PP
PG = 8
B4_TILES = 3
VW = SLOTS + 2 + 2 * HEADS
OFFC, ROWC, SRCC = SLOTS, SLOTS + 1, SLOTS + 2
FAR = 5000.0
NEGBIG = 1.0e30
ALPHA = 0.2
EPS = 1e-5
START_TICKS, FRONT_TICKS, NBR_TICKS, MID_TICKS, IDX_TICKS, EDGE_TICKS = 26, 9, 8, 49, 8, 15
ATT_TICKS, NORM_TICKS, ROWS1_TICKS, HIT_TICKS, SOFT_TICKS, EDGE1_TICKS = 3, 4, 1, 10, 7, 2
ARENA = 22720
SELF_SCORE = 1e-7


class Steps:

    def __init__(self, eng, sem, per, run):
        self.eng, self.sem, self.base, self.per, self.k = eng, sem, run * per, per, 0

    def __call__(self, instruction):
        instruction.then_inc(self.sem, 1)
        self.k += 1
        return self.k

    def after(self, k):
        self.eng.wait_ge(self.sem, self.base + k)

    def link(self, instruction):
        self.after(self(instruction))

    def end(self):
        assert self.k == self.per, (self.k, self.per)


def later(j, n):
    return not isinstance(j, int) or j >= n


def lone_wait(eng, met, sem, value):
    if not isinstance(value, int):
        eng.compute_val(value)
    eng.wait_ge(met, 1)
    eng.wait_ge(sem, value)


def gnn_kernel(nc, x, adj, w0, a1, a2, w1t, b1, w2t, b2, w3t, b3, w4t, b4, pairs, wqt, bq, wkt, bk, out):
    table0 = nc.dram_tensor("table0", [N, ROW], F32, kind="Internal").ap()
    table1 = nc.dram_tensor("table1", [N, D], F32, kind="Internal").ap()
    keys_dram = nc.dram_tensor("keys_dram", [N, SLOTS], F32, kind="Internal").ap()
    score_dram = nc.dram_tensor("score_dram", [N * SLOTS, HEADS], F32, kind="Internal").ap()

    adj_flat = adj.rearrange("n m -> (n m)").unsqueeze(1)
    adj_rows = adj.rearrange("n (s c) -> n s c", s=SEG)
    score_rows = score_dram.rearrange("(n k) h -> n (k h)", k=SLOTS)

    with ExitStack() as ctx:
        def sb(name, shape, dt=F32):
            return ctx.enter_context(nc.sbuf_tensor(name, shape, dt))

        def sem(name):
            return ctx.enter_context(nc.semaphore(name))

        iota = sb("iota", [P, EDGES])
        ident = sb("ident", [P, P])
        before = sb("before", [P, P])
        ones = sb("ones", [P, P])
        zeros = sb("zeros", [P, D])
        seg_base = sb("seg_base", [P, SEG, 8])
        self_key = sb("self_key", [P, TILES])
        edge_pos = sb("edge_pos", [P, PAIR, CH])
        iota16 = iota[:, 0:SLOTS]
        iota_row1 = iota[:, 1:P + 1]

        a_fold = sb("a_fold", [P, KC, 2 * HEADS])
        w1_sb = sb("w1_sb", [P, 4, 256])
        w2_sb = sb("w2_sb", [P, 2, 128])
        w3_sb = sb("w3_sb", [P, 256])
        w4_sb = sb("w4_sb", [P, 2, D])
        b1_sb = sb("b1_sb", [P, 2])
        b2_sb = sb("b2_sb", [P, 1])
        b3_sb = sb("b3_sb", [P, 2])
        b4_row = sb("b4_row", [P, D])

        x_all = sb("x_all", [P, TILES, D])
        node = sb("node", [P, TILES, VW])
        src_dst = sb("src_dst", [P, TILES, 2 * HEADS])
        seg_last = sb("seg_last", [P, TILES, SEG])
        neg_centre = sb("neg_centre", [P, TILES])
        half_count = sb("half_count", [P, TILES])
        count = sb("count", [P, TILES])
        slot_bias = sb("slot_bias", [P, TILES, SLOTS + 1])
        row_id = sb("row_id", [P, STEPS, EC])
        slot_id = sb("slot_id", [P, STEPS, EC])
        idx_all = sb("idx_all", [P, STEPS, EC], U32)

        arena = sb("arena", [P, ARENA])

        def carver():
            at = [0]

            def carve(shape, dt=F32):
                size = 1
                for n in shape:
                    size *= n
                view = arena[:, at[0]:at[0] + size]
                at[0] += size
                assert at[0] <= ARENA, at[0]
                names = "abc"[:len(shape)]
                if dt is not F32:
                    view = view.bitcast(dt)
                if len(shape) == 1:
                    return view
                return view.rearrange(f"p ({' '.join(names)}) -> p {' '.join(names)}", **dict(zip(names, shape)))

            return carve

        both = range(2)
        bufs = range(BUFS)
        front = carver()
        adj_sb = [front([SEG, SEGP]) for b in bufs]
        ones8 = sb("ones8", [P, 8])
        found = [front([SEG, 8], U32) for u in both]
        key_raw = [front([SEG, 8]) for u in both]
        key_any = [front([SEG, 8]) for u in both]
        key_nbr = [front([SEG * 8]) for u in both]
        key_left = [front([SEG * 8]) for u in both]
        key16 = [sb(f"key16{u}", [P, SLOTS]) for u in both]
        stats = [sb(f"stats{u}", [P, 6]) for u in both]
        mean_var = [sb(f"mean_var{u}", [P, 2]) for u in both]
        ln_scale = [sb(f"ln_scale{u}", [P, 1]) for u in both]
        ln_shift = [sb(f"ln_shift{u}", [P, 1]) for u in both]
        w0_sb = front([KC, D])
        h_sb = [front([D]) for u in both]
        hT = [front([KC, P]) for u in both]
        wh_row = [front([ROW]) for u in both]
        folding = carver()
        folding([BUFS * SEG * SEGP + 2 * 5 * SEG * 8 + KC * D])
        a_rows = folding([2, D])
        fold_tmp = folding([D])

        pair_sb = sb("pair_sb", [PP, PCOL, 2], I32)
        pair_flat = sb("pair_flat", [PP, PCOL])
        pair_ne = sb("pair_ne", [PP, PCOL])
        pair_idx = sb("pair_idx", [PP, PCOL], U32)
        idx8 = sb("idx8", [PP, PG], U32)
        adj8 = sb("adj8", [PP, PG])
        pair_adj = sb("pair_adj", [PP, PCOL])
        hit_key = sb("hit_key", [P, PCOL])
        hit8 = sb("hit8", [P, 8])
        hit_valid = sb("hit_valid", [P, 8])
        hit8_m1 = sb("hit8_m1", [P, 8], I32)
        hit_sub_i = sb("hit_sub_i", [P, 8], I32)
        hit_obj_i = sb("hit_obj_i", [P, 8], I32)
        hit_node = sb("hit_node", [P, 17])
        hit_end = sb("hit_end", [P, 2])
        hit_rows = sb("hit_rows", [P, P])
        hit_cmp = sb("hit_cmp", [P, P])
        hit_e = sb("hit_e", [P, 17])
        hit_slot = sb("hit_slot", [P, 1])
        hit_sel = sb("hit_sel", [P, 8])
        hit_tmp = sb("hit_tmp", [P, 8])
        hit_sub1 = sb("hit_sub1", [P, 1])
        hit_obj1 = sb("hit_obj1", [P, 1])
        hit_f = sb("hit_f", [P, 4])
        hit_sub = sb("hit_sub", [P, 1], U32)
        hit_obj = sb("hit_obj", [P, 1], U32)
        hit_dst = sb("hit_dst", [P, 1], U32)
        hit_keys = sb("hit_keys", [P, SLOTS])
        hit_att = sb("hit_att", [P, HEADS])
        flag_f = sb("flag_f", [P, 8])
        flag_i = sb("flag_i", [P, 1], I32)
        diag = sb("diag", [P, TILES])

        edge = carver()
        gath = [edge([GC, ROW]) for q in both]
        edge_hot = [edge([EC, P]) for q in both]
        edge_info = [sb(f"edge_info{q}", [P, EC, VW]) for q in both]
        slot_hot = [sb(f"slot_hot{q}", [P, EC, SLOTS]) for q in both]
        nbr_tmp = sb("nbr_tmp", [P, EC, SLOTS])
        nbr_key = sb("nbr_key", [P, 3, EC])
        edge_idx = [sb(f"edge_idx{q}", [P, EC], U32) for q in both]
        row_hot = [sb(f"row_hot{q}", [P, PAIR, EDGES]) for q in both]
        placed = edge([EC, SLOTS, HEADS])
        masked = edge([PAIR, SLOTS, HEADS])
        row_max_parts = [sb(f"row_max_parts{q}", [P, PAIR, 2 * HEADS]) for q in both]
        row_max = [sb(f"row_max{q}", [P, PAIR, HEADS]) for q in both]
        max_tmp = sb("max_tmp", [P, 3, PAIR, HEADS])
        edge_e = sb("edge_e", [P, 3, GC, HEADS])
        prob = [sb(f"prob{q}", [P, GC, HEADS]) for q in both]
        slot_sum = sb("slot_sum", [P, PAIR, HEADS])
        own_prob = sb("own_prob", [P, PAIR, HEADS])
        inv_sum = sb("inv_sum", [P, PAIR, HEADS])
        att = edge([PAIR, D])
        att_exp = edge([PAIR, D])
        h2_sb = edge([PAIR, D])
        encT = edge([KC, PAIR * P])
        z1 = edge([2, PAIR * P])
        z2 = edge([PAIR * P])
        z3 = z1

        late = carver()
        late([2 * GC * ROW + 2 * PAIR * EDGES])
        wq_sb = late([KC, D])
        wk_sb = late([KC, D])
        hit_h = [late([D]) for s in both]
        hit_hT = [late([KC, P]) for s in both]
        hit_q = late([D])
        hit_k = hit_h[0]
        bq_row, bk_row = b4_row, zeros
        w1_flat = w1_sb[:].rearrange("p a b -> p (a b)")
        score_in = [w1_flat[:, 256 * q:256 * (q + 1)].rearrange("p (u c) -> p u c", u=PAIR) for q in both]
        soft = w1_flat[:, 512:784].rearrange("p (u k h) -> p u k h", u=PAIR, h=HEADS)
        soft_max = max_tmp[:, 0]
        soft_sum = max_tmp[:, 1]
        weight = [sb(f"weight{q}", [P, PAIR, SLOTS + 1]) for q in both]
        edge_w = sb("edge_w", [P, EC])
        out_sb = [att, att_exp]
        ln2_scale = sb("ln2_scale", [P, STEPS, PAIR])
        ln2_shift = sb("ln2_shift", [P, STEPS, PAIR])
        own_scale = sb("own_scale", [P, 2, PAIR])
        own_shift = sb("own_shift", [P, 2, PAIR])
        bank = [ctx.enter_context(nc.psum_tensor(f"bank{i}", [P, 512], F32)) for i in range(8)]

        consts_made = sem("consts_made")
        weights0_in = sem("weights0_in")
        weights1_in = sem("weights1_in")
        weights2_in = sem("weights2_in")
        adj_in = [sem(f"adj_in{b}") for b in bufs]
        x_in = [sem(f"x_in{b}") for b in bufs]
        adj_searched = sem("adj_searched")
        dve_start = sem("dve_start")
        dve_front = sem("dve_front")
        dve_nbr = sem("dve_nbr")
        fold_ready = sem("fold_ready")
        ln_ready = sem("ln_ready")
        h_made = sem("h_made")
        h_turned = sem("h_turned")
        hT_ready = sem("hT_ready")
        wh_summed = sem("wh_summed")
        wh_copied = sem("wh_copied")
        wh_stored = [sem(f"wh_stored{u}") for u in both]
        b4_added = sem("b4_added")
        pair_in = sem("pair_in")
        pairs_ready = sem("pairs_ready")
        pool_pair = sem("pool_pair")
        pair_adj_in = sem("pair_adj_in")
        diag_in = sem("diag_in")
        dve_mid = sem("dve_mid")
        counts_ready = sem("counts_ready")
        offsets_summed = sem("offsets_summed")
        node_ready = sem("node_ready")
        flags_ready = sem("flags_ready")
        flags_summed = sem("flags_summed")
        hit_rows_ready = sem("hit_rows_ready")
        hit_summed = sem("hit_summed")
        keys_stored = sem("keys_stored")
        score_zeroed = sem("score_zeroed")
        distance_ready = sem("distance_ready")
        rows_ready = sem("rows_ready")
        info_summed = sem("info_summed")
        info_ready = sem("info_ready")
        idx_ready = sem("idx_ready")
        hot_ready = sem("hot_ready")
        gath_in = [sem(f"gath_in{q}") for q in both]
        self_in = [sem(f"self_in{q}") for q in both]
        dve_edge = sem("dve_edge")
        placed_ready = sem("placed_ready")
        slots_summed = sem("slots_summed")
        row_max_ready = sem("row_max_ready")
        edge_max_summed = sem("edge_max_summed")
        exponent_ready = sem("exponent_ready")
        prob_ready = sem("prob_ready")
        slot_exponent_ready = sem("slot_exponent_ready")
        slot_exp_ready = sem("slot_exp_ready")
        scaled = sem("scaled")
        own_prob_ready = sem("own_prob_ready")
        own_scaled = sem("own_scaled")
        own_added = sem("own_added")
        agg_summed = sem("agg_summed")
        att_ready = sem("att_ready")
        dve_idx = sem("dve_idx")
        dve_att = sem("dve_att")
        x_added = sem("x_added")
        own_ready = sem("own_ready")
        own_made = sem("own_made")
        out_added = sem("out_added")
        dve_norm = sem("dve_norm")
        elu_parts = sem("elu_parts")
        enc_ready = sem("enc_ready")
        enc_turned = sem("enc_turned")
        encT_ready = sem("encT_ready")
        mlp_summed = sem("mlp_summed")
        mlp_relu = sem("mlp_relu")
        ln2_ready = sem("ln2_ready")
        h2_made = sem("h2_made")
        h2_stored = [sem(f"h2_stored{u}") for u in both]
        hit_in = sem("hit_in")
        hit_turned = sem("hit_turned")
        hit_hT_ready = sem("hit_hT_ready")
        hit_proj = sem("hit_proj")
        dve_hit = sem("dve_hit")
        hit_att_ready = sem("hit_att_ready")
        hit_stored = sem("hit_stored")
        late_in = sem("late_in")
        dve_rows1 = sem("dve_rows1")
        idx1_ready = sem("idx1_ready")
        gath1_in = [sem(f"gath1_in{q}") for q in both]
        score_in_sem = [sem(f"score_in{q}") for q in both]
        dve_soft = sem("dve_soft")
        soft_ready = sem("soft_ready")
        soft_exp = sem("soft_exp")
        weight_ready = sem("weight_ready")
        edge_w_summed = sem("edge_w_summed")
        dve_edge1 = sem("dve_edge1")
        edge_w_ready = sem("edge_w_ready")
        hot1_ready = sem("hot1_ready")
        agg1_summed = sem("agg1_summed")
        out_ready = sem("out_ready")
        out_stored = [sem(f"out_stored{n}") for n in range(4)]

        neg_one = sb("neg_one", [P, 1])
        eps_col = sb("eps_col", [P, 1])
        std = [sb(f"std{u}", [P, 1]) for u in both]
        var_ready = sem("var_ready")
        std_ready = sem("std_ready")
        var2_ready = sem("var2_ready")
        std2_ready = sem("std2_ready")
        N_CONSTS = 10
        x_rows = x.rearrange("(t p) d -> t p d", p=P)
        out_rows = out.rearrange("(t p) d -> t p d", p=P)
        adj_tiles = adj_rows.rearrange("(t p) s c -> t p s c", p=P)
        table0_rows = table0.rearrange("(t p) d -> t p d", p=P)
        table0_steps = table0.rearrange("(j u p) d -> j p u d", u=PAIR, p=P)
        table1_rows = table1.rearrange("(t p) d -> t p d", p=P)
        score_steps = score_rows.rearrange("(j u p) c -> j p u c", u=PAIR, p=P)
        step_bias = slot_bias[:].rearrange("p (j u) k -> p j u k", u=PAIR)
        step_src_dst = src_dst[:].rearrange("p (j u) c -> p j u c", u=PAIR)

        def step_node(j):
            return node[:].rearrange("p (j u) v -> p j u v", u=PAIR)[:, j]

        def front_slots(eng, slot):
            for b in bufs:
                slot(0, b)
            with eng.Fori(1, TILES // BUFS) as i:
                for b in bufs:
                    slot(i, b)

        def edge_pipeline(eng, body):
            for j in range(2):
                body(j // 2, j % 2)
            with eng.Fori(1, STEPS // 2 - 1) as jj:
                for q in both:
                    body(jj, q)
            for j in range(STEPS - 2, STEPS + 2):
                body(j // 2, j % 2)

        def has(j, low, high):
            return not isinstance(j, int) or low <= j <= high


        wide = carver()
        d_whole = [wide([N]) for _ in range(4)]
        d_score, d_adj, d_turned, d_dst = d_whole
        d_head = wide([TILES, DH])
        d_diag = wide([KC, P])
        d_out = wide([D])
        d_agg = d_dst
        d_pair_att = wide([PCOL, HEADS])
        d_pair_att_flat = d_pair_att.rearrange("p c h -> p (c h)")
        d_h2 = arena[:, 2 * N:4 * N].rearrange("p (j d) -> p j d", d=D)
        half = TILES // 2
        d_weight = [arena[:, 0:KC * D].rearrange("p (k n) -> p k n", k=KC),
                    arena[:, KC * D:2 * KC * D].rearrange("p (k n) -> p k n", k=KC)]
        d_pair_h = [arena[0:PP, N + n * D:N + (n + 1) * D] for n in both]
        d_pair_hT = [arena[:, N + (2 + n) * D:N + (3 + n) * D].rearrange("p (k n) -> p k n", k=KC) for n in both]
        d_pair_q = [arena[0:PP, N + (4 + n) * D:N + (5 + n) * D] for n in both]
        d_bias = [arena[:, N + (6 + n) * D:N + (7 + n) * D] for n in both]
        d_max = sb("d_max", [P, 2])
        d_sum = sb("d_sum", [P, 2])
        d_idx = sb("d_idx", [PP, 2], U32)
        d_val = sb("d_val", [PP, 1])
        off_diag, on_diag = w1_flat[:, 0:P], w1_flat[:, P:2 * P]
        att_dram = nc.dram_tensor("att_dram", [N, D], F32, kind="Internal").ap()
        full_dram = nc.dram_tensor("full_dram", [N, N], F32, kind="Internal").ap()
        agg_dram = nc.dram_tensor("agg_dram", [N, N], F32, kind="Internal").ap()
        full_flat = full_dram.rearrange("n m -> (n m)").unsqueeze(1)
        full_rows = full_dram.rearrange("(t p) m -> t p m", p=P)
        agg_rows = agg_dram.rearrange("(t p) m -> t p m", p=P)
        whole_rows = adj.rearrange("(t p) m -> t p m", p=P)
        att_rows = att_dram.rearrange("(t p) d -> t p d", p=P)
        att_steps = att_dram.rearrange("(j u p) d -> j p u d", u=PAIR, p=P)
        table0_heads = table0.rearrange("(t p) c -> p t c", p=P)
        table1_halves = table1.rearrange("(g t p) d -> g p t d", g=2, p=P)

        g_head_in = sem("g_head_in")
        g_diag_ready = sem("g_diag_ready")
        g_dst_summed = sem("g_dst_summed")
        g_dst_ready = sem("g_dst_ready")
        g_adj_in = sem("g_adj_in")
        g_dve = sem("g_dve")
        g_max_ready = sem("g_max_ready")
        g_exp_ready = sem("g_exp_ready")
        g_turned = sem("g_turned")
        g_turned_ready = sem("g_turned_ready")
        g_summed = sem("g_summed")
        g_out_ready = sem("g_out_ready")
        g_stored = sem("g_stored")
        g_att_in = sem("g_att_in")
        e_weights_in = sem("e_weights_in")
        e_rows_in = sem("e_rows_in")
        e_turned = sem("e_turned")
        e_turned_ready = sem("e_turned_ready")
        e_proj = sem("e_proj")
        e_pair_dve = sem("e_pair_dve")
        e_pair_ready = sem("e_pair_ready")
        e_zero_ready = sem("e_zero_ready")
        e_zeroed = sem("e_zeroed")
        e_agg_zeroed = sem("e_agg_zeroed")
        e_pool = sem("e_pool")
        e_final = sem("e_final")
        e_scattered = sem("e_scattered")
        e_in = sem("e_in")
        e_dve = sem("e_dve")
        e_max_ready = sem("e_max_ready")
        e_exp_ready = sem("e_exp_ready")
        e_agg_ready = sem("e_agg_ready")
        e_agg_stored = sem("e_agg_stored")
        e_agg_in = sem("e_agg_in")
        e_agg_turned = sem("e_agg_turned")
        e_aggT_ready = sem("e_aggT_ready")
        e_half_in = sem("e_half_in")
        e_summed = sem("e_summed")
        e_out_ready = sem("e_out_ready")
        e_out_stored = sem("e_out_stored")

        def read_flag(eng):
            eng.wait_ge(node_ready, 1)
            return eng.value_load(flag_i[0:1, 0:1], min_val=0, max_val=1)

        def dense0_sync(sp):
            with sp.Fori(0, HEADS) as h:
                sp.dma_start(d_head, table0_heads[:, :, bass.ds(h * DH, DH)]).then_inc(g_head_in, 16)
                with sp.Fori(0, TILES) as t:
                    n = h * TILES + t
                    sp.dma_start(d_adj, whole_rows[t]).then_inc(g_adj_in, 16)
                    sp.wait_ge(g_out_ready, n + 1)
                    sp.dma_start(att_rows[t][:, bass.ds(h * DH, DH)], d_out[:, 0:DH]).then_inc(g_stored, 16)
                    lone_wait(sp, node_ready, g_stored, 16 * (n + 1))

        def dense0_vector(dve):
            v = nc.vector
            with dve.Fori(0, HEADS) as h:
                with dve.Fori(0, TILES // KC) as c:
                    m = h * (TILES // KC) + c
                    v.tensor_tensor(d_diag, ident[:].unsqueeze(1).to_broadcast([P, KC, P]),
                                    src_dst[:].rearrange("p (c k) s -> p c k s", k=KC)[:, c, :, bass.ds(h + HEADS, 1)]
                                    .to_broadcast([P, KC, P]), ALU.mult).then_inc(g_diag_ready, 1)
                    dve.wait_ge(g_dst_summed, m + 1)
                    v.tensor_copy(d_dst.rearrange("p (c n) -> p c n", n=D)[:, c, :], bank[0][:]).then_inc(g_dst_ready, 1)
                    dve.wait_ge(g_dst_ready, m + 1)
                with dve.Fori(0, TILES) as t:
                    n = h * TILES + t
                    st = Steps(dve, g_dve, 10, n)
                    st.link(v.tensor_scalar(d_score, d_dst,
                                            src_dst[:].rearrange("p t s -> p (t s)")[:, bass.ds(t * 2 * HEADS + h, 1)],
                                            None, ALU.add))
                    st.link(v.scalar_tensor_tensor(out=d_score, in0=d_score, scalar=ALPHA, in1=d_score,
                                                   op0=ALU.mult, op1=ALU.max))
                    dve.wait_ge(g_adj_in, 16 * (n + 1))
                    st.link(v.tensor_scalar(d_adj, d_adj, 0.0, None, ALU.is_gt))
                    st.link(v.tensor_tensor(d_score, d_score, d_adj, ALU.mult))
                    st.link(v.tensor_scalar(d_adj, d_adj, 1.0, 9.0e15, ALU.subtract, ALU.mult))
                    st.link(v.tensor_tensor(d_score, d_score, d_adj, ALU.add))
                    st.link(v.tensor_reduce(d_max[:, 0:1], d_score, X_AXIS, ALU.max))
                    v.tensor_scalar(d_max[:, 1:2], d_max[:, 0:1], -1.0, None, ALU.mult).then_inc(g_max_ready, 1)
                    dve.wait_ge(g_exp_ready, n + 1)
                    st.link(v.reciprocal(d_sum[:, 1:2], d_sum[:, 0:1]))
                    dve.wait_ge(g_turned, n + 1)
                    for b in range(8):
                        last = v.tensor_copy(d_turned[:, b * D:(b + 1) * D], bank[b][:])
                        if b == 0:
                            st(last)
                    last.then_inc(g_turned_ready, 1)
                    dve.wait_ge(g_summed, n + 1)
                    v.tensor_scalar(d_out[:, 0:DH], bank[0][:, 0:DH], d_sum[:, 1:2], None, ALU.mult
                                    ).then_inc(g_out_ready, 1)
                    dve.wait_ge(g_stored, 16 * (n + 1))
                    st(v.tensor_copy(d_sum[:, 0:1], d_sum[:, 1:2]))
                    st.end()

        def dense0_scalar(act):
            with act.Fori(0, HEADS * TILES) as n:
                act.wait_ge(g_max_ready, n + 1)
                nc.scalar.activation(d_score, d_score, ACT.Exp, bias=d_max[:, 1:2], accum_out=d_sum[:, 0:1]
                                     ).then_inc(g_exp_ready, 1)

        def dense0_tensor(pe):
            with pe.Fori(0, HEADS) as h:
                with pe.Fori(0, TILES // KC) as c:
                    pe.wait_ge(g_diag_ready, h * (TILES // KC) + c + 1)
                    nc.tensor.matmul(bank[0][:], ones[:], d_diag.rearrange("p k n -> p (k n)"), start=True, stop=True
                                     ).then_inc(g_dst_summed, 1)
                with pe.Fori(0, TILES) as t:
                    n = h * TILES + t
                    pe.wait_ge(g_exp_ready, n + 1)
                    for b in range(TILES):
                        last = nc.tensor.transpose(bank[b // KC][:, b % KC * P:(b % KC + 1) * P],
                                                   d_score[:, b * P:(b + 1) * P], ident[:])
                    last.then_inc(g_turned, 1)
                    pe.wait_ge(g_head_in, 16 * (h + 1))
                    pe.wait_ge(g_turned_ready, n + 1)
                    for b in range(TILES):
                        last = nc.tensor.matmul(bank[0][:, 0:DH], d_turned[:, b * P:(b + 1) * P], d_head[:, b, :],
                                                start=(b == 0), stop=(b == TILES - 1))
                    last.then_inc(g_summed, 1)

        def dense1_sync(sp):
            for dst, src in ((d_weight[0], wqt.rearrange("(k p) n -> p k n", p=P)),
                             (d_weight[1], wkt.rearrange("(k p) n -> p k n", p=P)),
                             (d_bias[0], bq.partition_broadcast(P)), (d_bias[1], bk.partition_broadcast(P))):
                sp.dma_start(dst, src).then_inc(e_weights_in, 16)
            sp.wait_ge(e_zero_ready, 1)
            with sp.Fori(0, TILES) as t:
                for c in range(N // D):
                    sp.dma_start(agg_rows[t][:, c * D:(c + 1) * D], d_out).then_inc(e_agg_zeroed, 16)
            sp.wait_ge(e_agg_zeroed, 16 * 8 * TILES)
            with sp.Fori(0, HEADS) as h:
                with sp.Fori(0, TILES) as t:
                    for c in range(N // D):
                        sp.dma_start(full_rows[t][:, c * D:(c + 1) * D], d_out).then_inc(e_zeroed, 16)
                    lone_wait(sp, node_ready, e_zeroed, 16 * 8 * (h * TILES + t + 1))
                with sp.Fori(0, TILES) as t:
                    n = h * TILES + t
                    sp.wait_ge(e_scattered, 16 * PCOL * (h + 1))
                    sp.dma_start(d_score, full_rows[t]).then_inc(e_in, 16)
                    sp.dma_start(d_adj, whole_rows[t]).then_inc(e_in, 16)
                    sp.dma_start(d_agg, agg_rows[t]).then_inc(e_in, 16)
                    sp.wait_ge(e_agg_ready, n + 1)
                    sp.dma_start(agg_rows[t], d_agg).then_inc(e_agg_stored, 16)
                    lone_wait(sp, node_ready, e_agg_stored, 16 * (n + 1))
            with sp.Fori(0, TILES) as t:
                sp.dma_start(d_score, agg_rows[t]).then_inc(e_agg_in, 16)
                for g in both:
                    if g == 1:
                        sp.wait_ge(e_summed, 2 * t + 1)
                    sp.dma_start(d_h2, table1_halves[g]).then_inc(e_half_in, 16)
                sp.wait_ge(e_out_ready, t + 1)
                sp.dma_start(out_rows[t], d_out).then_inc(e_out_stored, 16)
                lone_wait(sp, node_ready, e_out_stored, 16 * (t + 1))

        def dense1_gpsimd(pool):
            g = nc.gpsimd
            with pool.Fori(0, PCOL) as c:
                g.tensor_copy(d_idx[:], pair_sb[:, c, :]).then_inc(e_pool, 1)
                lone_wait(pool, pairs_ready, e_pool, c + 1)
                for n in both:
                    g.indirect_dma_start(d_pair_h[n], None, table1,
                                         bass.IndirectOffsetOnAxis(ap=d_idx[:, n:n + 1], axis=0),
                                         bounds_check=N - 1, oob_is_err=False).then_inc(e_rows_in, 16)
                pool.wait_ge(e_pair_ready, c + 1)
            with pool.Fori(0, HEADS) as h:
                lone_wait(pool, node_ready, e_zeroed, 16 * 8 * TILES * (h + 1))
                with pool.Fori(0, PCOL) as c:
                    n = h * PCOL + c
                    g.tensor_copy(d_idx[:, 0:1], pair_idx[:, bass.ds(c, 1)]).then_inc(e_pool, 1)
                    g.tensor_copy(d_val[:], d_pair_att_flat[0:PP, bass.ds(c * HEADS + h, 1)]).then_inc(e_pool, 1)
                    lone_wait(pool, pairs_ready, e_pool, 2 * n + PCOL + 2)
                    g.indirect_dma_start(full_flat, bass.IndirectOffsetOnAxis(ap=d_idx[:, 0:1], axis=0), d_val[:], None,
                                         bounds_check=N * N - 1, oob_is_err=False).then_inc(e_scattered, 16)
                    pool.wait_ge(e_scattered, 16 * (n + 1))

        def dense1_scalar(act):
            with act.Fori(0, HEADS * TILES) as n:
                act.wait_ge(e_max_ready, n + 1)
                nc.scalar.activation(d_score, d_score, ACT.Exp, bias=d_max[:, 1:2], accum_out=d_sum[:, 0:1]
                                     ).then_inc(e_exp_ready, 1)

        def dense1_tensor(pe):
            pe.wait_ge(e_weights_in, 64)
            with pe.Fori(0, PCOL) as c:
                pe.wait_ge(e_rows_in, 32 * (c + 1))
                for n in both:
                    for k in range(KC):
                        last = nc.tensor.transpose(bank[n][:, k * P:k * P + PP], d_pair_h[n][:, k * P:(k + 1) * P],
                                                   ident[0:PP, 0:PP])
                last.then_inc(e_turned, 1)
                pe.wait_ge(e_turned_ready, c + 1)
                for n in both:
                    for k in range(KC):
                        last = nc.tensor.matmul(bank[2 + n][0:PP, :], d_pair_hT[n][:, k, 0:PP], d_weight[n][:, k, :],
                                                start=(k == 0), stop=(k == KC - 1))
                last.then_inc(e_proj, 1)
            with pe.Fori(0, TILES) as t:
                pe.wait_ge(e_agg_in, 16 * (t + 1))
                for b in range(TILES):
                    last = nc.tensor.transpose(bank[b // KC][:, b % KC * P:(b % KC + 1) * P],
                                               d_score[:, b * P:(b + 1) * P], ident[:])
                last.then_inc(e_agg_turned, 1)
                pe.wait_ge(e_aggT_ready, t + 1)
                for b in range(TILES):
                    if b % half == 0:
                        pe.wait_ge(e_half_in, 16 * (2 * t + b // half + 1))
                    last = nc.tensor.matmul(bank[0][:], d_adj[:, b * P:(b + 1) * P], d_h2[:, b % half, :],
                                            start=(b == 0), stop=(b == TILES - 1))
                    if b % half == half - 1:
                        last.then_inc(e_summed, 1)

        def dense1_vector(dve):
            v = nc.vector
            v.memset(d_out, 0.0).then_inc(e_zero_ready, 1)
            v.tensor_scalar(off_diag, ident[:], 0.0, None, ALU.is_equal).then_inc(e_final, 1)
            v.tensor_scalar(on_diag, ident[:], SELF_SCORE, None, ALU.mult).then_inc(e_final, 1)
            dve.wait_ge(e_final, 2)
            dve.wait_ge(e_weights_in, 64)
            with dve.Fori(0, PCOL) as c:
                st = Steps(dve, e_pair_dve, 5, c)
                dve.wait_ge(e_turned, c + 1)
                for n in both:
                    last = v.tensor_copy(d_pair_hT[n][:, :, 0:PP],
                                         bank[n][:].rearrange("p (k n) -> p k n", k=KC)[:, :, 0:PP])
                    if n == 0:
                        st(last)
                last.then_inc(e_turned_ready, 1)
                dve.wait_ge(e_proj, c + 1)
                for n in both:
                    st.link(v.tensor_tensor(d_pair_q[n], bank[2 + n][0:PP, :], d_bias[n][0:PP, :], ALU.add))
                st.link(v.tensor_tensor(d_pair_q[0], d_pair_q[0], d_pair_q[1], ALU.mult))
                st.link(v.tensor_reduce(d_pair_att[0:PP, c, :], d_pair_q[0].rearrange("p (h d) -> p h d", h=HEADS),
                                        X_AXIS, ALU.add))
                v.tensor_scalar(d_pair_att[0:PP, c, :], d_pair_att[0:PP, c, :], DH ** -0.5, None, ALU.mult
                                ).then_inc(e_pair_ready, 1)
                st.end()
            with dve.Fori(0, HEADS) as h:
                with dve.Fori(0, TILES) as t:
                    n = h * TILES + t
                    st = Steps(dve, e_dve, 8, n)
                    dve.wait_ge(e_in, 48 * (n + 1))
                    st.link(v.tensor_scalar(d_adj, d_adj, 1.0, None, ALU.is_equal))
                    st.link(v.tensor_tensor(d_score, d_score, d_adj, ALU.mult))
                    st.link(v.tensor_scalar(d_adj, d_adj, 1.0, NEGBIG, ALU.subtract, ALU.mult))
                    st.link(v.tensor_tensor(d_score, d_score, d_adj, ALU.add))
                    block_own = d_score[:, bass.ds(t * P, P)]
                    st.link(v.tensor_tensor(block_own, block_own, off_diag, ALU.mult))
                    st.link(v.tensor_tensor(block_own, block_own, on_diag, ALU.add))
                    st.link(v.tensor_reduce(d_max[:, 0:1], d_score, X_AXIS, ALU.max))
                    v.tensor_scalar(d_max[:, 1:2], d_max[:, 0:1], -1.0, None, ALU.mult).then_inc(e_max_ready, 1)
                    dve.wait_ge(e_exp_ready, n + 1)
                    st.link(v.reciprocal(d_sum[:, 1:2], d_sum[:, 0:1]))
                    v.tensor_scalar(d_sum[:, 1:2], d_sum[:, 1:2], 1.0 / HEADS, None, ALU.mult).then_inc(e_final, 1)
                    dve.wait_ge(e_final, n + 3)
                    v.scalar_tensor_tensor(out=d_agg, in0=d_score, scalar=d_sum[:, 1:2], in1=d_agg,
                                           op0=ALU.mult, op1=ALU.add).then_inc(e_agg_ready, 1)
                    dve.wait_ge(e_agg_ready, n + 1)
                    st.end()
            with dve.Fori(0, TILES) as t:
                dve.wait_ge(e_agg_turned, t + 1)
                for b in range(8):
                    last = v.tensor_copy(d_adj[:, b * D:(b + 1) * D], bank[b][:])
                last.then_inc(e_aggT_ready, 1)
                dve.wait_ge(e_summed, 2 * t + 2)
                v.tensor_tensor(d_out, bank[0][:], x_all[:, t, :], ALU.add).then_inc(e_out_ready, 1)
                dve.wait_ge(e_out_stored, 16 * (t + 1))
        block = ctx.enter_context(nc.Block())

        @block.sync
        def _(sp):
            sp.dma_start(pair_sb[:], pairs.rearrange("(p c) two -> p c two", c=PCOL)).then_inc(pair_in, 16)
            sp.dma_start(w0_sb, w0.rearrange("(k p) n -> p k n", p=P)).then_inc(weights0_in, 16)
            sp.dma_start(a_rows[:, 0, :], a1.partition_broadcast(P)).then_inc(weights0_in, 16)
            sp.dma_start(a_rows[:, 1, :], a2.partition_broadcast(P)).then_inc(weights0_in, 16)

            sp.dma_start(b4_row[:], b4.partition_broadcast(P)).then_inc(weights1_in, 16)

            def load(i, b):
                t = BUFS * i + b
                if later(t, BUFS):
                    sp.wait_ge(adj_searched, t - BUFS + 1)
                sp.dma_start(x_all[:, t, :], x_rows[t]).then_inc(x_in[b], 16)
                sp.dma_start(adj_sb[b][:, :, 0:SEGW], adj_tiles[t]).then_inc(adj_in[b], 16)

            front_slots(sp, load)
            sp.dma_start(diag[:], bass.AP(tensor=adj.tensor, offset=0, ap=[[N + 1, P], [(N + 1) * P, TILES]]),
                         allow_slow_non_contiguous=True).then_inc(diag_in, 16)
            sp.wait_ge(node_ready, 1)
            sp.dma_start(keys_dram.rearrange("(t p) k -> p t k", p=P), node[:, :, 0:SLOTS]).then_inc(keys_stored, 16)

            for u in both:
                sp.wait_ge(wh_stored[u], 16 * STEPS)
            flag = read_flag(sp)
            with sp.If(flag > 0):
                dense0_sync(sp)

            def dense_att(j):
                with sp.If(flag > 0):
                    sp.wait_ge(own_added, 2 * j + 2)
                    sp.dma_start(att, att_steps[j]).then_inc(g_att_in, 16)

            def self_rows(jj, q, first):
                if not first:
                    sp.wait_ge(own_added, 4 * jj + 2 * q - 2)
                sp.dma_start(gath[q][:, EC:GC, :], table0_steps[2 * jj + q]).then_inc(self_in[q], 16)

            for q in both:
                self_rows(0, q, True)
            sp.dma_start(w1_sb[:], w1t.rearrange("(k p) n -> p k n", p=P)).then_inc(weights2_in, 16)
            sp.dma_start(w2_sb[:], w2t.rearrange("(k p) n -> p k n", p=P)).then_inc(weights2_in, 16)
            sp.dma_start(w3_sb[:], w3t).then_inc(weights2_in, 16)
            sp.dma_start(w4_sb[:], w4t.rearrange("(k p) n -> p k n", p=P)).then_inc(weights2_in, 16)
            sp.dma_start(b1_sb[:], b1).then_inc(weights2_in, 16)
            sp.dma_start(b2_sb[:], b2).then_inc(weights2_in, 16)
            sp.dma_start(b3_sb[:], b3).then_inc(weights2_in, 16)
            sp.wait_ge(consts_made, N_CONSTS)
            for n in range(8):
                sp.dma_start(score_dram.rearrange("(n p r) h -> n p (r h)", n=8, p=P)[n], zeros[:]
                             ).then_inc(score_zeroed, 16)
            with sp.Fori(1, STEPS // 2) as jj:
                for q in both:
                    self_rows(jj, q, False)
                    dense_att(2 * jj + q - 2)
            for q in both:
                dense_att(STEPS - 2 + q)

            sp.wait_ge(score_zeroed, 16 * 8)
            for u in both:
                sp.wait_ge(h2_stored[u], 16 * STEPS)
            sp.wait_ge(b4_added, TILES)
            sp.dma_start(wq_sb, wqt.rearrange("(k p) n -> p k n", p=P)).then_inc(late_in, 16)
            sp.dma_start(wk_sb, wkt.rearrange("(k p) n -> p k n", p=P)).then_inc(late_in, 16)
            sp.dma_start(bq_row[:], bq.partition_broadcast(P)).then_inc(late_in, 16)
            sp.dma_start(bk_row[:], bk.partition_broadcast(P)).then_inc(late_in, 16)

            def late_rows(jj, q, first):
                if not first:
                    sp.wait_ge(weight_ready, 2 * jj + q - 1)
                if first and q == 0:
                    sp.wait_ge(hit_stored, 16)
                sp.dma_start(score_in[q], score_steps[2 * jj + q]).then_inc(score_in_sem[q], 16)

            def store_out(jj, q):
                for u in both:
                    sp.wait_ge(out_ready, 4 * jj + 2 * q + u + 1)
                    sp.dma_start(out_rows[4 * jj + 2 * q + u], out_sb[q][:, u, :]).then_inc(out_stored[2 * q + u], 16)

            for q in both:
                late_rows(0, q, True)
            late_rows(1, 0, False)
            with sp.Fori(1, STEPS // 2 - 1) as jj:
                late_rows(jj, 1, False)
                store_out(jj - 1, 0)
                late_rows(jj + 1, 0, False)
                store_out(jj - 1, 1)
            late_rows(STEPS // 2 - 1, 1, False)
            for jj in (STEPS // 2 - 2, STEPS // 2 - 1):
                for q in both:
                    store_out(jj, q)
            for stored in out_stored:
                sp.wait_ge(stored, 8 * STEPS)
            with sp.If(flag > 0):
                dense1_sync(sp)

        @block.gpsimd
        def _(pool):
            g = nc.gpsimd
            g.iota(iota[:], pattern=[[1, EDGES]], base=0, channel_multiplier=0,
                   allow_small_or_imprecise_dtypes=True).then_inc(consts_made, 1)
            g.memset(ident[:], 0.0).then_inc(consts_made, 1)
            g.memset(before[:], 1.0).then_inc(consts_made, 1)
            g.memset(ones[:], 1.0).then_inc(consts_made, 1)
            g.memset(zeros[:], 0.0).then_inc(consts_made, 1)
            pool.wait_ge(consts_made, 5)
            g.affine_select(out=ident[:], in_=ident[:], compare_op=ALU.not_equal, fill=1.0, base=0,
                            pattern=[[1, P]], channel_multiplier=-1).then_inc(consts_made, 1)
            g.affine_select(out=before[:], in_=before[:], compare_op=ALU.is_gt, fill=0.0, base=0,
                            pattern=[[1, P]], channel_multiplier=-1).then_inc(consts_made, 1)
            g.iota(seg_base[:], pattern=[[SEGW, SEG], [0, 8]], base=1, channel_multiplier=0,
                   allow_small_or_imprecise_dtypes=True).then_inc(consts_made, 1)
            g.iota(self_key[:], pattern=[[P, TILES]], base=1, channel_multiplier=1,
                   allow_small_or_imprecise_dtypes=True).then_inc(consts_made, 1)
            g.iota(edge_pos[:], pattern=[[0, PAIR], [P, CH]], base=0, channel_multiplier=1,
                   allow_small_or_imprecise_dtypes=True).then_inc(consts_made, 1)

            def add_b4(t):
                pool.wait_ge(h_made, t + 1)
                g.tensor_tensor(x_all[:, t, :], x_all[:, t, :], b4_row[:], ALU.add).then_inc(b4_added, 1)

            def pair_group(n):
                g.tensor_copy(idx8[:], pair_idx[:].rearrange("p (n c) -> p n c", c=PG)[:, n, :]).then_inc(pool_pair, 1)
                lone_wait(pool, pairs_ready, pool_pair, 2 * n + 1)
                for c in range(PG):
                    g.indirect_dma_start(adj8[:, c:c + 1], None, adj_flat,
                                         bass.IndirectOffsetOnAxis(ap=idx8[:, c:c + 1], axis=0),
                                         bounds_check=N * N - 1, oob_is_err=False).then_inc(pair_adj_in, 16)
                if later(n, 1):
                    for k in range(B4_TILES):
                        add_b4(B4_TILES * (n - 1) + k)
                pool.wait_ge(pair_adj_in, 16 * PG * (n + 1))
                g.tensor_copy(pair_adj[:].rearrange("p (n c) -> p n c", c=PG)[:, n, :], adj8[:]).then_inc(pool_pair, 1)

            pool.wait_ge(pairs_ready, 1)
            pair_group(0)
            pool.wait_ge(weights1_in, 16)
            with pool.Fori(1, PCOL // PG) as n:
                pair_group(n)
            with pool.Fori(B4_TILES * (PCOL // PG - 1), TILES) as t:
                add_b4(t)

            for u in both:
                pool.wait_ge(wh_stored[u], 16 * STEPS)
            flag = read_flag(pool)
            with pool.If(flag > 0):
                pool.wait_ge(g_stored, 16 * HEADS * TILES)

            def gather(table, width, jj, q, first, ready, used, into, low=0, high=EC):
                lone_wait(pool, pairs_ready, ready, 2 * jj + q + 1)
                for c in range(low, high):
                    if not first and c % CH == 0:
                        lone_wait(pool, pairs_ready, used, 4 * jj + 2 * q - 3 + c // CH)
                    g.indirect_dma_start(gath[q][:, c, 0:width], None, table,
                                         bass.IndirectOffsetOnAxis(ap=edge_idx[q][:, c:c + 1], axis=0),
                                         bounds_check=N - 1, oob_is_err=False).then_inc(into[q], 16)

            def place(jj, q):
                j = 2 * jj + q
                pool.wait_ge(gath_in[q], 16 * EC * (jj + 1))
                if later(j, 1):
                    pool.wait_ge(slots_summed, j)
                g.tensor_tensor(placed, slot_hot[q][:].unsqueeze(3).to_broadcast([P, EC, SLOTS, HEADS]),
                                gath[q][:, 0:EC, D:ROW].unsqueeze(2).to_broadcast([P, EC, SLOTS, HEADS]), ALU.mult
                                ).then_inc(placed_ready, 1)

            def scale_own(jj, q):
                pool.wait_ge(own_prob_ready, 2 * jj + q + 1)
                pool.wait_ge(self_in[q], 16 * (jj + 1))
                own = gath[q][:, EC:GC, 0:D].rearrange("p c (h d) -> p c h d", h=HEADS)
                g.tensor_tensor(own, own, own_prob[:].unsqueeze(3).to_broadcast([P, PAIR, HEADS, DH]),
                                ALU.mult).then_inc(own_scaled, 1)

            def add_own(j, q, u):
                pool.wait_ge(own_scaled, j + 1)
                pool.wait_ge(att_ready, 2 * j + u + 1)
                g.tensor_tensor(att[:, u, :], att[:, u, :], gath[q][:, EC + u, 0:D], ALU.add).then_inc(own_added, 1)

            for q in both:
                gather(table0, ROW, 0, q, True, idx_ready, agg_summed, gath_in)
                if q == 0:
                    place(0, 0)

            def body(jj, q):
                j = 2 * jj + q
                if has(j, 0, STEPS - 1):
                    scale_own(jj, q)
                if has(j, 0, STEPS - 2):
                    place(jj + q, 1 - q)
                if has(j, 0, STEPS - 1):
                    add_own(j, q, 0)
                if has(j, 0, STEPS - 3):
                    gather(table0, ROW, jj + 1, q, False, idx_ready, agg_summed, gath_in, 0, CH - 2)
                if has(j, 0, STEPS - 1):
                    add_own(j, q, 1)
                if has(j, 0, STEPS - 3):
                    gather(table0, ROW, jj + 1, q, False, idx_ready, agg_summed, gath_in, CH - 2, EC)

            edge_pipeline(pool, body)

            pool.wait_ge(keys_stored, 16)
            g.memset(hit_keys[:], 0.0).then_inc(pool_pair, 1)
            pool.wait_ge(pool_pair, 2 * (PCOL // PG) + 1)
            pool.wait_ge(hit_summed, 1)
            pool.wait_ge(dve_mid, MID_TICKS)
            for dst, table, idx in ((hit_keys[:], keys_dram, hit_sub), (hit_h[0], table1, hit_sub),
                                    (hit_h[1], table1, hit_obj)):
                if table is table1 and idx is hit_sub:
                    for u in both:
                        pool.wait_ge(h2_stored[u], 16 * STEPS)
                g.indirect_dma_start(dst, None, table, bass.IndirectOffsetOnAxis(ap=idx[:, 0:1], axis=0),
                                     bounds_check=N - 1, oob_is_err=False).then_inc(hit_in, 16)
            gather(table1, D, 0, 0, True, idx1_ready, agg1_summed, gath1_in)
            pool.wait_ge(hit_att_ready, 1)
            g.indirect_dma_start(score_dram, bass.IndirectOffsetOnAxis(ap=hit_dst[:, 0:1], axis=0), hit_att[:], None,
                                 bounds_check=N * SLOTS - 1, oob_is_err=False).then_inc(hit_stored, 16)
            gather(table1, D, 0, 1, True, idx1_ready, agg1_summed, gath1_in)
            with pool.Fori(1, STEPS // 2) as jj:
                for q in both:
                    gather(table1, D, jj, q, False, idx1_ready, agg1_summed, gath1_in)
            for stored in out_stored:
                pool.wait_ge(stored, 8 * STEPS)
            with pool.If(flag > 0):
                dense1_gpsimd(pool)

        @block.scalar
        def _(act):
            s = nc.scalar

            def turn_copy(t, u):
                act.wait_ge(h_turned, t + 1)
                if later(t, 2):
                    act.wait_ge(wh_summed, t - 1)
                s.copy(hT[u].rearrange("p k n -> p (k n)"), bank[u][:]).then_inc(hT_ready, 1)

            def copy_table(t, u, stored_before):
                act.wait_ge(wh_summed, t + 1)
                if later(t, 2):
                    act.wait_ge(wh_stored[u], 16 * stored_before)
                s.copy(wh_row[u][:, 0:D], bank[2 + u][:]).then_inc(wh_copied, 1)
                s.copy(wh_row[u][:, D:ROW], bank[4 + u][:, HEADS:2 * HEADS]).then_inc(wh_copied, 1)
                s.copy(src_dst[:, t, :], bank[4 + u][:, 0:2 * HEADS]).then_inc(wh_copied, 1)
                act.wait_ge(wh_copied, 3 * t + 2)
                act.dma_start(table0_rows[t], wh_row[u]).then_inc(wh_stored[u], 16)

            def front(i, b):
                t, u = BUFS * i + b, b % 2
                act.wait_ge(var_ready, t + 1)
                s.activation(std[u][:], mean_var[u][:, 1:2], ACT.Sqrt, bias=eps_col[:, 0:1]).then_inc(std_ready, 1)
                if later(t, 1):
                    turn_copy(t - 1, 1 - u)
                act.wait_ge(ln_ready, t + 1)
                if later(t, 2):
                    act.wait_ge(h_turned, t - 1)
                s.activation(h_sb[u], x_all[:, t, :], ACT.Relu, bias=ln_shift[u][:, 0:1],
                             scale=ln_scale[u][:, 0:1]).then_inc(h_made, 1)
                if later(t, 2):
                    copy_table(t - 2, u, 2 * i + b // 2 - 1)

            front_slots(act, front)
            turn_copy(TILES - 1, 1)
            copy_table(TILES - 2, 0, STEPS - 1)
            copy_table(TILES - 1, 1, STEPS - 1)

            def info(j, q):
                act.wait_ge(info_summed, j + 1)
                if later(j, 2):
                    act.wait_ge(exponent_ready, j - 1)
                s.copy(edge_info[q][:].rearrange("p c v -> p (c v)"), bank[0][:, 0:EC * VW]).then_inc(info_ready, 1)

            def probabilities(j, q):
                act.wait_ge(slot_exponent_ready, j + 1)
                s.activation(masked, masked, ACT.Exp).then_inc(slot_exp_ready, 1)
                act.wait_ge(exponent_ready, j + 1)
                if later(j, 2):
                    act.wait_ge(agg_summed, 2 * j - 2)
                s.activation(prob[q][:], edge_e[:, 2], ACT.Exp).then_inc(prob_ready, 1)

            def distances(j, q):
                for u in both:
                    s.activation(row_hot[q][:, u, :].bitcast(F32R), iota[:], ACT.Abs,
                                 bias=neg_centre[:, bass.ds(2 * j + u, 1)]).then_inc(distance_ready, 1)

            def elu_parts_of(j, u):
                with act.If(flag > 0):
                    lone_wait(act, node_ready, g_att_in, 16 * (j + 1))
                act.wait_ge(own_added, 2 * j + u + 1)
                s.activation(att_exp[:, u, :], att[:, u, :], ACT.Exp).then_inc(elu_parts, 1)
                act.wait_ge(elu_parts, 4 * j + 2 * u + 1)
                s.activation(att[:, u, :], att[:, u, :], ACT.Relu).then_inc(elu_parts, 1)

            def mlp_bias_relu(j, layer):
                act.wait_ge(mlp_summed, 5 * j + layer)
                if layer == 2:
                    s.activation(z2, bank[7][:, 0:PAIR * P], ACT.Relu, bias=b2_sb[:, 0:1]).then_inc(mlp_relu, 1)
                else:
                    for m in range(2):
                        s.activation((z1, z3)[layer // 2][:, m, :], bank[6][:, 256 * m:256 * (m + 1)], ACT.Relu,
                                     bias=(b1_sb, b3_sb)[layer // 2][:, m:m + 1]).then_inc(mlp_relu, 1)

            def layer1_input(j):
                for u in both:
                    act.wait_ge(ln2_ready, 2 * j + u + 1)
                    if later(j, 1):
                        act.wait_ge(h2_stored[u], 16 * j)
                    s.activation(h2_sb[:, u, :], x_all[:, 2 * j + u, :], ACT.Relu, bias=ln2_shift[:, j, u:u + 1],
                                 scale=ln2_scale[:, j, u:u + 1]).then_inc(h2_made, 1)
                    act.wait_ge(h2_made, 2 * j + u + 1)
                    act.dma_start(table1_rows[2 * j + u], h2_sb[:, u, :]).then_inc(h2_stored[u], 16)

            flag = read_flag(act)
            with act.If(flag > 0):
                dense0_scalar(act)
            for q in both:
                distances(q, q)
            info(0, 0)
            info(1, 1)
            probabilities(0, 0)

            def body(jj, q):
                j = 2 * jj + q
                if has(j, 0, STEPS - 3):
                    distances(j + 2, q)
                if isinstance(j, int) and j == 1:
                    act.wait_ge(weights2_in, 7 * 16)
                if has(j, 1, STEPS):
                    for u in both:
                        act.wait_ge(enc_turned, 2 * j + u - 1)
                        s.activation(encT[:, :, u * P:(u + 1) * P], bank[4 + u][:].rearrange("p (k n) -> p k n", k=KC),
                                     ACT.Identity, bias=neg_one[:, 0:1]).then_inc(encT_ready, 1)
                if has(j, 0, STEPS - 3):
                    info(j + 2, q)
                if has(j, 0, STEPS - 1):
                    elu_parts_of(j, 0)
                if has(j, 1, STEPS):
                    mlp_bias_relu(j - 1, 1)
                if has(j, 0, STEPS - 1):
                    elu_parts_of(j, 1)
                if has(j, 1, STEPS):
                    mlp_bias_relu(j - 1, 2)
                if has(j, 2, STEPS + 1):
                    for u in both:
                        act.wait_ge(var2_ready, 2 * j + u - 3)
                        s.activation(std[u][:], mean_var[u][:, 1:2], ACT.Sqrt, bias=eps_col[:, 0:1]
                                     ).then_inc(std2_ready, 1)
                if has(j, 1, STEPS):
                    mlp_bias_relu(j - 1, 3)
                if has(j, 0, STEPS - 2):
                    probabilities(j + 1, 1 - q)
                if has(j, 2, STEPS + 1):
                    layer1_input(j - 2)

            edge_pipeline(act, body)

            for q in both:
                distances(q, q)
            for n in both:
                act.wait_ge(hit_turned, n + 1)
                s.copy(hit_hT[n].rearrange("p k n -> p (k n)"), bank[n][:]).then_inc(hit_hT_ready, 1)

            def late_exp(j):
                act.wait_ge(soft_ready, j + 1)
                s.activation(soft, soft, ACT.Exp).then_inc(soft_exp, 1)

            def own_part(j, q):
                act.wait_ge(own_ready, j + 1)
                if later(j, 2):
                    act.wait_ge(out_ready, 2 * j - 2)
                for u in both:
                    s.activation(gath[q][:, EC + u, 0:D], x_all[:, 2 * j + u, :], ACT.Relu,
                                 bias=own_shift[:, q, u:u + 1], scale=own_scale[:, q, u:u + 1]).then_inc(own_made, 1)

            def weigh(j, q):
                act.wait_ge(edge_w_ready, j + 1)
                for n in range(EC):
                    s.activation(edge_hot[q][:, n, :], edge_hot[q][:, n, :], ACT.Copy, scale=edge_w[:, n:n + 1]
                                 ).then_inc(hot1_ready, 1)

            def begin(j, q):
                late_exp(j)
                own_part(j, q)

            def next_distances(j, q):
                act.wait_ge(edge_w_summed, j - 1)
                distances(j, q)

            def late(jj, q):
                j = 2 * jj + q
                next_distances(j + 2, q)
                weigh(j + 1, 1 - q)
                begin(j + 2, q)

            begin(0, 0)
            weigh(0, 0)
            begin(1, 1)
            next_distances(2, 0)
            begin(2, 0)
            weigh(1, 1)
            late(0, 1)
            with act.Fori(1, STEPS // 2 - 1) as jj:
                for q in both:
                    late(jj, q)
            weigh(STEPS - 1, 1)
            with act.If(flag > 0):
                dense1_scalar(act)

        @block.tensor
        def _(pe):
            mm = nc.tensor.matmul
            turn = nc.tensor.transpose
            pe.wait_ge(consts_made, N_CONSTS)
            pe.wait_ge(weights0_in, 48)
            pe.wait_ge(fold_ready, 1)

            def project(t, u):
                pe.wait_ge(hT_ready, t + 1)
                if later(t, 2):
                    pe.wait_ge(wh_copied, 3 * t - 3)
                for k in range(KC):
                    mm(bank[2 + u][:], hT[u][:, k, :], w0_sb[:, k, :], start=(k == 0), stop=(k == KC - 1))
                for k in range(KC):
                    last = mm(bank[4 + u][:, 0:2 * HEADS], hT[u][:, k, :], a_fold[:, k, :],
                              start=(k == 0), stop=(k == KC - 1))
                last.then_inc(wh_summed, 1)

            def front(i, b):
                t, u = BUFS * i + b, b % 2
                if later(t, 1):
                    project(t - 1, 1 - u)
                pe.wait_ge(h_made, t + 1)
                if later(t, 2):
                    pe.wait_ge(hT_ready, t - 1)
                for k in range(KC):
                    last = turn(bank[u][:, k * P:(k + 1) * P], h_sb[u][:, k * P:(k + 1) * P], ident[:])
                last.then_inc(h_turned, 1)

            front_slots(pe, front)

            pe.wait_ge(counts_ready, 1)
            mm(bank[6][:, 0:TILES], before[:], count[:], start=True, stop=True)
            mm(bank[6][:, TILES:2 * TILES], ones[:], count[:], start=True, stop=True)
            mm(bank[6][:, 64:65], before[:], hit_end[:, 0:1], start=True, stop=True)
            mm(bank[6][:, 65:66], ones[:], hit_end[:, 0:1], start=True, stop=True).then_inc(offsets_summed, 1)
            project(TILES - 1, 1)
            pe.wait_ge(flags_ready, 1)
            mm(bank[7][:, 0:1], ones[:], flag_f[:, 0:1], start=True, stop=True).then_inc(flags_summed, 1)

            def info(j, q):
                if later(j, 2):
                    pe.wait_ge(exponent_ready, j - 1)
                if later(j, 1):
                    pe.wait_ge(info_ready, j)
                for u in both:
                    pe.wait_ge(rows_ready, 2 * j + u + 1)
                    for c in range(CH):
                        last = mm(bank[0][:, (u * CH + c) * VW:(u * CH + c + 1) * VW],
                                  row_hot[q][:, u, c * P:(c + 1) * P].bitcast(F32R), step_node(j)[:, u, :].bitcast(F32R),
                                  start=True, stop=True)
                last.then_inc(info_summed, 1)

            def slots(j, q):
                pe.wait_ge(placed_ready, j + 1)
                pe.wait_ge(hot_ready, j + 1)
                for u in both:
                    for c in range(CH):
                        last = mm(bank[1][:, u * P:(u + 1) * P], edge_hot[q][:, u * CH + c, :],
                                  placed[:, u * CH + c].rearrange("p k h -> p (k h)"),
                                  start=(c == 0), stop=(c == CH - 1))
                last.then_inc(slots_summed, 1)

            def edge_max(j, q, copied):
                pe.wait_ge(row_max_ready, j + 1)
                pe.wait_ge(info_ready, copied)
                for u in both:
                    for c in range(CH):
                        n = u * CH + c
                        last = mm(bank[0][:, EC * VW + n * 2 * HEADS:EC * VW + (n + 1) * 2 * HEADS],
                                  row_hot[q][:, u, c * P:(c + 1) * P].bitcast(F32R),
                                  row_max_parts[q][:, u, :].bitcast(F32R), start=True, stop=True)
                last.then_inc(edge_max_summed, 1)

            def aggregate(j, q, u):
                if later(j, 1):
                    pe.wait_ge(att_ready, 2 * j + u - 1)
                for c in range(CH):
                    if c in (0, 2):
                        pe.wait_ge(scaled, 4 * j + 1 + c // 2 + 2 * u)
                    last = mm(bank[2 + u][:], edge_hot[q][:, u * CH + c, :], gath[q][:, u * CH + c, 0:D],
                              start=(c == 0), stop=(c == CH - 1))
                last.then_inc(agg_summed, 1)

            def turn_enc(j):
                pe.wait_ge(enc_ready, 2 * j + 2)
                for u in both:
                    for k in range(KC):
                        last = turn(bank[4 + u][:, k * P:(k + 1) * P], att_exp[:, u, k * P:(k + 1) * P], ident[:])
                    last.then_inc(enc_turned, 1)

            def mlp(j, layer):
                if layer == 1:
                    pe.wait_ge(encT_ready, 2 * j + 2)
                    if later(j, 1):
                        pe.wait_ge(x_added, 2 * j)
                    for m in range(2):
                        for k in range(KC):
                            last = mm(bank[6][:, 256 * m:256 * (m + 1)], w1_sb[:, k, m * P:(m + 1) * P],
                                      encT[:, k, :], start=(k == 0), stop=(k == KC - 1))
                elif layer == 2:
                    pe.wait_ge(mlp_relu, 5 * j + 2)
                    for k in range(2):
                        last = mm(bank[7][:, 0:PAIR * P], w2_sb[:, k, :], z1[:, k, :], start=(k == 0), stop=(k == 1))
                elif layer == 3:
                    pe.wait_ge(mlp_relu, 5 * j + 3)
                    for m in range(2):
                        last = mm(bank[6][:, 256 * m:256 * (m + 1)], w3_sb[:, m * P:(m + 1) * P], z2,
                                  start=True, stop=True)
                else:
                    pe.wait_ge(mlp_relu, 5 * j + 5)
                    for u in both:
                        for k in range(2):
                            last = mm(bank[7 - u][:], z3[:, k, u * P:(u + 1) * P], w4_sb[:, k, :],
                                      start=(k == 0), stop=(k == 1))
                        if u == 0:
                            last.then_inc(mlp_summed, 1)
                last.then_inc(mlp_summed, 1)

            flag = read_flag(pe)
            with pe.If(flag > 0):
                dense0_tensor(pe)
            info(0, 0)
            pe.wait_ge(hit_rows_ready, 1)
            mm(bank[7][:, 0:17], hit_rows[:], hit_node[:], start=True, stop=True).then_inc(hit_summed, 1)
            info(1, 1)
            slots(0, 0)
            edge_max(0, 0, 2)

            def body(jj, q):
                j = 2 * jj + q
                if has(j, 0, STEPS - 1):
                    aggregate(j, q, 0)
                if has(j, 1, STEPS):
                    turn_enc(j - 1)
                if has(j, 0, STEPS - 3):
                    info(j + 2, q)
                if has(j, 0, STEPS - 1):
                    aggregate(j, q, 1)
                if isinstance(j, int) and j == 1:
                    pe.wait_ge(weights2_in, 7 * 16)
                if has(j, 1, STEPS):
                    mlp(j - 1, 1)
                if has(j, 0, STEPS - 2):
                    slots(j + 1, 1 - q)
                if has(j, 1, STEPS):
                    mlp(j - 1, 2)
                    mlp(j - 1, 3)
                if has(j, 0, STEPS - 2):
                    edge_max(j + 1, 1 - q, STEPS if isinstance(j, int) and j == STEPS - 2 else j + 3)
                if has(j, 1, STEPS):
                    mlp(j - 1, 4)

            edge_pipeline(pe, body)

            pe.wait_ge(hit_in, 48)
            for n in both:
                for k in range(KC):
                    last = turn(bank[n][:, k * P:(k + 1) * P], hit_h[n][:, k * P:(k + 1) * P], ident[:])
                last.then_inc(hit_turned, 1)
            pe.wait_ge(late_in, 64)
            for n in both:
                pe.wait_ge(hit_hT_ready, n + 1)
                for k in range(KC):
                    last = mm(bank[6 + n][:], hit_hT[n][:, k, :], (wq_sb, wk_sb)[n][:, k, :],
                              start=(k == 0), stop=(k == KC - 1))
                last.then_inc(hit_proj, 1)

            def edge_weights(j, q):
                pe.wait_ge(rows_ready, TILES + 2 * j + 2)
                pe.wait_ge(weight_ready, j + 1)
                if later(j, 1):
                    pe.wait_ge(edge_w_ready, j)
                for n in range(EC):
                    last = mm(bank[0][:, n * SLOTS:(n + 1) * SLOTS], row_hot[q][:, n // CH, n % CH * P:(n % CH + 1) * P],
                              weight[q][:, n // CH, 0:SLOTS], start=True, stop=True)
                last.then_inc(edge_w_summed, 1)

            def late(jj, q, first, last_step=False):
                j = 2 * jj + q
                weights_last = isinstance(j, int) and j == 0
                if not last_step and not weights_last:
                    edge_weights(j + 1, 1 - q)
                if not first:
                    pe.wait_ge(out_ready, 2 * j - 2)
                pe.wait_ge(gath1_in[q], 16 * EC * (jj + 1))
                for u in both:
                    pe.wait_ge(hot1_ready, EC * j + CH * (u + 1))
                    for c in range(CH):
                        last = mm(bank[2 + 2 * q + u][:], edge_hot[q][:, u * CH + c, :], gath[q][:, u * CH + c, 0:D],
                                  start=(c == 0), stop=(c == CH - 1))
                    last.then_inc(agg1_summed, 1)
                if weights_last:
                    edge_weights(j + 1, 1 - q)

            edge_weights(0, 0)
            for q in both:
                late(0, q, True)
            with pe.Fori(1, STEPS // 2 - 1) as jj:
                for q in both:
                    late(jj, q, False)
            late(STEPS // 2 - 1, 0, False)
            late(STEPS // 2 - 1, 1, False, True)
            for stored in out_stored:
                pe.wait_ge(stored, 8 * STEPS)
            with pe.If(flag > 0):
                dense1_tensor(pe)

        @block.vector
        def _(dve):
            v = nc.vector

            st = Steps(dve, dve_start, START_TICKS, 0)
            for b in bufs:
                st(v.memset(adj_sb[b][:, :, SEGW:SEGP], 1.0))
            st(v.memset(ones8[:], 1.0))
            st(v.memset(neg_one[:], -1.0))
            st(v.memset(eps_col[:], EPS))
            st(v.memset(hit_key[:], 0.0))
            st(v.memset(slot_bias[:, :, SLOTS:SLOTS + 1], 0.0))
            dve.wait_ge(pair_in, 16)
            st(v.scalar_tensor_tensor(out=pair_flat[:], in0=pair_sb[:, :, 0], scalar=float(N), in1=pair_sb[:, :, 1],
                                      op0=ALU.mult, op1=ALU.add))
            st.link(v.tensor_tensor(pair_ne[:], pair_sb[:, :, 0], pair_sb[:, :, 1], ALU.not_equal))
            v.tensor_copy(pair_idx[:], pair_flat[:]).then_inc(pairs_ready, 1)
            dve.wait_ge(weights0_in, 48)
            for k in range(KC):
                for a in range(2):
                    st.link(v.tensor_tensor(fold_tmp, w0_sb[:, k, :], a_rows[:, a, :], ALU.mult))
                    last = v.tensor_reduce(a_fold[:, k, a * HEADS:(a + 1) * HEADS],
                                           fold_tmp.rearrange("p (h d) -> p h d", h=HEADS), X_AXIS, ALU.add)
                    if (k, a) != (KC - 1, 1):
                        st.link(last)
            last.then_inc(fold_ready, 1)
            st.end()

            def alone(sem, value):
                lone_wait(dve, fold_ready, sem, value)


            def neighbours(t, u, st, k):
                if k == 0:
                    st(v.tensor_tensor(key_raw[u], found[u], seg_base[:], ALU.add))
                elif k == 1:
                    st.after(st.k)
                    st(v.scalar_tensor_tensor(out=key_any[u], in0=found[u], scalar=float(SEGW), in1=key_raw[u],
                                              op0=ALU.is_lt, op1=ALU.mult))
                elif k == 2:
                    st.after(st.k)
                    flat = key_any[u].rearrange("p s c -> p (s c)")
                    st(v.scalar_tensor_tensor(out=key_nbr[u], in0=flat, scalar=self_key[:, bass.ds(t, 1)], in1=flat,
                                              op0=ALU.not_equal, op1=ALU.mult))
                elif k == 3:
                    alone(st.sem, st.base + st.k)
                    st(v.max(key16[u][:, 0:8], key_nbr[u]))
                elif k == 4:
                    alone(st.sem, st.base + st.k)
                    st(v.match_replace(key_left[u], key16[u][:, 0:8], key_nbr[u], 0.0))
                elif k == 5:
                    alone(st.sem, st.base + st.k)
                    st(v.max(key16[u][:, 8:16], key_left[u]))
                elif k == 6:
                    st(v.tensor_copy(seg_last[:, t, :], key_any[u][:, :, 7]))
                elif k == 7:
                    st.after(st.k - 1)
                    st(v.tensor_copy(node[:, t, 0:SLOTS].bitcast(F32R), key16[u][:]))

            def front(i, b):
                t, u = BUFS * i + b, b % 2
                st = Steps(dve, dve_front, FRONT_TICKS, t)
                nbr = Steps(dve, dve_nbr, NBR_TICKS, t - 1)
                alone(x_in[b], 16 * (i + 1))
                stats_at = st(v.bn_stats(stats[u][:], x_all[:, t, :]))
                alone(adj_in[b], 16 * (i + 1))
                for g in range(SEG):
                    done = v.max_index(found[u][:, g, :], ones8[:], adj_sb[b][:, g, :])
                    if g == SEG - 1:
                        done.then_inc(adj_searched, 1)
                    else:
                        st(done)
                    if g == 0:
                        alone(st.sem, st.base + stats_at)
                        v.bn_aggr(mean_var[u][:], stats[u][:]).then_inc(var_ready, 1)
                    if g == 5:
                        dve.wait_ge(std_ready, t + 1)
                        if later(t, 2):
                            dve.wait_ge(h_made, t - 1)
                        stats_at = st(v.reciprocal(ln_scale[u][:], std[u][:]))
                    if g == 6:
                        st.after(stats_at)
                        v.scalar_tensor_tensor(out=ln_shift[u][:], in0=mean_var[u][:, 0:1], scalar=-1.0,
                                               in1=ln_scale[u][:], op0=ALU.mult, op1=ALU.mult
                                               ).then_inc(ln_ready, 1)
                    if later(t, 1):
                        if g == 0:
                            dve.wait_ge(adj_searched, t)
                        neighbours(t - 1, 1 - u, nbr, g)
                st.end()

            dve.wait_ge(consts_made, N_CONSTS)
            front_slots(dve, front)
            dve.wait_ge(adj_searched, TILES)
            nbr = Steps(dve, dve_nbr, NBR_TICKS, TILES - 1)
            for k in range(NBR_TICKS):
                neighbours(TILES - 1, 1, nbr, k)
            nbr.end()
            dve.wait_ge(dve_nbr, NBR_TICKS * TILES)

            st = Steps(dve, dve_mid, MID_TICKS, 0)
            valid = slot_bias[:, :, 0:SLOTS]
            st.link(v.tensor_scalar(valid, node[:, :, 0:SLOTS], 0.0, None, ALU.is_gt))
            st(v.tensor_reduce(count[:], valid, X_AXIS, ALU.add))
            dve.wait_ge(pool_pair, 2 * (PCOL // PG))
            st.link(v.scalar_tensor_tensor(out=pair_ne[:], in0=pair_adj[:], scalar=1.0, in1=pair_ne[:],
                                           op0=ALU.is_equal, op1=ALU.mult))
            st.link(v.scalar_tensor_tensor(out=hit_key[0:PP, :], in0=pair_flat[:], scalar=1.0, in1=pair_ne[:],
                                           op0=ALU.add, op1=ALU.mult))
            st.link(v.max(hit8[:], hit_key[:]))
            st(v.tensor_scalar(hit8_m1[:], hit8[:], -1.0, None, ALU.add))
            st.link(v.tensor_scalar(hit_valid[:], hit8[:], 0.0, None, ALU.is_gt))
            v.tensor_reduce(hit_end[:, 0:1], hit_valid[:], X_AXIS, ALU.add).then_inc(counts_ready, 1)
            st(v.tensor_scalar(valid, valid, 1.0, NEGBIG, ALU.subtract, ALU.mult))
            st(v.tensor_scalar(hit_sub_i[:], hit8_m1[:], 12, None, ALU.logical_shift_right))
            st.link(v.tensor_scalar(hit_obj_i[:], hit8_m1[:], N - 1, None, ALU.bitwise_and))
            st(v.scalar_tensor_tensor(out=hit_node[:, 0:8], in0=hit_sub_i[:], scalar=1.0, in1=hit_valid[:],
                                      op0=ALU.add, op1=ALU.mult))
            st(v.scalar_tensor_tensor(out=hit_node[:, 8:16], in0=hit_obj_i[:], scalar=1.0, in1=hit_valid[:],
                                      op0=ALU.add, op1=ALU.mult))
            st(v.tensor_reduce(flag_f[:, 1:2], seg_last[:].rearrange("p t s -> p (t s)"), X_AXIS, ALU.max))
            st(v.tensor_reduce(flag_f[:, 2:3], node[:, :, SLOTS - 1], X_AXIS, ALU.max))
            dve.wait_ge(diag_in, 16)
            st.link(v.tensor_reduce(flag_f[:, 3:4], diag[:], X_AXIS, ALU.min))
            st.link(v.tensor_tensor(flag_f[:, 1:2], flag_f[:, 1:2], flag_f[:, 2:3], ALU.max))
            st.link(v.tensor_tensor(flag_f[:, 1:2], flag_f[:, 1:2], hit8[:, 7:8], ALU.max))
            st(v.tensor_scalar(flag_f[:, 1:2], flag_f[:, 1:2], 0.0, None, ALU.is_gt))
            st.link(v.tensor_scalar(flag_f[:, 3:4], flag_f[:, 3:4], 1.0, None, ALU.not_equal))
            st.link(v.tensor_tensor(flag_f[:, 1:2], flag_f[:, 1:2], flag_f[:, 3:4], ALU.add))
            dve.wait_ge(offsets_summed, 1)
            st(v.tensor_copy(node[:, :, OFFC].bitcast(F32R), bank[6][:, 0:TILES]))
            st.link(v.tensor_scalar(half_count[:], count[:], 0.5, None, ALU.mult))
            st.link(v.scalar_tensor_tensor(out=neg_centre[:], in0=bank[6][:, 0:TILES], scalar=-1.0, in1=half_count[:],
                                      op0=ALU.mult, op1=ALU.subtract))
            st(v.tensor_scalar(neg_centre[:], neg_centre[:], 0.5, None, ALU.add))
            st(v.tensor_copy(node[:, :, ROWC].bitcast(F32R), self_key[:, 0:1].to_broadcast([P, TILES])))
            st(v.tensor_copy(hit_node[:, 16:17], bank[6][:, 64:65]))
            st(v.tensor_tensor(hit_end[:, 1:2], bank[6][:, 64:65], hit_end[:, 0:1], ALU.add))
            st(v.tensor_reduce(flag_f[:, 4:5], bank[6][:, TILES:2 * TILES], X_AXIS, ALU.max))
            st.link(v.tensor_scalar(flag_f[:, 5:6], bank[6][:, 65:66], float(P), None, ALU.is_gt))
            st.link(v.tensor_scalar(flag_f[:, 4:5], flag_f[:, 4:5], float(EDGES), None, ALU.is_gt))
            st.link(v.tensor_tensor(flag_f[:, 1:2], flag_f[:, 1:2], flag_f[:, 4:5], ALU.add))
            v.tensor_tensor(flag_f[:, 0:1], flag_f[:, 1:2], flag_f[:, 5:6], ALU.add).then_inc(flags_ready, 1)
            dve.wait_ge(wh_copied, 6 * STEPS)
            upper = node[:, :, SRCC:SRCC + HEADS]
            st.link(v.tensor_copy(upper.bitcast(F32R), src_dst[:, :, 0:HEADS]))
            st.link(v.tensor_tensor(node[:, :, SRCC + HEADS:VW].bitcast(F32R), src_dst[:, :, 0:HEADS], upper, ALU.subtract))
            dve.wait_ge(flags_summed, 1)
            st.link(v.tensor_scalar(flag_f[:, 6:7], bank[7][:, 0:1], 1.0, None, ALU.min))
            st.link(v.tensor_copy(flag_i[:], flag_f[:, 6:7]))
            v.tensor_copy(flag_f[:, 7:8], flag_f[:, 6:7]).then_inc(node_ready, 1)

            flag = read_flag(dve)
            with dve.If(flag > 0):
                for u in both:
                    dve.wait_ge(wh_stored[u], 16 * STEPS)
                dense0_vector(dve)

            def row_onehots(j, q, layer=0):
                for u in both:
                    t = 2 * j + u
                    dve.wait_ge(distance_ready, layer * TILES + t + 1)
                    v.tensor_scalar(row_hot[q][:, u, :].bitcast(F32R), row_hot[q][:, u, :], half_count[:, bass.ds(t, 1)], None,
                                    ALU.is_lt).then_inc(rows_ready, 1)

            def indices(j, q):
                st = Steps(dve, dve_idx, IDX_TICKS, j)
                dve.wait_ge(info_ready, j + 1)
                info = edge_info[q]
                st(v.tensor_copy(row_id[:, j, :], info[:, :, ROWC]))
                st.link(v.tensor_tensor(slot_id[:, j, :], edge_pos[:].rearrange("p u c -> p (u c)"), info[:, :, OFFC],
                                        ALU.subtract))
                st.link(v.tensor_tensor(slot_hot[q][:], iota16.unsqueeze(1).to_broadcast([P, EC, SLOTS]),
                                        slot_id[:, j, :].unsqueeze(2).to_broadcast([P, EC, SLOTS]), ALU.is_equal))
                st.link(v.tensor_tensor(nbr_tmp[:], slot_hot[q][:], info[:, :, 0:SLOTS], ALU.mult))
                st.link(v.tensor_reduce(nbr_key[:, 0, :], nbr_tmp[:], X_AXIS, ALU.add))
                st.link(v.tensor_scalar(nbr_key[:, 1, :], nbr_key[:, 0, :], 0.0, FAR, ALU.is_equal, ALU.mult))
                st.link(v.scalar_tensor_tensor(out=nbr_key[:, 2, :], in0=nbr_key[:, 0, :], scalar=-1.0,
                                               in1=nbr_key[:, 1, :], op0=ALU.add, op1=ALU.add))
                v.tensor_copy(edge_idx[q][:], nbr_key[:, 2, :]).then_inc(idx_ready, 1)
                st(v.tensor_copy(idx_all[:, j, :], nbr_key[:, 2, :]))
                st.end()

            def edge_onehots(j, q):
                v.tensor_tensor(edge_hot[q][:], iota_row1.unsqueeze(1).to_broadcast([P, EC, P]),
                                row_id[:, j, :].unsqueeze(2).to_broadcast([P, EC, P]), ALU.is_equal
                                ).then_inc(hot_ready, 1)

            def edge_scores(st, jj, q):
                j = 2 * jj + q
                dst = gath[q][:, 0:EC, D:ROW]
                own = step_src_dst[:, j]
                dve.wait_ge(gath_in[q], 16 * EC * (jj + 1))
                src = edge_info[q][:, :, SRCC:VW]
                st.link(v.tensor_tensor(edge_e[:, 0, 0:EC, :], src[:, :, 0:HEADS], src[:, :, HEADS:], ALU.add))
                st(v.tensor_tensor(edge_e[:, 0, 0:EC, :], edge_e[:, 0, 0:EC, :], dst, ALU.add))
                st.link(v.tensor_tensor(edge_e[:, 0, EC:GC, :], own[:, :, 0:HEADS], own[:, :, HEADS:], ALU.add))
                return st(v.scalar_tensor_tensor(out=edge_e[:, 1], in0=edge_e[:, 0], scalar=ALPHA, in1=edge_e[:, 0],
                                                 op0=ALU.mult, op1=ALU.max))

            def row_maxima(st, j, q):
                own = step_src_dst[:, j]
                dve.wait_ge(slots_summed, j + 1)
                st.link(v.tensor_tensor(masked, bank[1][:, 0:PAIR * P].rearrange("p (u k h) -> p u k h", u=PAIR, k=SLOTS),
                                        step_bias[:, j, :, 0:SLOTS].unsqueeze(3).to_broadcast([P, PAIR, SLOTS, HEADS]),
                                        ALU.add))
                st.link(v.tensor_reduce(max_tmp[:, 0], masked.rearrange("p u k h -> p u h k"), X_AXIS, ALU.max))
                st.link(v.tensor_tensor(max_tmp[:, 1], max_tmp[:, 0], own[:, :, HEADS:], ALU.max))
                st.link(v.tensor_tensor(max_tmp[:, 2], max_tmp[:, 1], own[:, :, 0:HEADS], ALU.add))
                st.link(v.scalar_tensor_tensor(out=row_max[q][:], in0=max_tmp[:, 2], scalar=ALPHA, in1=max_tmp[:, 2],
                                               op0=ALU.mult, op1=ALU.max))
                upper, rest = row_max_parts[q][:, :, 0:HEADS], row_max_parts[q][:, :, HEADS:]
                st.link(v.tensor_copy(upper.bitcast(F32R), row_max[q][:]))
                v.tensor_tensor(rest.bitcast(F32R), row_max[q][:], upper, ALU.subtract).then_inc(row_max_ready, 1)
                st.link(v.tensor_tensor(masked, masked, own[:, :, 0:HEADS].unsqueeze(2).to_broadcast(
                    [P, PAIR, SLOTS, HEADS]), ALU.add))
                st.link(v.scalar_tensor_tensor(out=masked, in0=masked, scalar=ALPHA, in1=masked,
                                               op0=ALU.mult, op1=ALU.max))
                v.tensor_tensor(masked, masked, row_max[q][:].unsqueeze(2).to_broadcast([P, PAIR, SLOTS, HEADS]),
                                ALU.subtract).then_inc(slot_exponent_ready, 1)

            def exponents(st, j, q):
                dve.wait_ge(row_max_ready, j + 1)
                if later(j, 1):
                    dve.wait_ge(prob_ready, j)
                st(v.tensor_tensor(edge_e[:, 0, EC:GC, :], edge_e[:, 1, EC:GC, :], row_max[q][:], ALU.subtract))
                dve.wait_ge(edge_max_summed, j + 1)
                st.link(v.tensor_reduce(edge_e[:, 0, 0:EC, :], bank[0][:, EC * VW:EC * (VW + 2 * HEADS)].rearrange(
                    "p (c parts h) -> p c h parts", c=EC, h=HEADS), X_AXIS, ALU.add))
                st.link(v.tensor_tensor(edge_e[:, 0, 0:EC, :], edge_e[:, 1, 0:EC, :], edge_e[:, 0, 0:EC, :],
                                        ALU.subtract))
                v.tensor_scalar(edge_e[:, 2], edge_e[:, 0], 0.0, None, ALU.min).then_inc(exponent_ready, 1)

            def scale(q, parts):
                for c0, c1 in parts:
                    part = gath[q][:, c0:c1, 0:D].rearrange("p c (h d) -> p c h d", h=HEADS)
                    v.tensor_tensor(part, part, prob[q][:, c0:c1, :].unsqueeze(3).to_broadcast([P, c1 - c0, HEADS, DH]),
                                    ALU.mult).then_inc(scaled, 1)

            def divisors(j, q):
                st = Steps(dve, dve_att, ATT_TICKS, j)
                dve.wait_ge(slot_exp_ready, j + 1)
                st.link(v.tensor_reduce(slot_sum[:], masked.rearrange("p u k h -> p u h k"), X_AXIS, ALU.add))
                st.link(v.tensor_tensor(slot_sum[:], slot_sum[:], prob[q][:, EC:GC, :], ALU.add))
                st.link(v.reciprocal(inv_sum[:], slot_sum[:]))
                v.tensor_tensor(own_prob[:], prob[q][:, EC:GC, :], inv_sum[:], ALU.mult).then_inc(own_prob_ready, 1)
                st.end()

            def normalise(j, u):
                dve.wait_ge(agg_summed, 2 * j + u + 1)
                v.tensor_tensor(att[:, u, :].rearrange("p (h d) -> p h d", h=HEADS),
                                bank[2 + u][:].rearrange("p (h d) -> p h d", h=HEADS),
                                inv_sum[:, u, :].unsqueeze(2).to_broadcast([P, HEADS, DH]), ALU.mult
                                ).then_inc(att_ready, 1)

            def elu(j, u):
                dve.wait_ge(elu_parts, 4 * j + 2 * u + 2)
                v.scalar_tensor_tensor(out=att_exp[:, u, :], in0=att_exp[:, u, :], scalar=1.0, in1=att[:, u, :],
                                       op0=ALU.min, op1=ALU.add).then_inc(enc_ready, 1)

            def add_to_x(j):
                for u in both:
                    dve.wait_ge(mlp_summed, 5 * j + 4 + u)
                    v.tensor_tensor(x_all[:, 2 * j + u, :], bank[7 - u][:], x_all[:, 2 * j + u, :], ALU.add
                                    ).then_inc(x_added, 1)

            def norm_stats(st, j):
                for u in both:
                    alone(x_added, 2 * j + u + 1)
                    st(v.bn_stats(stats[u][:], x_all[:, 2 * j + u, :]))
                at = st.k
                for u in both:
                    alone(st.sem, st.base + at - 1 + u)
                    v.bn_aggr(mean_var[u][:], stats[u][:]).then_inc(var2_ready, 1)

            def norm_scale(st, j):
                for u in both:
                    dve.wait_ge(std2_ready, 2 * j + u + 1)
                    st(v.reciprocal(ln2_scale[:, j, u:u + 1], std[u][:]))
                for u in both:
                    st.after(st.k - 1 + u)
                    v.scalar_tensor_tensor(out=ln2_shift[:, j, u:u + 1], in0=mean_var[u][:, 0:1], scalar=-1.0,
                                           in1=ln2_scale[:, j, u:u + 1], op0=ALU.mult, op1=ALU.mult
                                           ).then_inc(ln2_ready, 1)

            def begin(jj, q):
                st = Steps(dve, dve_edge, EDGE_TICKS, 2 * jj + q)
                edge_scores(st, jj, q)
                row_maxima(st, 2 * jj + q, q)
                exponents(st, 2 * jj + q, q)
                st.end()

            row_onehots(0, 0)
            st.link(v.tensor_scalar(hit_cmp[:], iota[:, 0:P], hit_node[:, 16:17], None, ALU.is_ge))
            v.scalar_tensor_tensor(out=hit_rows[:], in0=iota[:, 0:P], scalar=hit_end[:, 1:2], in1=hit_cmp[:],
                                   op0=ALU.is_lt, op1=ALU.mult).then_inc(hit_rows_ready, 1)
            row_onehots(1, 1)
            indices(0, 0)
            edge_onehots(0, 0)
            dve.wait_ge(hit_summed, 1)
            st(v.tensor_copy(hit_e[:], bank[7][:, 0:17]))
            st.link(v.tensor_tensor(hit_slot[:], edge_pos[:, 0, 0:1], bank[7][:, 16:17], ALU.subtract))
            st.link(v.tensor_scalar(hit_sel[:], iota[:, 0:8], hit_slot[:, 0:1], None, ALU.is_equal))
            for part, node1, idx, f in ((0, hit_sub1, hit_sub, 0), (8, hit_obj1, hit_obj, 2)):
                st.link(v.tensor_tensor(hit_tmp[:], hit_e[:, part:part + 8], hit_sel[:], ALU.mult))
                st.link(v.tensor_reduce(node1[:], hit_tmp[:], X_AXIS, ALU.add))
                st.link(v.tensor_scalar(hit_f[:, f:f + 1], node1[:], 0.0, FAR, ALU.is_equal, ALU.mult))
                st.link(v.scalar_tensor_tensor(out=hit_f[:, f + 1:f + 2], in0=node1[:], scalar=-1.0,
                                               in1=hit_f[:, f:f + 1], op0=ALU.add, op1=ALU.add))
                st.link(v.tensor_copy(idx[:], hit_f[:, f + 1:f + 2]))
            st.end()
            indices(1, 1)
            edge_onehots(1, 1)
            begin(0, 0)

            def body(jj, q):
                j = 2 * jj + q
                norm = Steps(dve, dve_norm, NORM_TICKS, j - 2)
                if has(j, 0, STEPS - 1):
                    dve.wait_ge(prob_ready, j + 1)
                    scale(q, ((0, 2), (2, CH)))
                    divisors(j, q)
                if has(j, 0, STEPS - 3):
                    row_onehots(j + 2, q)
                if has(j, 0, STEPS - 1):
                    scale(q, ((CH, CH + 2), (CH + 2, EC)))
                if has(j, 2, STEPS + 1):
                    add_to_x(j - 2)
                if has(j, 0, STEPS - 1):
                    normalise(j, 0)
                if has(j, 0, STEPS - 3):
                    indices(j + 2, q)
                if has(j, 2, STEPS + 1):
                    norm_stats(norm, j - 2)
                if has(j, 0, STEPS - 1):
                    normalise(j, 1)
                    elu(j, 0)
                if has(j, 0, STEPS - 2):
                    st = Steps(dve, dve_edge, EDGE_TICKS, j + 1)
                    edge_scores(st, jj + q, 1 - q)
                if has(j, 0, STEPS - 3):
                    edge_onehots(j + 2, q)
                if has(j, 0, STEPS - 2):
                    row_maxima(st, j + 1, 1 - q)
                if has(j, 0, STEPS - 1):
                    elu(j, 1)
                if has(j, 2, STEPS + 1):
                    norm_scale(norm, j - 2)
                    norm.end()
                if has(j, 0, STEPS - 2):
                    exponents(st, j + 1, 1 - q)
                    st.end()

            dve.wait_ge(b4_added, TILES)
            edge_pipeline(dve, body)

            def rows1(jj, q, first, st):
                j = 2 * jj + q
                if not first:
                    dve.wait_ge(gath1_in[q], 16 * EC * jj)
                    dve.wait_ge(edge_w_summed, j - 1)
                st.link(v.tensor_copy(edge_idx[q][:], idx_all[:, j, :]))
                v.tensor_tensor(slot_hot[q][:], iota16.unsqueeze(1).to_broadcast([P, EC, SLOTS]),
                                slot_id[:, j, :].unsqueeze(2).to_broadcast([P, EC, SLOTS]), ALU.is_equal
                                ).then_inc(idx1_ready, 1)
                row_onehots(j, q, layer=1)

            for q in both:
                st = Steps(dve, dve_rows1, ROWS1_TICKS, q)
                rows1(0, q, True, st)
                st.end()
            st = Steps(dve, dve_hit, HIT_TICKS, 0)
            dve.wait_ge(hit_in, 48)
            st.link(v.scalar_tensor_tensor(out=hit_keys[:], in0=hit_keys[:], scalar=hit_obj1[:, 0:1],
                                           in1=iota[:, 1:SLOTS + 1], op0=ALU.is_equal, op1=ALU.mult))
            st.link(v.tensor_reduce(hit_slot[:], hit_keys[:], X_AXIS, ALU.add))
            st(v.tensor_scalar(hit_f[:, 2:3], hit_slot[:], 0.0, float(2 * N * SLOTS), ALU.is_equal, ALU.mult))
            st.link(v.scalar_tensor_tensor(out=hit_f[:, 0:1], in0=hit_f[:, 1:2], scalar=float(SLOTS), in1=hit_slot[:],
                                           op0=ALU.mult, op1=ALU.add))
            st.link(v.scalar_tensor_tensor(out=hit_f[:, 0:1], in0=hit_f[:, 0:1], scalar=-1.0, in1=hit_f[:, 2:3],
                                           op0=ALU.add, op1=ALU.add))
            st(v.tensor_copy(hit_dst[:], hit_f[:, 0:1]))
            dve.wait_ge(hit_proj, 1)
            st(v.tensor_tensor(hit_q, bank[6][:], bq_row[:], ALU.add))
            dve.wait_ge(hit_proj, 2)
            st.link(v.tensor_tensor(hit_k, bank[7][:], bk_row[:], ALU.add))
            st.link(v.tensor_tensor(hit_q, hit_q, hit_k, ALU.mult))
            st.link(v.tensor_reduce(hit_tmp[:], hit_q.rearrange("p (h d) -> p h d", h=HEADS), X_AXIS, ALU.add))
            v.tensor_scalar(hit_att[:], hit_tmp[:], DH ** -0.5, None, ALU.mult).then_inc(hit_att_ready, 1)
            st.end()

            def softmax(jj, q, first):
                j = 2 * jj + q
                st = Steps(dve, dve_soft, SOFT_TICKS, j)
                dve.wait_ge(score_in_sem[q], 16 * (jj + 1))
                st(v.tensor_tensor(soft[:, :, 0:SLOTS, :], score_in[q].rearrange("p u (k h) -> p u k h", k=SLOTS),
                                   step_bias[:, j, :, 0:SLOTS].unsqueeze(3).to_broadcast([P, PAIR, SLOTS, HEADS]),
                                   ALU.add))
                st.link(v.memset(soft[:, :, SLOTS, :], SELF_SCORE))
                by_slot = soft.rearrange("p u k h -> p u h k")
                over_slots = [P, PAIR, SLOTS + 1, HEADS]
                st.link(v.tensor_reduce(soft_max, by_slot, X_AXIS, ALU.max))
                v.tensor_tensor(soft, soft, soft_max.unsqueeze(2).to_broadcast(over_slots), ALU.subtract
                                ).then_inc(soft_ready, 1)
                dve.wait_ge(soft_exp, j + 1)
                st.link(v.tensor_reduce(soft_sum, by_slot, X_AXIS, ALU.add))
                st.link(v.reciprocal(soft_sum, soft_sum))
                st.link(v.tensor_tensor(soft, soft, soft_sum.unsqueeze(2).to_broadcast(over_slots), ALU.mult))
                if not first:
                    dve.wait_ge(edge_w_summed, j - 1)
                    dve.wait_ge(own_made, 2 * j - 2)
                v.tensor_reduce(weight[q][:], soft, X_AXIS, ALU.add).then_inc(weight_ready, 1)
                dve.wait_ge(weight_ready, j + 1)
                own = weight[q][:, :, SLOTS]
                st(v.scalar_tensor_tensor(out=own_scale[:, q, :], in0=own, scalar=1.0 / HEADS, in1=ln2_scale[:, j, :],
                                          op0=ALU.mult, op1=ALU.mult))
                v.scalar_tensor_tensor(out=own_shift[:, q, :], in0=own, scalar=1.0 / HEADS, in1=ln2_shift[:, j, :],
                                       op0=ALU.mult, op1=ALU.mult).then_inc(own_ready, 1)
                st.end()

            def weighted_onehots(jj, q):
                j = 2 * jj + q
                st = Steps(dve, dve_edge1, EDGE1_TICKS, j)
                if later(j, 2):
                    dve.wait_ge(agg1_summed, 2 * j - 2)
                st(v.tensor_tensor(edge_hot[q][:], iota_row1.unsqueeze(1).to_broadcast([P, EC, P]),
                                   row_id[:, j, :].unsqueeze(2).to_broadcast([P, EC, P]), ALU.is_equal))
                dve.wait_ge(edge_w_summed, j + 1)
                st.link(v.scalar_tensor_tensor(
                    out=nbr_tmp[:], in0=bank[0][:, 0:EC * SLOTS].rearrange("p (c k) -> p c k", c=EC),
                    scalar=1.0 / HEADS, in1=slot_hot[q][:], op0=ALU.mult, op1=ALU.mult))
                if later(j, 1):
                    dve.wait_ge(hot1_ready, EC * j)
                v.tensor_reduce(edge_w[:], nbr_tmp[:], X_AXIS, ALU.add).then_inc(edge_w_ready, 1)
                dve.wait_ge(edge_w_ready, j + 1)
                st.end()

            def outputs(jj, q):
                j = 2 * jj + q
                for u in both:
                    dve.wait_ge(agg1_summed, 2 * j + u + 1)
                    if later(j, 2):
                        dve.wait_ge(out_stored[2 * q + u], 16 * jj)
                    v.tensor_tensor(out_sb[q][:, u, :], bank[2 + 2 * q + u][:], x_all[:, 2 * j + u, :], ALU.add
                                    ).then_inc(out_added, 1)
                for u in both:
                    dve.wait_ge(own_made, 2 * j + u + 1)
                    dve.wait_ge(out_added, 2 * j + u + 1)
                    v.tensor_tensor(out_sb[q][:, u, :], out_sb[q][:, u, :], gath[q][:, EC + u, 0:D], ALU.add
                                    ).then_inc(out_ready, 1)

            def late(jj, q, following=2):
                onehots_last = isinstance(jj, int) and jj == 0 and q == 0
                if following >= 1 and not onehots_last:
                    weighted_onehots(jj + q, 1 - q)
                if following >= 2:
                    st = Steps(dve, dve_rows1, ROWS1_TICKS, 2 * jj + q + 2)
                    rows1(jj + 1, q, False, st)
                    st.end()
                    softmax(jj + 1, q, False)
                if onehots_last:
                    weighted_onehots(jj + q, 1 - q)
                outputs(jj, q)

            softmax(0, 0, True)
            weighted_onehots(0, 0)
            softmax(0, 1, True)
            for q in both:
                late(0, q)
            with dve.Fori(1, STEPS // 2 - 1) as jj:
                for q in both:
                    late(jj, q)
            late(STEPS // 2 - 1, 0, 1)
            late(STEPS // 2 - 1, 1, 0)
            for stored in out_stored:
                dve.wait_ge(stored, 8 * STEPS)
            with dve.If(flag > 0):
                dense1_vector(dve)


def kernel(**inputs):
    import numpy as _np
    import concourse.bacc as _bacc
    from concourse import mybir as _mybir
    from concourse.bass_utils import run_bass_kernel_spmd as _run

    def host(name):
        return _np.asarray(inputs[name])

    laid_out = {
        "x": host("x"),
        "adj": host("adj"),
        "w0": host("L0_gnn_W").transpose(1, 0, 2).reshape(D, D),
        "a1": host("L0_gnn_a1").reshape(D),
        "a2": host("L0_gnn_a2").reshape(D),
        "w1t": host("L0_gnn_W1").T,
        "b1": host("L0_gnn_b1").reshape(-1, P).T,
        "w2t": host("L0_gnn_W2").T,
        "b2": host("L0_gnn_b2").reshape(-1, P).T,
        "w3t": host("L0_gnn_W3").T,
        "b3": host("L0_gnn_b3").reshape(-1, P).T,
        "w4t": host("L0_gnn_W4").T,
        "b4": host("L0_gnn_b4"),
        "pairs": host("L1_gnn_rel_pair_index"),
        "wqt": host("L1_gnn_Wq").T,
        "bq": host("L1_gnn_bq"),
        "wkt": host("L1_gnn_Wk").T,
        "bk": host("L1_gnn_bk"),
    }
    nc = _bacc.Bacc("TRN2", target_bir_lowering=False, num_devices=1)
    arrays, args = {}, []
    for name, a in laid_out.items():
        a = _np.ascontiguousarray(a)
        arrays[f"in_{name}_dram"] = a
        args.append(nc.dram_tensor(f"in_{name}_dram", a.shape, _mybir.dt.from_np(a.dtype), kind="ExternalInput").ap())
    out = nc.dram_tensor("out_dram", (N, D), F32, kind="ExternalOutput").ap()
    gnn_kernel(nc, *args, out)
    r = _run(nc, [arrays], core_ids=[0])
    return r.results[0]["out_dram"]
```
